# Optimizing a Trainium2 kernel written in Bass

```python
import numpy as np
import jax
import jax.numpy as jnp

def _softmax(x, axis=-1):
    return jax.nn.softmax(x, axis=axis)

def _gelu(x):
    return jax.nn.gelu(x, approximate=True)

def _silu(x):
    return jax.nn.silu(x)

def _sigmoid(x):
    return jax.nn.sigmoid(x)

def _layernorm(x, axis=-1, eps=1e-05):
    m = jnp.mean(x, axis=axis, keepdims=True)
    v = jnp.var(x, axis=axis, keepdims=True)
    return (x - m) / jnp.sqrt(v + eps)

def _scatter_add(tgt, idx, src, axis=0):
    return tgt.at[idx].add(src)

def _segment_sum(src, seg, n):
    return jax.ops.segment_sum(src, seg, n)
kernel_name = 'mk_adj_resnorm_d4_adj_r2_f97d93'

def setup_inputs(seed: int=0):
    np.random.seed(seed)
    _w = jnp.asarray

    def _rec_inputs():
        import jax
        import jax.numpy as jnp
        _gk = jax.random.key(seed)
        x = -0.003407 + 1.001 * jax.random.normal(jax.random.fold_in(_gk, 1), (64, 128, 64), jnp.float32)
        _a = jax.random.bernoulli(jax.random.fold_in(_gk, 2), 0.015625, (64, 128, 128))
        _a = jnp.logical_or(_a, jnp.swapaxes(_a, -1, -2))
        _a = jnp.logical_or(_a, jnp.eye(128, dtype=bool))
        _af = _a.astype(jnp.float32)
        adj = _af
        _nm = jnp.ones((64, 128), dtype=bool)
        nodemask = _nm
        return (x, adj, nodemask)
    x, adj, nodemask = _rec_inputs()

    def _L0_gnn_setup():
        import jax, jax.numpy as jnp
        import numpy as np
        B, N, DIN, DOUT = (8, 128, 64, 64)
        AVG_D_LOG = 4.86
        EPS = 1e-05
        NEG_BIG = 1000000000.0
        N_AGG, N_SCALE = (4, 3)

        def _pna_forward(x, adj, W_pre, b_pre, W_post, b_post):
            n = adj.shape[1]
            h_i = jnp.broadcast_to(x[:, :, None, :], (x.shape[0], n, n, x.shape[-1]))
            h_j = jnp.broadcast_to(x[:, None, :, :], (x.shape[0], n, n, x.shape[-1]))
            h_cat = jnp.concatenate([h_i, h_j], axis=-1)
            h_mod = jnp.einsum('bnme,ed->bnmd', h_cat, W_pre) + b_pre
            deg = adj.sum(-1)
            deg_safe = jnp.maximum(deg, 1.0)[..., None]
            mask = (adj > 0)[..., None]
            s1 = jnp.einsum('bnm,bnmd->bnd', adj, h_mod)
            mean = s1 / deg_safe
            s2 = jnp.einsum('bnm,bnmd->bnd', adj, h_mod * h_mod)
            var = jax.nn.relu(s2 / deg_safe - mean * mean)
            std = jnp.sqrt(var + EPS)
            mx = jnp.max(jnp.where(mask, h_mod, -NEG_BIG), axis=2)
            mn = jnp.min(jnp.where(mask, h_mod, NEG_BIG), axis=2)
            m = jnp.concatenate([mean, mx, mn, std], axis=-1)
            log_deg = jnp.log(deg + 1.0)[..., None]
            amp = m * (log_deg / AVG_D_LOG)
            att = m * (AVG_D_LOG / jnp.maximum(log_deg, EPS))
            m_all = jnp.concatenate([m, amp, att], axis=-1)
            m_cat = jnp.concatenate([x, m_all], axis=-1)
            return jnp.einsum('bne,ed->bnd', m_cat, W_post) + b_post
        key = jax.random.key(seed)
        k1, k2, k3, k4, k5, k6 = jax.random.split(key, 6)
        inp = jax.random.normal(k1, (B, N, DIN), dtype=jnp.float32)
        adj = jax.random.randint(k2, (B, N, N), 0, 2).astype(jnp.float32)
        W_pre = jax.random.normal(k3, (2 * DIN, DIN), dtype=jnp.float32) / np.sqrt(2 * DIN)
        b_pre = jnp.zeros((DIN,), dtype=jnp.float32)
        post_in = (N_AGG * N_SCALE + 1) * DIN
        W_post = jax.random.normal(k4, (post_in, DOUT), dtype=jnp.float32) / np.sqrt(post_in)
        b_post = jnp.zeros((DOUT,), dtype=jnp.float32)
        return {'input': inp, 'adj': adj, 'W_pre': W_pre, 'b_pre': b_pre, 'W_post': W_post, 'b_post': b_post}
    _L0_gnn_all = _L0_gnn_setup()
    _L0_gnn_in = {k: v for k, v in _L0_gnn_all.items() if k in ('W_pre', 'b_pre', 'W_post', 'b_post')}
    del _L0_gnn_all

    def _L1_gnn_setup():
        import jax, jax.numpy as jnp
        import numpy as np
        B, L, F = (8, 2048, 64)
        key = jax.random.key(seed)
        k1, k2, k3, k4 = jax.random.split(key, 4)
        text = jax.random.normal(k1, (B, L, F), dtype=jnp.float32)
        adj = jax.random.uniform(k2, (B, L, L), dtype=jnp.float32)
        weight = jax.random.normal(k3, (F, F), dtype=jnp.float32) * (1.0 / np.sqrt(F))
        bias = jax.random.normal(k4, (F,), dtype=jnp.float32) * 0.01
        return {'text': text, 'adj': adj, 'weight': weight, 'bias': bias}
    _L1_gnn_all = _L1_gnn_setup()
    _L1_gnn_in = {k: v for k, v in _L1_gnn_all.items() if k in ('weight', 'bias')}
    del _L1_gnn_all

    def _L2_gnn_setup():
        import jax, jax.numpy as jnp
        import numpy as np
        TAUS = [0.25, 0.5, 0.75]
        QWEIGHTS = [0.25, 0.5, 0.25]
        T_THRESH = 10
        K_DIL = 2
        EPS_GIN = 0.0

        def _dilate_adj(adj, mask):
            B, N, _ = adj.shape
            eye = jnp.eye(N, dtype=bool)
            adj_ = jnp.where(eye[None], 1.0, adj)
            nb = (adj_ > 0) & (~eye)[None]
            m = nb.sum(-1)
            rank = jnp.cumsum(nb, axis=-1) - 1
            skip = jnp.where(m > T_THRESH, (m + K_DIL - 1) // K_DIL, 1)
            do_dil = (skip > 1) & mask
            removed = nb & do_dil[..., None] & ((rank + 1) % skip[..., None] == 0)
            rem = removed | jnp.swapaxes(removed, 1, 2)
            return jnp.where(rem, 0.0, adj_)

        def _weighted_nanquantile_agg(x, valid):
            B, N, C = x.shape
            big = jnp.finfo(x.dtype).max / 4
            vals = jnp.where(valid[..., None], x[:, None, :, :], big)
            sv = jnp.sort(vals, axis=2)
            m = valid.sum(-1)
            mf = m.astype(x.dtype)

            def gather(idx):
                idxb = jnp.broadcast_to(idx[:, :, None, None], (B, N, 1, C))
                return jnp.take_along_axis(sv, idxb, axis=2)[:, :, 0, :]
            agg = jnp.zeros_like(x)
            for tau, wt in zip(TAUS, QWEIGHTS):
                pos = jnp.clip(tau * (mf - 1.0), 0.0)
                lo = jnp.floor(pos).astype(jnp.int32)
                hi = jnp.ceil(pos).astype(jnp.int32)
                frac = (pos - lo.astype(x.dtype))[..., None]
                q = gather(lo) * (1.0 - frac) + gather(hi) * frac
                agg = agg + wt * q
            return jnp.where((m > 0)[..., None], agg, 0.0)
        key = jax.random.key(seed)
        k0, k1, k2, k3 = jax.random.split(key, 4)
        B, N, C, H, CO = (4, 256, 64, 128, 64)
        x = jax.random.normal(k0, (B, N, C), dtype=jnp.float32)
        u = jax.random.uniform(k1, (B, N, N))
        a = (u < 0.03).astype(jnp.float32)
        adj = jnp.maximum(a, jnp.swapaxes(a, 1, 2))
        mask = jnp.broadcast_to(jnp.arange(N) < N - 32, (B, N))
        W1 = jax.random.normal(k2, (C, H), dtype=jnp.float32) * (1.0 / np.sqrt(C))
        b1 = jnp.zeros((H,), dtype=jnp.float32)
        W2 = jax.random.normal(k3, (H, CO), dtype=jnp.float32) * (1.0 / np.sqrt(H))
        b2 = jnp.zeros((CO,), dtype=jnp.float32)
        return {'x': x, 'adj': adj, 'mask': mask, 'W1': W1, 'b1': b1, 'W2': W2, 'b2': b2}
    _L2_gnn_all = _L2_gnn_setup()
    _L2_gnn_in = {k: v for k, v in _L2_gnn_all.items() if k in ('W1', 'b1', 'W2', 'b2')}
    del _L2_gnn_all

    def _L3_gnn_setup():
        import jax, jax.numpy as jnp
        import numpy as np
        key = jax.random.key(seed)
        k1, k2 = jax.random.split(key)
        B, N, D = (16, 1024, 64)
        nodes = jax.random.normal(k1, (B, N, D), dtype=jnp.float32)
        edges = jax.random.uniform(k2, (B, N, N), dtype=jnp.float32)
        return {'nodes': nodes, 'edges': edges}
    _L3_gnn_all = _L3_gnn_setup()
    _L3_gnn_in = {k: v for k, v in _L3_gnn_all.items() if k in ()}
    del _L3_gnn_all
    return {'x': x, 'adj': adj, 'nodemask': nodemask, 'L0_gnn_W_pre': _L0_gnn_in['W_pre'], 'L0_gnn_b_pre': _L0_gnn_in['b_pre'], 'L0_gnn_W_post': _L0_gnn_in['W_post'], 'L0_gnn_b_post': _L0_gnn_in['b_post'], 'L1_gnn_weight': _L1_gnn_in['weight'], 'L1_gnn_bias': _L1_gnn_in['bias'], 'L2_gnn_W1': _L2_gnn_in['W1'], 'L2_gnn_b1': _L2_gnn_in['b1'], 'L2_gnn_W2': _L2_gnn_in['W2'], 'L2_gnn_b2': _L2_gnn_in['b2']}

def reference(x, adj, nodemask, L0_gnn_W_pre, L0_gnn_b_pre, L0_gnn_W_post, L0_gnn_b_post, L1_gnn_weight, L1_gnn_bias, L2_gnn_W1, L2_gnn_b1, L2_gnn_W2, L2_gnn_b2):
    import jax
    import jax.numpy as jnp

    def _L0_gnn_ref(input, adj, W_pre, b_pre, W_post, b_post):
        import jax, jax.numpy as jnp
        import numpy as np
        B, N, DIN, DOUT = (8, 128, 64, 64)
        AVG_D_LOG = 4.86
        EPS = 1e-05
        NEG_BIG = 1000000000.0
        N_AGG, N_SCALE = (4, 3)

        def _pna_forward(x, adj, W_pre, b_pre, W_post, b_post):
            n = adj.shape[1]
            h_i = jnp.broadcast_to(x[:, :, None, :], (x.shape[0], n, n, x.shape[-1]))
            h_j = jnp.broadcast_to(x[:, None, :, :], (x.shape[0], n, n, x.shape[-1]))
            h_cat = jnp.concatenate([h_i, h_j], axis=-1)
            h_mod = jnp.einsum('bnme,ed->bnmd', h_cat, W_pre) + b_pre
            deg = adj.sum(-1)
            deg_safe = jnp.maximum(deg, 1.0)[..., None]
            mask = (adj > 0)[..., None]
            s1 = jnp.einsum('bnm,bnmd->bnd', adj, h_mod)
            mean = s1 / deg_safe
            s2 = jnp.einsum('bnm,bnmd->bnd', adj, h_mod * h_mod)
            var = jax.nn.relu(s2 / deg_safe - mean * mean)
            std = jnp.sqrt(var + EPS)
            mx = jnp.max(jnp.where(mask, h_mod, -NEG_BIG), axis=2)
            mn = jnp.min(jnp.where(mask, h_mod, NEG_BIG), axis=2)
            m = jnp.concatenate([mean, mx, mn, std], axis=-1)
            log_deg = jnp.log(deg + 1.0)[..., None]
            amp = m * (log_deg / AVG_D_LOG)
            att = m * (AVG_D_LOG / jnp.maximum(log_deg, EPS))
            m_all = jnp.concatenate([m, amp, att], axis=-1)
            m_cat = jnp.concatenate([x, m_all], axis=-1)
            return jnp.einsum('bne,ed->bnd', m_cat, W_post) + b_post
        return _pna_forward(input, adj, W_pre, b_pre, W_post, b_post)

    def _L1_gnn_ref(text, adj, weight, bias):
        import jax, jax.numpy as jnp
        import numpy as np
        B, L, F = (8, 2048, 64)
        hidden = jnp.einsum('blf,fo->blo', text, weight)
        out = jnp.einsum('bij,bjo->bio', adj, hidden)
        return out + bias

    def _L2_gnn_ref(x, adj, mask, W1, b1, W2, b2):
        import jax, jax.numpy as jnp
        import numpy as np
        TAUS = [0.25, 0.5, 0.75]
        QWEIGHTS = [0.25, 0.5, 0.25]
        T_THRESH = 10
        K_DIL = 2
        EPS_GIN = 0.0

        def _dilate_adj(adj, mask):
            B, N, _ = adj.shape
            eye = jnp.eye(N, dtype=bool)
            adj_ = jnp.where(eye[None], 1.0, adj)
            nb = (adj_ > 0) & (~eye)[None]
            m = nb.sum(-1)
            rank = jnp.cumsum(nb, axis=-1) - 1
            skip = jnp.where(m > T_THRESH, (m + K_DIL - 1) // K_DIL, 1)
            do_dil = (skip > 1) & mask
            removed = nb & do_dil[..., None] & ((rank + 1) % skip[..., None] == 0)
            rem = removed | jnp.swapaxes(removed, 1, 2)
            return jnp.where(rem, 0.0, adj_)

        def _weighted_nanquantile_agg(x, valid):
            B, N, C = x.shape
            big = jnp.finfo(x.dtype).max / 4
            vals = jnp.where(valid[..., None], x[:, None, :, :], big)
            sv = jnp.sort(vals, axis=2)
            m = valid.sum(-1)
            mf = m.astype(x.dtype)

            def gather(idx):
                idxb = jnp.broadcast_to(idx[:, :, None, None], (B, N, 1, C))
                return jnp.take_along_axis(sv, idxb, axis=2)[:, :, 0, :]
            agg = jnp.zeros_like(x)
            for tau, wt in zip(TAUS, QWEIGHTS):
                pos = jnp.clip(tau * (mf - 1.0), 0.0)
                lo = jnp.floor(pos).astype(jnp.int32)
                hi = jnp.ceil(pos).astype(jnp.int32)
                frac = (pos - lo.astype(x.dtype))[..., None]
                q = gather(lo) * (1.0 - frac) + gather(hi) * frac
                agg = agg + wt * q
            return jnp.where((m > 0)[..., None], agg, 0.0)
        dtp = x.dtype
        adj_d = _dilate_adj(adj, mask)
        agg = _weighted_nanquantile_agg(x, adj_d > 0)
        out = (1.0 + EPS_GIN) * x + agg
        h = jax.nn.relu(jnp.einsum('bnc,ch->bnh', out, W1) + b1)
        y = jnp.einsum('bnh,ho->bno', h, W2) + b2
        return y * mask[..., None].astype(dtp)

    def _L3_gnn_ref(nodes, edges):
        import jax, jax.numpy as jnp
        import numpy as np
        N = nodes.shape[1]
        A = edges + jnp.eye(N, dtype=edges.dtype)
        num = jnp.einsum('bij,bjd->bid', A, nodes)
        denom = jnp.sum(A, axis=2, keepdims=True)
        out = num / denom
        return jnp.where(jnp.isnan(out), jnp.zeros_like(out), out)
    x = _layernorm(x + _L0_gnn_ref(x, adj, L0_gnn_W_pre, L0_gnn_b_pre, L0_gnn_W_post, L0_gnn_b_post), axis=-1)
    x = _layernorm(x + _L1_gnn_ref(x, adj, L1_gnn_weight, L1_gnn_bias), axis=-1)
    x = _layernorm(x + _L2_gnn_ref(x, adj, nodemask, L2_gnn_W1, L2_gnn_b1, L2_gnn_W2, L2_gnn_b2), axis=-1)
    x = _layernorm(x + _L3_gnn_ref(x, adj), axis=-1)
    return x

_drawn_inputs = setup_inputs


def setup_inputs(seed=0):
    import zlib

    import numpy as np

    out = dict(_drawn_inputs(seed))
    spreads = {'L0_gnn_b_pre': (0.0, 0.1),
     'L0_gnn_b_post': (0.0, 0.1),
     'L2_gnn_b1': (0.0, 0.1),
     'L2_gnn_b2': (0.0, 0.1)}
    factors = {'L1_gnn_bias': 8.0}
    for name, (base, spread) in spreads.items():
        noise = np.random.default_rng([zlib.crc32(name.encode()), seed]).standard_normal(out[name].shape)
        drawn = base * np.exp(spread * noise) if base else spread * noise
        out[name] = jnp.asarray(drawn.astype(out[name].dtype))
    for name, factor in factors.items():
        out[name] = (out[name] * factor).astype(out[name].dtype)
    return out
```

```python
from contextlib import ExitStack

import numpy as np

import concourse.bass as bass
from concourse import mybir

ALU = mybir.AluOpType
ACT = mybir.ActivationFunctionType
AX = mybir.AxisListType
F32 = mybir.dt.float32
BF16 = mybir.dt.bfloat16
I32 = mybir.dt.int32
U8 = mybir.dt.uint8

B, N, D, H = 64, 128, 64, 128
G = 4
NG = B // G
C = G * D
HC = 64
LN_EPS = 1e-5
PNA_EPS = 1e-5
AVG_D_LOG = 4.86
DILATE_ABOVE = 10.0
TAUS = (0.25, 0.5, 0.75)
QUANTILE_WEIGHTS = (0.25, 0.5, 0.25)
NEG_BIG = 1.0e9
BIG_PARTS = (999292928.0, 708608.0, -1536.0)
ROUND = 8388608.0
FLT_MAX = 3.4028234e38
NPART = len(BIG_PARTS)
KP = NPART * G

K0 = 13
K2 = 11
K0B = (K0 + 1) // 2
K2B = (K2 + 1) // 2
HOTS = K0 + K2
RING = 8
assert HOTS % RING == 0

NETWORK = (
    ((0, 9), (1, 6), (2, 4), (3, 7), (5, 8)),
    ((0, 1), (3, 5), (4, 10), (6, 9), (7, 8)),
    ((1, 3), (2, 5), (4, 7), (8, 10)),
    ((0, 4), (1, 2), (3, 7), (5, 9), (6, 8)),
    ((0, 1), (2, 6), (4, 5), (7, 8), (9, 10)),
    ((2, 4), (3, 6), (5, 7), (8, 9)),
    ((1, 2), (3, 4), (5, 6), (7, 8)),
    ((2, 3), (4, 5), (6, 7)),
)
PLACE = (10, 9, 8, 6, 2, 7, 3, 0, 1, 4, 5)
RANKS = int(np.ceil(max(TAUS) * (K2 - 1))) + 1


def plan_sort():
    live = set(range(RANKS))
    layers = []
    for layer in reversed(NETWORK):
        kept = [(a, b, a in live, b in live) for a, b in layer if a in live or b in live]
        for a, b, _, _ in kept:
            live |= {a, b}
        layers.append(kept)
    layers.reverse()
    side = [0] * K2
    plan = []
    for layer in layers:
        steps = []
        for is_min in (True, False):
            todo = []
            for a, b, low, high in layer:
                if low if is_min else high:
                    x, y = (a, b) if PLACE[a] < PLACE[b] else (b, a)
                    out = a if is_min else b
                    todo.append((PLACE[x], PLACE[y], side[x], side[y], out == x))
            todo.sort()
            while todo:
                first = todo[0]
                best = [first]
                for second in todo[1:]:
                    dx, dy = second[0] - first[0], second[1] - first[1]
                    if dx <= 0 or dy <= 0 or second[2:] != first[2:]:
                        continue
                    run = [first]
                    while (first[0] + len(run) * dx, first[1] + len(run) * dy) + first[2:] in todo:
                        run.append((first[0] + len(run) * dx, first[1] + len(run) * dy) + first[2:])
                    if len(run) > len(best):
                        best = run
                for x in best:
                    todo.remove(x)
                n = len(best)
                dx = best[1][0] - first[0] if n > 1 else 1
                dy = best[1][1] - first[1] if n > 1 else 1
                in0, in1 = (first[2], first[0], dx, n), (first[3], first[1], dy, n)
                src = in0 if first[4] else in1
                steps.append((is_min, in0, in1, (1 - src[0],) + src[1:]))
        for a, b, _, _ in layer:
            side[a] ^= 1
            side[b] ^= 1
        plan.append(steps)
    ends = []
    todo = sorted((PLACE[r], side[r]) for r in range(RANKS))
    while todo:
        p, s = todo[0]
        best = [(p, s)]
        for q, z in todo[1:]:
            run = [(p, s)]
            while z == s and (p + len(run) * (q - p), s) in todo:
                run.append((p + len(run) * (q - p), s))
            if len(run) > len(best):
                best = run
        for x in best:
            todo.remove(x)
        ends.append((s, p, best[1][0] - p if len(best) > 1 else 1, len(best)))
    return plan, ends


class Turn:

    def __init__(self, i, offset, past=0):
        self.g = offset if i is None else i * 2 + offset
        self.n = self.g + past
        self.u = offset % 2
        self.half = past // 2 + (offset // 2 if i is None else i + offset // 2)
        self.least = offset + past
        self.fast = past == 0
        self.i = i


def adj_kernel(nc, x_pairs, adj_rows, adj_cols, node_mask, w_pre, b_pre, w_post, b_post,
               w_l1, b_l1, w1, b1, w2, b2, out):
    with ExitStack() as ctx:
        def sb(name, shape, dt=F32):
            return ctx.enter_context(nc.sbuf_tensor(name, shape, dt))

        def sem(name):
            return ctx.enter_context(nc.semaphore(name))

        bank = [ctx.enter_context(nc.psum_tensor(f"bank{k}", [128, 512], F32)) for k in range(8)]
        PA, PA2, PB, PB2, RG0, RG1, PX, PX2 = bank
        GATHER = (RG0, RG1)

        ident = sb("ident", [128, 128])
        identb = sb("identb", [128, 128], BF16)
        upto = sb("upto", [128, 128], BF16)
        onesf = sb("onesf", [128, 128])
        onesb = sb("onesb", [128, 1], BF16)
        column = sb("column", [128, G, KP], BF16)
        fill = sb("fill", [KP, 2, G, D], BF16)
        parts = sb("parts", [KP, 2])
        partsum = sb("partsum", [KP, NPART])
        row_id = sb("row_id", [128, 1])
        row_idi = sb("row_idi", [128, 1], I32)
        sqrt_eps = sb("sqrt_eps", [128, 2])
        raw = sb("raw", [128, 10, D])
        rawmean = sb("rawmean", [128, 10])
        bd = sb("bd", [128, 6, 2, D])
        wpost = sb("wpost", [128, 2, 3, D])
        w1t = sb("w1t", [128, 2, H])
        b1t = sb("b1t", [128, 1])
        biasr = sb("biasr", [1, 4, D])
        biasm = sb("biasm", [1, 4])
        biast = sb("biast", [1, 4, G, D])
        rank_of = sb("rank_of", [128, 3, K2, G])
        tau_w = sb("tau_w", [128, 3, K2, G])
        mask8 = sb("mask8", [128, B], U8)

        adj_all = sb("adj_all", [128, B, N])
        deg = sb("deg", [128, B])
        rows = sb("rows", [128, 6, B])
        rtmp = sb("rtmp", [128, 2, B])
        INV, RATIO, AMP, ATT, RDEN, MASK = range(6)
        mostn = sb("mostn", [128, 2])
        most = sb("most", [128, 2])
        over = sb("over", [1, 1])
        overi = sb("overi", [1, 1], I32)

        adjT = [sb(f"adjT{u}", [128, G, N]) for u in range(2)]
        adjB = [sb(f"adjB{u}", [128, G, N]) for u in range(2)]
        xT0 = [sb(f"xT0_{u}", [128, G // 2, N]) for u in range(2)]
        rowc = [sb(f"rowc{u}", [128, 6, G]) for u in range(2)]
        rowb = sb("rowb", [128, 2, G])
        maskT = sb("maskT", [128, G, N], BF16)
        nbN = sb("nbN", [128, G, N], BF16)
        nbT = sb("nbT", [128, G, N], BF16)
        selfT = sb("selfT", [128, G, N], BF16)
        keyN = sb("keyN", [128, G, N], BF16)
        drop = sb("drop", [128, G, N], BF16)
        drop2 = sb("drop2", [128, G, N], BF16)
        validT = sb("validT", [128, G, N], BF16)
        key1 = sb("key1", [128, G, N], BF16)
        key2 = sb("key2", [128, G, N], BF16)
        hot = sb("hot", [128, RING, G, N], BF16)
        cnt = sb("cnt", [128, 3, G])
        cntT1 = sb("cntT1", [KP, N])
        cntT2 = sb("cntT2", [KP, N])
        empty1 = sb("empty1", [KP, K0, N], BF16)
        empty2 = sb("empty2", [KP, K2, N], BF16)
        skp = sb("skp", [128, 6, G])
        QQ = sb("QQ", [128, G, 2, D])
        pS = sb("pS", [128, G, D])
        rp = sb("rp", [128, G, D])
        hml = sb("hml", [128, 3, G, D], BF16)
        rest = sb("rest", [128, 2, G, D])
        ac = sb("ac", [128, G, 2, D])
        asq = sb("asq", [128, G, D])
        wpt = sb("wpt", [128, 2, G, D])
        vr = sb("vr", [128, G, D])
        m4 = sb("m4", [128, G, 4, D])
        mT = sb("mT", [128, 2, G, N])
        slotP = sb("slotP", [128, 2 * K0B, C])
        slotM = sb("slotM", [128, 2 * K0B, C])
        ys = sb("ys", [128, 2, G, D])
        off = slotP[:, 0:2, :].rearrange("p k c -> p (k c)").rearrange("p (g n) -> p g n", g=G)
        gmax = slotP[:, 2, :].rearrange("p (g d) -> p g d", g=G)
        gmin = slotP[:, 3, :].rearrange("p (g d) -> p g d", g=G)
        gtmp = slotP[:, 4:6, :].rearrange("p k (g d) -> p k g d", g=G)
        earlier = slotP[:, 6, 0:128]
        validN = hot[:, 0, :, :]
        selfN = hot[:, 1, :, :]
        below = hot[:, 2:4, :, :].rearrange("p k g n -> p (k g n)")[:, 0:C].rearrange("p (g d) -> p g d", g=G)
        pick = hot[:, 4, 0, :]
        excess = sb("excess", [128, 3])
        zf = sb("zf", [128, G, D])
        sqf = sb("sqf", [128, C])
        stf = sb("stf", [128, 3, G])
        x1 = sb("x1", [128, G, D])
        x1T = sb("x1T", [128, G // 2, N])
        h1 = sb("h1", [128, G, D])
        x2 = [sb(f"x2_{u}", [128, G, D]) for u in range(2)]
        slot2 = [sb(f"slot2_{u}", [128, 2 * K2B, C]) for u in range(2)]
        swap = sb("swap", [128, K2, C])
        prod = sb("prod", [128, RANKS, C])
        hatd = sb("hatd", [128, 3, K2, G])
        hatn = sb("hatn", [128, 3, K2, G])
        post = sb("post", [128, 3, G])
        rankw = [sb(f"rankw{u}", [128, K2, G]) for u in range(2)]
        o2 = sb("o2", [128, G, D])
        o2T = sb("o2T", [128, G // 2, N])
        x2T = sb("x2T", [128, G // 2, N])
        hT = sb("hT", [128, G, N])
        yb = sb("yb", [128, G, D])
        zb = sb("zb", [128, G, D])
        sqb = sb("sqb", [128, C])
        stb = sb("stb", [128, 3, G])
        x3 = sb("x3", [128, G, D])
        x3T = sb("x3T", [128, G // 2, N])
        x3c = sb("x3c", [128, G, D])
        xo = [sb(f"xo{u}", [128, G, D]) for u in range(2)]

        plan, ends = plan_sort()

        def slots(buffers, run):
            s, first, stride, n = run
            return buffers[s][:, first:first + stride * (n - 1) + 1:stride, :]

        w_in = sem("w_in")
        deg_in = [sem(f"deg_in{k}") for k in range(4)]
        made_pool = sem("made_pool")
        made_dve = sem("made_dve")
        logs_in = sem("logs_in")
        logs = sem("logs")
        over_a, over_b, over_c = (sem(f"over_{k}") for k in "abc")

        names = """maskT nbN0 nbN nbT selfT rowc pos1_ps key1 cnt_ps cnts posN_ps keyN drop rem_ps
            validT qp_ps qs qh ps rpS rest1 qm parts1 ac_ps acs asq mean stt vsum std pos2_ps key2 cnt2_ps
            cnt2s empty1 empty2 hot slot_ps slotP minus_ps slotM extremes mT_ps mTs y_ps yss ysum sqf
            varf sdf x1 x1T_ps x1Ts h1_ps h1s z1_ps sq1 var1 sd1 x2 xh xrest1 xm parts2 slot2_ps slot2
            rankw o2 o2T_ps o2Ts hT_ps hTs y2_ps y2sum sq2 var2 sd2 x3 x3T_ps x3Ts x3c_ps x3cs z3_ps
            z3sum sq3 var3 sd3 xo selfN pick row_ps below below_ps seen_pool chain_dve chain_pool""".split()
        s = {n: sem(n) for n in names}
        adj_in = [sem(f"adj_in{u}") for u in range(2)]
        adjB_in = [sem(f"adjB_in{u}") for u in range(2)]
        x_in = [sem(f"x_in{u}") for u in range(2)]
        stored = [sem(f"stored{u}") for u in range(2)]

        def done(eng, name, t, per=1, k=None):
            eng.wait_ge(s[name], t.n * per + (per if k is None else k))

        def before(eng, name, t, back=1, per=1, k=None):
            if t.least >= back:
                eng.wait_ge(s[name], (t.n - back) * per + (per if k is None else k))

        WEIGHT_LOADS = 23
        MADE_POOL = 3

        def load_group(eng, t):
            before(eng, "z1_ps", t, 2)
            eng.dma_start(adjT[t.u][:], adj_cols[:, bass.ds(t.g * G, G), :]).then_inc(adj_in[t.u], 16)
            eng.dma_start(xT0[t.u][:], x_pairs[:, bass.ds(t.g * (G // 2), G // 2), :]).then_inc(x_in[t.u], 16)

        def load_back(eng, t):
            before(eng, "z3_ps", t, 2)
            eng.dma_start(adjB[t.u][:], adj_cols[:, bass.ds(t.g * G, G), :]).then_inc(adjB_in[t.u], 16)

        def store_group(eng, t):
            done(eng, "xo", t)
            eng.dma_start(out[:, bass.ds(t.g * G, G), :], xo[t.u][:]).then_inc(stored[t.u], 16)

        def sync_fast(sp):
            small = [(raw[0:64, 0, :], w_post[0:64, :]), (raw[64:128, 0, :], w_post[0:64, :]),
                     (raw[0:64, 1, :], w_l1), (raw[64:128, 1, :], w_l1), (raw[:, 9, :], w2),
                     (bd[0:64, 0, 0, :], w_pre[64:128, :]), (bd[64:128, 0, 1, :], w_pre[64:128, :]),
                     (bd[0:64, 1, 0, :], w_pre[0:64, :]), (bd[64:128, 1, 1, :], w_pre[0:64, :]),
                     (w1t[0:64, 0, :], w1), (w1t[64:128, 1, :], w1),
                     (b1t[:, :], b1.rearrange("(h a) -> h a", a=1)), (mask8[:, :], node_mask)]
            for k in range(2):
                for f in range(3):
                    r = D + f * 4 * D + k * 2 * D
                    small.append((raw[:, 3 + 3 * k + f, :], w_post[r:r + 128, :]))
            for k, b in enumerate((b_pre, b_post, b_l1, b2)):
                small.append((biasr[0:1, k, :], b.rearrange("(a d) -> a d", a=1)))
            assert len(small) == WEIGHT_LOADS
            sp.wait_ge(made_pool, 1)
            for k in range(4):
                sp.dma_start(adj_all[:, k * 16:(k + 1) * 16, :],
                             adj_rows[:, k * 16:(k + 1) * 16, :]).then_inc(deg_in[k], 16)
                if k == 0:
                    for dst, src in small:
                        sp.dma_start(dst, src).then_inc(w_in, 16)
                    load_group(sp, Turn(None, 0))
            load_group(sp, Turn(None, 1))
            with sp.Fori(0, NG // 2 - 1) as i:
                load_group(sp, Turn(i, 2))
                load_back(sp, Turn(i, 0))
                store_group(sp, Turn(i, 0))
                load_group(sp, Turn(i, 3))
                load_back(sp, Turn(i, 1))
                store_group(sp, Turn(i, 1))
            for t in (NG - 2, NG - 1):
                load_back(sp, Turn(None, t))
                store_group(sp, Turn(None, t))
            for u in range(2):
                sp.wait_ge(stored[u], 16 * (NG // 2))

        ORDER = ("f1", "b1", "f2", "b2", "f3", "b3", "f4", "b4", "b5", "b6", "f5", "f6",
                 "f7", "f8", "f9", "f10")

        def one_slot(part, t, back, front):
            for step in ORDER:
                group = back if step[0] == "b" else front
                if group is not None and step in part:
                    part[step](group)

        def all_slots(eng, part, slot):
            one_slot(part, None, None, Turn(None, 0))
            slot(Turn(None, 0), None, Turn(None, 1))
            with eng.Fori(0, NG // 2 - 1) as i:
                slot(Turn(i, 1), Turn(i, 0), Turn(i, 2))
                slot(Turn(i, 2), Turn(i, 1), Turn(i, 3))
            slot(Turn(None, NG - 1), Turn(None, NG - 2), None)
            one_slot(part, None, Turn(None, NG - 1), None)

        def tensor_steps(pe):
            mm = nc.tensor.matmul

            def pair(k):
                return bd[:, k, :, :].rearrange("p a d -> p (a d)")

            def flat(ap):
                return ap.rearrange("p g n -> p (g n)")

            def bias(k):
                return biast[0:1, k, :, :].rearrange("a g d -> a (g d)")

            def two(ps, p):
                return ps[:, p * 128:(p + 1) * 128]

            def f1(t):
                done(pe, "maskT", t)
                before(pe, "ysum", t)
                mm(PB[:, :], upto[:, :], flat(maskT[:, :, :]), start=True, stop=True).then_inc(s["pos1_ps"], 1)
                before(pe, "h1s", t)
                done(pe, "nbT", t)
                for g in range(G):
                    mm(PA[:, g:g + 1], nbT[:, g, :], onesb[:, :], start=True, stop=True)
                    mm(PA[:, 8 + g:9 + g], maskT[:, g, :], onesb[:, :], start=True, stop=True)
                for g in range(G):
                    last = mm(PA[0:KP, 128:256], column[:, g, :], maskT[:, g, :], start=g == 0, stop=g == G - 1)
                last.then_inc(s["cnt_ps"], 1)
                done(pe, "key1", t)
                for g in range(G):
                    last = mm(PB[:, g * N:(g + 1) * N], nbT[:, g, :], upto[:, :], start=True, stop=True)
                last.then_inc(s["posN_ps"], 1)

            def f2(t):
                pe.wait_ge(x_in[t.u], t.half * 16 + 16)
                before(pe, "mTs", t, 1, 2)
                for p in range(G // 2):
                    mm(two(PA2, p), xT0[t.u][:, p, :], pair(0), start=True, stop=True)
                mm(PA2[:, C:2 * C], onesf[0:1, :], bias(0), start=True, stop=False, skip_group_check=True)
                for p in range(G // 2):
                    last = mm(two(PA2, p + G // 2), xT0[t.u][:, p, :], pair(1),
                              start=False, stop=True, skip_group_check=True)
                last.then_inc(s["qp_ps"], 1)

            def f3(t):
                done(pe, "qs", t)
                done(pe, "cnts", t)
                pe.wait_ge(adj_in[t.u], t.half * 16 + 16)
                for g in range(G):
                    last = mm(two(PA, g), adjT[t.u][:, g, :], QQ[:, g, :, :].rearrange("p a d -> p (a d)"),
                              start=True, stop=True)
                last.then_inc(s["ac_ps"], 1)
                done(pe, "drop", t)
                done(pe, "keyN", t)
                for g in range(G):
                    mm(two(PB, g), drop[:, g, :], identb[:, :], start=True, stop=False)
                    last = mm(two(PB, g), identb[:, :], drop[:, g, :], start=False, stop=True)
                last.then_inc(s["rem_ps"], 1)

            def f4(t):
                done(pe, "validT", t)
                mm(PB[:, :], upto[:, :], flat(validT[:, :, :]), start=True, stop=True).then_inc(s["pos2_ps"], 1)
                done(pe, "acs", t)
                for g in range(G):
                    mm(PA[:, g:g + 1], validT[:, g, :], onesb[:, :], start=True, stop=True)
                for g in range(G):
                    last = mm(PA[0:KP, 128:256], column[:, g, :], validT[:, g, :], start=g == 0, stop=g == G - 1)
                last.then_inc(s["cnt2_ps"], 1)

            def gather_slot(t, ps, half, slot, hot0, empty):
                k = hot0 + slot
                mm(ps[:, half * C:(half + 1) * C], empty[:, slot, :], flat(fill[:, 0, :, :]),
                   start=half == 0, stop=False, skip_group_check=True)
                pe.wait_ge(s["hot"], t.n * HOTS + k + 1)
                for g in range(G):
                    for part in range(3):
                        last = mm(ps[:, half * C + g * D:half * C + (g + 1) * D], hot[:, k % RING, g, :],
                                  hml[:, part, g, :], start=False, stop=True, skip_group_check=True)
                return last

            def f5(t):
                done(pe, "parts1", t)
                done(pe, "empty1", t)
                before(pe, "slot2", t, 1, K2B)
                for b in range(K0B + 1):
                    if b < K0B:
                        if b >= 2:
                            done(pe, "slotM", t, K0B, b - 1)
                        for half in range(2):
                            if 2 * b + half < K0:
                                last = gather_slot(t, GATHER[b % 2], half, 2 * b + half, 0, empty1)
                        last.then_inc(s["slot_ps"], 1)
                    if b >= 1:
                        done(pe, "slotP", t, K0B, b)
                        for half in range(2):
                            slot = 2 * (b - 1) + half
                            if slot < K0:
                                last = mm(GATHER[(b - 1) % 2][:, half * C:(half + 1) * C], empty1[:, slot, :],
                                          flat(fill[:, 1, :, :]), start=False, stop=True, skip_group_check=True)
                        last.then_inc(s["minus_ps"], 1)

            def f6(t):
                done(pe, "extremes", t)
                done(pe, "std", t)
                done(pe, "cnt2s", t)
                done(pe, "rpS", t)
                for k in range(2):
                    for g in range(G):
                        last = nc.tensor.transpose(two((PA, PA2)[k], g),
                                                   m4[:, g, 2 * k:2 * k + 2, :].rearrange("p a d -> p (a d)"),
                                                   ident[:, :])
                    last.then_inc(s["mT_ps"], 1)

            def f7(t):
                done(pe, "key2", t)
                before(pe, "x2", t)
                done(pe, "mTs", t, 2)
                for p in range(G // 2):
                    both = (PB, PB2)[p][:, 0:6 * D].rearrange("p (a f d) -> p a f d", a=2, f=3)
                    mm(both[:, :, 0, :], onesf[0:1, :], biast[0:1, 1, 0:2, :], start=True, stop=False,
                       skip_group_check=True)
                    mm(both[:, :, 0, :], xT0[t.u][:, p, :], bd[:, 2, :, :], start=False, stop=False,
                       skip_group_check=True)
                    for a in range(2):
                        for k in range(2):
                            last = mm(both[:, a, :, :], mT[:, k, 2 * p + a, :], wpost[:, k, :, :],
                                      start=False, stop=True, skip_group_check=True)
                last.then_inc(s["y_ps"], 1)

            def f8(t):
                done(pe, "x1", t)
                for p in range(G // 2):
                    last = nc.tensor.transpose(two(PA, p), x1[:, 2 * p:2 * p + 2, :].rearrange("p a d -> p (a d)"),
                                               ident[:, :])
                last.then_inc(s["x1T_ps"], 1)
                done(pe, "x1Ts", t)
                for p in range(G // 2):
                    last = mm(two(PA, p + G // 2), x1T[:, p, :], pair(3), start=True, stop=True)
                last.then_inc(s["h1_ps"], 1)

            def f9(t):
                done(pe, "ysum", t)
                mm(PB2[:, 0:C], onesf[0:1, :], bias(2), start=True, stop=False, skip_group_check=True)
                for p in range(G // 2):
                    mm(two(PB2, p), x1T[:, p, :], pair(4), start=False, stop=False, skip_group_check=True)
                done(pe, "h1s", t)
                for g in range(G):
                    last = mm(PB2[:, g * D:(g + 1) * D], adjT[t.u][:, g, :], h1[:, g, :],
                              start=False, stop=True, skip_group_check=True)
                last.then_inc(s["z1_ps"], 1)

            def f10(t):
                done(pe, "parts2", t)
                done(pe, "empty2", t)
                done(pe, "slotM", t, K0B)
                for b in range(K2B):
                    if b >= 2:
                        done(pe, "slot2", t, K2B, b - 1)
                    for half in range(2):
                        if 2 * b + half < K2:
                            last = gather_slot(t, GATHER[b % 2], half, 2 * b + half, K0, empty2)
                    last.then_inc(s["slot2_ps"], 1)

            def b1(t):
                done(pe, "o2", t)
                before(pe, "z3sum", t)
                for p in range(G // 2):
                    nc.tensor.transpose(two(PX, p + G // 2),
                                        x2[t.u][:, 2 * p:2 * p + 2, :].rearrange("p a d -> p (a d)"), ident[:, :])
                for p in range(G // 2):
                    last = nc.tensor.transpose(two(PX, p), o2[:, 2 * p:2 * p + 2, :].rearrange("p a d -> p (a d)"),
                                               ident[:, :])
                last.then_inc(s["o2T_ps"], 1)

            def b2(t):
                done(pe, "o2Ts", t)
                before(pe, "x3cs", t)
                for a in range(2):
                    last = mm(PX2[:, a * C:(a + 1) * C], w1t[:, a, :], flat(o2T[:, :, :]), start=True, stop=True)
                last.then_inc(s["hT_ps"], 1)

            def b3(t):
                mm(PX[:, 0:C], onesf[0:1, :], bias(3), start=True, stop=False, skip_group_check=True)
                for p in range(G // 2):
                    mm(two(PX, p + G // 2), x2T[:, p, :], pair(4), start=False, stop=True, skip_group_check=True)
                done(pe, "hTs", t)
                for g in range(G):
                    last = mm(PX[:, g * D:(g + 1) * D], hT[:, (g % 2) * (G // 2) + g // 2, :], raw[:, 9, :],
                              start=False, stop=True, skip_group_check=True)
                last.then_inc(s["y2_ps"], 1)

            def b4(t):
                done(pe, "x3", t)
                for p in range(G // 2):
                    last = nc.tensor.transpose(two(PX, p), x3[:, 2 * p:2 * p + 2, :].rearrange("p a d -> p (a d)"),
                                               ident[:, :])
                last.then_inc(s["x3T_ps"], 1)

            def b5(t):
                done(pe, "x3Ts", t)
                for p in range(G // 2):
                    last = mm(two(PX2, p), x3T[:, p, :], pair(4), start=True, stop=True)
                last.then_inc(s["x3c_ps"], 1)

            def b6(t):
                done(pe, "x3cs", t)
                pe.wait_ge(adjB_in[t.u], t.half * 16 + 16)
                for g in range(G):
                    last = mm(PX[:, g * D:(g + 1) * D], adjB[t.u][:, g, :], x3c[:, g, :], start=True, stop=True)
                last.then_inc(s["z3_ps"], 1)

            def general0(t):
                with pe.Fori(0, N) as m:
                    done(pe, "parts1", t)
                    node_row(t, m, 0)

            def general2(t):
                with pe.Fori(0, N) as m:
                    done(pe, "parts2", t)
                    node_row(t, m, N)
                    pe.wait_ge(s["below"], t.g * N + m + 1)
                    for g in range(G):
                        last = mm(RG1[:, g * D:(g + 1) * D], validT[:, g, :], below[:, g, :], start=True, stop=True)
                    last.then_inc(s["below_ps"], 1)

            def node_row(t, m, offset):
                pe.wait_ge(s["pick"], t.g * (2 * N) + m + offset + 1)
                for part in range(3):
                    last = mm(RG0[:, 0:C], pick, flat(hml[:, part, :, :]), start=part == 0, stop=part == 2)
                last.then_inc(s["row_ps"], 1)

            return dict(f1=f1, f2=f2, f3=f3, f4=f4, f5=f5, f6=f6, f7=f7, f8=f8, f9=f9, f10=f10, b1=b1, b2=b2,
                        b3=b3, b4=b4, b5=b5, b6=b6, general0=general0, general2=general2)

        def tensor_fast(pe):
            part = tensor_steps(pe)
            pe.wait_ge(made_pool, MADE_POOL)
            pe.wait_ge(made_dve, 1)
            all_slots(pe, part, lambda t, back, front: one_slot(part, t, back, front))
            pe.wait_ge(over_a, 1)
            nc.tensor.transpose(PX[0:1, 0:128], excess[:, 2:3], ident[:, :]).then_inc(over_b, 1)

        def scalar_steps(act):
            A = nc.scalar.activation

            def flat(ap):
                return ap.rearrange("p g d -> p (g d)")

            def root(t, st, ready, signal):
                done(act, ready, t)
                A(st[:, 1, :], st[:, 0, :], ACT.Sqrt, bias=sqrt_eps[:, 1:2], scale=1.0 / D).then_inc(s[signal], 1)

            def f1(t):
                done(act, "cnt_ps", t)
                A(cnt[:, 0, :], PA[:, 0:G], ACT.Copy)
                A(cnt[:, 1, :], PA[:, 8:8 + G], ACT.Copy)
                A(cntT1[:, :], PA[0:KP, 128:256], ACT.Copy).then_inc(s["cnts"], 1)

            def f2(t):
                q = PA2[:, 0:C].rearrange("p (g d) -> p g d", g=G)
                done(act, "qp_ps", t)
                if t.fast:
                    before(act, "slot2_ps", t, 1, K2B)
                A(QQ[:, :, 0, :], q, ACT.Copy)
                A(QQ[:, :, 1, :], q, ACT.Square).then_inc(s["qs"], 1)
                A(flat(hml[:, 0, :, :]), PA2[:, 0:C], ACT.Copy).then_inc(s["qh"], 1)
                A(flat(pS[:, :, :]), PA2[:, C:2 * C], ACT.Copy).then_inc(s["ps"], 1)
                done(act, "rowc", t)
                for g in range(G):
                    last = A(rp[:, g, :], PA2[:, C + g * D:C + (g + 1) * D], ACT.Copy,
                             scale=rowc[t.u][:, RATIO, g:g + 1])
                last.then_inc(s["rpS"], 1)
                done(act, "rest1", t)
                A(flat(hml[:, 1, :, :]), flat(rest[:, 0, :, :]), ACT.Copy).then_inc(s["qm"], 1)

            def f3(t):
                done(act, "ac_ps", t)
                for g in range(G):
                    last = A(ac[:, g, :, :].rearrange("p a d -> p (a d)"), PA[:, g * 128:(g + 1) * 128], ACT.Copy,
                             scale=rowc[t.u][:, INV, g:g + 1])
                last.then_inc(s["acs"], 1)
                done(act, "acs", t)
                A(asq[:, :, :], ac[:, :, 0, :], ACT.Square).then_inc(s["asq"], 1)

            def f4(t):
                done(act, "cnt2_ps", t)
                A(cnt[:, 2, :], PA[:, 0:G], ACT.Copy)
                A(cntT2[:, :], PA[0:KP, 128:256], ACT.Copy).then_inc(s["cnt2s"], 1)
                done(act, "vsum", t)
                A(m4[:, :, 3, :], vr[:, :, :], ACT.Sqrt, bias=sqrt_eps[:, 0:1]).then_inc(s["std"], 1)

            def f5(t):
                for b in range(K0B + 1):
                    if b < K0B:
                        n = min(2, K0 - 2 * b)
                        done(act, "slot_ps", t, K0B, b + 1)
                        A(flat(slotP[:, 2 * b:2 * b + n, :]), GATHER[b % 2][:, 0:n * C],
                          ACT.Copy).then_inc(s["slotP"], 1)
                    if b >= 1:
                        n = min(2, K0 - 2 * (b - 1))
                        done(act, "minus_ps", t, K0B, b)
                        A(flat(slotM[:, 2 * b - 2:2 * b - 2 + n, :]), GATHER[(b - 1) % 2][:, 0:n * C],
                          ACT.Copy).then_inc(s["slotM"], 1)

            def f6(t):
                for k in range(2):
                    done(act, "mT_ps", t, 2, k + 1)
                    A(flat(mT[:, k, :, :]), (PA, PA2)[k][:, :], ACT.Copy).then_inc(s["mTs"], 1)

            def f7(t):
                done(act, "y_ps", t)
                for f, which in ((1, AMP), (2, ATT)):
                    for g in range(G):
                        o = (g % 2) * 3 * D + f * D
                        last = A(ys[:, f - 1, g, :], (PB, PB2)[g // 2][:, o:o + D], ACT.Copy,
                                 scale=rowc[t.u][:, which, g:g + 1])
                last.then_inc(s["yss"], 1)
                done(act, "ysum", t)
                A(sqf[:, :], flat(zf[:, :, :]), ACT.Square).then_inc(s["sqf"], 1)
                root(t, stf, "varf", "sdf")

            def f8(t):
                done(act, "x1T_ps", t)
                A(flat(x1T[:, :, :]), PA[:, 0:C], ACT.Copy).then_inc(s["x1Ts"], 1)
                done(act, "h1_ps", t)
                A(flat(h1[:, :, :]), PA[:, C:2 * C], ACT.Copy).then_inc(s["h1s"], 1)

            def f9(t):
                done(act, "z1_ps", t)
                A(sqf[:, :], PB2[:, 0:C], ACT.Square).then_inc(s["sq1"], 1)
                root(t, stf, "var1", "sd1")

            def f10a(t):
                done(act, "x2", t)
                if t.fast:
                    done(act, "slot_ps", t, K0B)
                A(flat(hml[:, 0, :, :]), flat(x2[t.u][:, :, :]), ACT.Copy).then_inc(s["xh"], 1)
                done(act, "xrest1", t)
                A(flat(hml[:, 1, :, :]), flat(rest[:, 0, :, :]), ACT.Copy).then_inc(s["xm"], 1)

            def f10(t):
                f10a(t)
                for b in range(K2B):
                    n = min(2, K2 - 2 * b)
                    done(act, "slot2_ps", t, K2B, b + 1)
                    A(flat(slot2[t.u][:, 2 * b:2 * b + n, :]), GATHER[b % 2][:, 0:n * C],
                      ACT.Copy).then_inc(s["slot2"], 1)

            def b1(t):
                done(act, "o2T_ps", t)
                A(flat(x2T[:, :, :]), PX[:, C:2 * C], ACT.Copy)
                A(flat(o2T[:, :, :]), PX[:, 0:C], ACT.Copy).then_inc(s["o2Ts"], 1)

            def b2(t):
                done(act, "hT_ps", t)
                A(flat(hT[:, :, :]), PX2[:, :], ACT.Relu, bias=b1t[:, 0:1]).then_inc(s["hTs"], 1)

            def b3(t):
                done(act, "y2sum", t)
                A(sqb[:, :], flat(zb[:, :, :]), ACT.Square).then_inc(s["sq2"], 1)
                root(t, stb, "var2", "sd2")

            def b4(t):
                done(act, "x3T_ps", t)
                A(flat(x3T[:, :, :]), PX[:, 0:C], ACT.Copy).then_inc(s["x3Ts"], 1)

            def b5(t):
                done(act, "x3c_ps", t)
                A(flat(x3c[:, :, :]), PX2[:, 0:C], ACT.Copy).then_inc(s["x3cs"], 1)

            def b6(t):
                done(act, "z3sum", t)
                A(sqb[:, :], flat(zb[:, :, :]), ACT.Square).then_inc(s["sq3"], 1)
                root(t, stb, "var3", "sd3")

            return dict(f1=f1, f2=f2, f3=f3, f4=f4, f5=f5, f6=f6, f7=f7, f8=f8, f9=f9, f10=f10, f10a=f10a,
                        b1=b1, b2=b2, b3=b3, b4=b4, b5=b5, b6=b6)

        def scalar_fast(act):
            part = scalar_steps(act)
            act.wait_ge(logs_in, 1)
            nc.scalar.activation(rtmp[:, 1, :], rtmp[:, 0, :], ACT.Ln).then_inc(logs, 1)
            act.wait_ge(made_dve, 1)
            all_slots(act, part, lambda t, back, front: one_slot(part, t, back, front))

        def gpsimd_steps(pool):
            P = nc.gpsimd
            count = [0]

            def own(ins):
                count[0] += 1
                ins.then_inc(s["chain_pool"], 1)
                pool.wait_ge(s["chain_pool"], count[0])

            def ready(name, t):
                done(pool, name, t)
                pool.sem_inc(s["seen_pool"], 1)

            def per_row(ap, n):
                return ap.unsqueeze(2).broadcast_to([128, G, n])

            def constants():
                own(P.memset(w1t[:, :, :], 0.0))
                P.memset(bd[:, :, :, :], 0.0).then_inc(made_pool, 1)
                own(P.memset(ident[:, :], 0.0))
                own(P.affine_select(out=ident[:, :], in_=ident[:, :], compare_op=ALU.not_equal, fill=1.0,
                                    base=0, pattern=[[-1, 128]], channel_multiplier=1))
                P.tensor_copy(identb[:, :], ident[:, :])
                own(P.memset(onesf[:, :], 1.0))
                P.memset(onesb[:, :], 1.0)
                P.affine_select(out=upto[:, :], in_=onesf[:, :], compare_op=ALU.is_ge, fill=0.0,
                                base=0, pattern=[[1, 128]], channel_multiplier=-1)
                own(P.memset(column[:, :, :], 0.0))
                for g in range(G):
                    P.memset(column[:, g, g::G], 1.0)
                own(P.memset(partsum[:, :], 0.0))
                for j in range(NPART):
                    own(P.memset(partsum[:, j:j + 1], BIG_PARTS[j]))
                    own(P.affine_select(out=partsum[:, j:j + 1], in_=partsum[:, j:j + 1], compare_op=ALU.is_ge,
                                        fill=0.0, base=-G * j, pattern=[[0, 1]], channel_multiplier=1))
                    own(P.affine_select(out=partsum[:, j:j + 1], in_=partsum[:, j:j + 1], compare_op=ALU.is_ge,
                                        fill=0.0, base=G * (j + 1) - 1, pattern=[[0, 1]], channel_multiplier=-1))
                own(P.tensor_tensor(parts[:, 0:1], partsum[:, 0:1], partsum[:, 1:2], ALU.add))
                own(P.tensor_tensor(parts[:, 0:1], parts[:, 0:1], partsum[:, 2:3], ALU.add))
                own(P.tensor_scalar(parts[:, 1:2], parts[:, 0:1], -2.0, None, ALU.mult))
                own(P.memset(fill[:, :, :, :], 0.0))
                for g in range(G):
                    for j in range(NPART):
                        own(P.affine_select(out=fill[:, :, g, :], in_=fill[:, :, g, :], compare_op=ALU.not_equal,
                                            fill=1.0, base=-(G * j + g), pattern=[[0, 2], [0, D]], channel_multiplier=1))
                for k in range(2):
                    own(P.tensor_scalar(fill[:, k, :, :], fill[:, k, :, :], parts[:, k:k + 1], None, ALU.mult))
                P.memset(sqrt_eps[:, 0:1], PNA_EPS)
                P.memset(sqrt_eps[:, 1:2], LN_EPS)
                for r in range(K2):
                    P.memset(rank_of[:, :, PLACE[r], :], float(r))
                for k in range(3):
                    P.memset(tau_w[:, k, :, :], QUANTILE_WEIGHTS[k])
                own(P.memset(most[:, :], 0.0))
                P.sem_inc(made_pool, MADE_POOL - 1)

            def f1(t):
                ready("nbN0", t)
                P.affine_select(out=nbN[:, :, :], in_=nbN[:, :, :], compare_op=ALU.not_equal, fill=0.0,
                                base=0, pattern=[[0, G], [-1, N]], channel_multiplier=1).then_inc(s["nbN"], 1)
                if not t.fast:
                    ready("nbN", t)
                    P.affine_select(out=selfN[:, :, :], in_=nbN[:, :, :], compare_op=ALU.not_equal, fill=1.0,
                                    base=0, pattern=[[0, G], [-1, N]], channel_multiplier=1).then_inc(s["selfN"], 1)
                ready("maskT", t)
                P.affine_select(out=nbT[:, :, :], in_=maskT[:, :, :], compare_op=ALU.not_equal, fill=0.0,
                                base=0, pattern=[[0, G], [-1, N]], channel_multiplier=1).then_inc(s["nbT"], 1)
                P.affine_select(out=selfT[:, :, :], in_=maskT[:, :, :], compare_op=ALU.not_equal, fill=1.0,
                                base=0, pattern=[[0, G], [-1, N]], channel_multiplier=1).then_inc(s["selfT"], 1)
                ready("cnts", t)
                own(P.tensor_scalar(skp[:, 0, :], cnt[:, 0, :], 0.5, 0.25, ALU.mult, ALU.add))
                own(P.tensor_scalar(skp[:, 1, :], skp[:, 0, :], ROUND, None, ALU.add))
                own(P.tensor_scalar(skp[:, 0, :], skp[:, 1, :], -ROUND, None, ALU.add))
                own(P.tensor_scalar(skp[:, 1, :], cnt[:, 0, :], DILATE_ABOVE, None, ALU.is_gt))
                ready("rowc", t)
                own(P.tensor_tensor(skp[:, 2, :], skp[:, 1, :], rowc[t.u][:, MASK, :], ALU.mult))
                own(P.tensor_tensor(skp[:, 3, :], skp[:, 0, :], skp[:, 2, :], ALU.mult))
                own(P.tensor_tensor(skp[:, 4, :], skp[:, 3, :], skp[:, 2, :], ALU.add))
                own(P.tensor_scalar(skp[:, 4, :], skp[:, 4, :], -1.0, None, ALU.add))
                own(P.tensor_tensor(skp[:, 5, :], skp[:, 4, :], skp[:, 3, :], ALU.add))
                ready("keyN", t)
                own(P.tensor_tensor(drop[:, :, :], keyN[:, :, :], per_row(skp[:, 4, :], N), ALU.subtract))
                own(P.tensor_tensor(drop2[:, :, :], keyN[:, :, :], per_row(skp[:, 5, :], N), ALU.subtract))
                own(P.tensor_tensor(drop[:, :, :], drop[:, :, :], drop2[:, :, :], ALU.mult))
                P.tensor_scalar(drop[:, :, :], drop[:, :, :], 0.0, None, ALU.is_equal).then_inc(s["drop"], 1)

            def f2(t):
                ready("qh", t)
                P.tensor_tensor(rest[:, 0, :, :], QQ[:, :, 0, :], hml[:, 0, :, :], ALU.subtract).then_inc(s["rest1"], 1)
                ready("qm", t)
                P.tensor_tensor(hml[:, 2, :, :], rest[:, 0, :, :], hml[:, 1, :, :],
                                ALU.subtract).then_inc(s["parts1"], 1)
                for k in range(K0):
                    last = P.tensor_scalar(empty1[:, k, :], cntT1[:, :], k + 1.0, None, ALU.is_lt)
                last.then_inc(s["empty1"], 1)

            def f3(t):
                ready("rpS", t)
                P.tensor_tensor(wpt[:, 0, :, :], pS[:, :, :], rp[:, :, :], ALU.subtract)
                ready("mean", t)
                own(P.tensor_tensor(wpt[:, 1, :, :], m4[:, :, 0, :], ac[:, :, 0, :], ALU.add))
                P.tensor_tensor(wpt[:, 1, :, :], wpt[:, 1, :, :], wpt[:, 0, :, :], ALU.mult).then_inc(s["stt"], 1)

            def f4(t):
                ready("cnt2s", t)
                for k in range(K2):
                    last = P.tensor_scalar(empty2[:, k, :], cntT2[:, :], k + 1.0, None, ALU.is_lt)
                last.then_inc(s["empty2"], 1)
                before(pool, "o2", t, 2)
                pool.sem_inc(s["seen_pool"], 1)
                for k in range(3):
                    own(P.tensor_scalar(post[:, k, :], cnt[:, 2, :], -1.0, TAUS[k], ALU.add, ALU.mult))
                own(P.tensor_tensor(hatd[:, :, :, :], rank_of[:, :, :, :],
                                    post[:, :, :].unsqueeze(2).broadcast_to([128, 3, K2, G]), ALU.subtract))
                own(P.tensor_scalar(hatn[:, :, :, :], hatd[:, :, :, :], 0.0, 2.0, ALU.max, ALU.mult))
                own(P.tensor_tensor(hatd[:, :, :, :], hatn[:, :, :, :], hatd[:, :, :, :], ALU.subtract))
                own(P.tensor_scalar(hatd[:, :, :, :], hatd[:, :, :, :], -1.0, 1.0, ALU.mult, ALU.add))
                own(P.tensor_scalar(hatd[:, :, :, :], hatd[:, :, :, :], 0.0, None, ALU.max))
                own(P.tensor_tensor(hatd[:, :, :, :], hatd[:, :, :, :], tau_w[:, :, :, :], ALU.mult))
                own(P.tensor_tensor(hatn[:, 0, :, :], hatd[:, 0, :, :], hatd[:, 1, :, :], ALU.add))
                P.tensor_tensor(rankw[t.u][:, :, :], hatn[:, 0, :, :], hatd[:, 2, :, :],
                                ALU.add).then_inc(s["rankw"], 1)

            def f10(t):
                ready("xh", t)
                P.tensor_tensor(rest[:, 0, :, :], x2[t.u][:, :, :], hml[:, 0, :, :],
                                ALU.subtract).then_inc(s["xrest1"], 1)
                ready("xm", t)
                P.tensor_tensor(hml[:, 2, :, :], rest[:, 0, :, :], hml[:, 1, :, :],
                                ALU.subtract).then_inc(s["parts2"], 1)

            def restart():
                pool.sem_clear(s["chain_pool"])
                count[0] = 0

            return dict(constants=constants, restart=restart, f1=f1, f2=f2, f3=f3, f4=f4, f10=f10)

        def gpsimd_fast(pool):
            part = gpsimd_steps(pool)
            part["constants"]()

            def slot(t, back, front):
                part["restart"]()
                one_slot(part, t, back, front)
            all_slots(pool, part, slot)

        def vector_steps(dve):
            V = nc.vector
            count = [0]

            def own(ins):
                count[0] += 1
                ins.then_inc(s["chain_dve"], 1)
                dve.wait_ge(s["chain_dve"], count[0])

            def per_row(ap, n=D):
                return ap.unsqueeze(2).broadcast_to([128, ap.shape[1], n])

            def flat(ap):
                return ap.rearrange("p g d -> p (g d)")

            def prepare():
                for k in range(4):
                    dve.wait_ge(deg_in[k], 16)
                    own(V.tensor_reduce(deg[:, k * 16:(k + 1) * 16], adj_all[:, k * 16:(k + 1) * 16, :], AX.X, ALU.add))
                V.tensor_scalar(rtmp[:, 0, :], deg[:, :], 1.0, None, ALU.add).then_inc(logs_in, 1)
                dve.wait_ge(logs_in, 1)
                own(V.reciprocal(rows[:, RDEN, :], rtmp[:, 0, :]))
                own(V.tensor_scalar(rows[:, RDEN, :], rows[:, RDEN, :], FLT_MAX, None, ALU.min))
                own(V.tensor_scalar(rows[:, RATIO, :], deg[:, :], 1.0, None, ALU.max))
                own(V.reciprocal(rows[:, INV, :], rows[:, RATIO, :]))
                own(V.tensor_tensor(rows[:, RATIO, :], deg[:, :], rows[:, INV, :], ALU.mult))
                dve.wait_ge(w_in, 16 * WEIGHT_LOADS)
                own(V.tensor_copy(rows[:, MASK, :], mask8[:, :]))
                dve.wait_ge(logs, 1)
                own(V.tensor_scalar(rows[:, AMP, :], rtmp[:, 1, :], 1.0 / AVG_D_LOG, None, ALU.mult))
                own(V.tensor_scalar(rtmp[:, 0, :], rtmp[:, 1, :], PNA_EPS, None, ALU.max))
                own(V.reciprocal(rtmp[:, 1, :], rtmp[:, 0, :]))
                own(V.tensor_scalar(rows[:, ATT, :], rtmp[:, 1, :], AVG_D_LOG, None, ALU.mult))

                dve.wait_ge(made_pool, MADE_POOL)
                own(V.tensor_copy(raw[0:64, 2, :], ident[0:64, 0:64]))
                own(V.tensor_copy(raw[64:128, 2, :], ident[64:128, 64:128]))
                own(V.tensor_tensor(raw[:, 0, :], raw[:, 0, :], raw[:, 2, :], ALU.add))
                own(V.tensor_reduce(rawmean[:, :], raw[:, :, :], AX.X, ALU.add))
                own(V.tensor_scalar(rawmean[:, :], rawmean[:, :], 1.0 / D, None, ALU.mult))
                own(V.tensor_tensor(raw[:, :, :], raw[:, :, :], per_row(rawmean[:, :]), ALU.subtract))
                for block_of, k in ((0, 2), (1, 3), (2, 4)):
                    V.tensor_copy(bd[0:64, k, 0, :], raw[0:64, block_of, :])
                    V.tensor_copy(bd[64:128, k, 1, :], raw[64:128, block_of, :])
                own(V.tensor_copy(wpost[:, :, :, :].rearrange("p k f d -> p (k f) d"), raw[:, 3:9, :]))
                own(V.tensor_reduce(biasm[0:1, :], biasr[0:1, :, :], AX.X, ALU.add))
                own(V.tensor_scalar(biasm[0:1, :], biasm[0:1, :], 1.0 / D, None, ALU.mult))
                own(V.memset(biasm[0:1, 0:1], 0.0))
                own(V.tensor_tensor(biasr[0:1, :, :], biasr[0:1, :, :],
                                    biasm[0:1, :].unsqueeze(2).broadcast_to([1, 4, D]), ALU.subtract))
                own(V.tensor_copy(biast[0:1, :, :, :], biasr[0:1, :, :].unsqueeze(2).broadcast_to([1, 4, G, D])))
                dve.sem_inc(made_dve, 1)

            def hots(t, lo, hi):
                for k in range(lo, hi):
                    j = k - RING
                    if j < 0:
                        before(dve, "slot2_ps", t, 1, K2B, (j + HOTS - K0) // 2 + 1)
                    elif j < K0:
                        done(dve, "slot_ps", t, K0B, j // 2 + 1)
                    else:
                        done(dve, "slot2_ps", t, K2B, (j - K0) // 2 + 1)
                    key, slot = (key1, k) if k < K0 else (key2, k - K0)
                    V.tensor_scalar(hot[:, k % RING, :, :], key[:, :, :], slot + 1.0, None,
                                    ALU.is_equal).then_inc(s["hot"], 1)

            def f1(t):
                dve.wait_ge(adj_in[t.u], t.half * 16 + 16)
                V.tensor_scalar(maskT[:, :, :], adjT[t.u][:, :, :], 0.0, None, ALU.is_gt).then_inc(s["maskT"], 1)
                V.tensor_scalar(nbN[:, :, :], adj_all[:, bass.ds(t.g * G, G), :], 0.0, None,
                                ALU.is_gt).then_inc(s["nbN0"], 1)
                V.tensor_copy(rowc[t.u][:, :, :], rows[:, :, bass.ds(t.g * G, G)]).then_inc(s["rowc"], 1)

            def f1b(t):
                done(dve, "pos1_ps", t)
                done(dve, "maskT", t)
                V.tensor_tensor(flat(key1[:, :, :]), PB[:, :], flat(maskT[:, :, :]), ALU.mult).then_inc(s["key1"], 1)
                if t.fast:
                    done(dve, "key1", t)
                    hots(t, 0, RING)
                done(dve, "posN_ps", t)
                done(dve, "nbN", t)
                V.tensor_tensor(flat(keyN[:, :, :]), PB[:, :], flat(nbN[:, :, :]), ALU.mult).then_inc(s["keyN"], 1)

            def f3(t):
                done(dve, "acs", t)
                done(dve, "rpS", t)
                V.tensor_tensor(m4[:, :, 0, :], rp[:, :, :], ac[:, :, 0, :], ALU.add).then_inc(s["mean"], 1)
                done(dve, "asq", t)
                own(V.tensor_tensor(vr[:, :, :], ac[:, :, 1, :], asq[:, :, :], ALU.subtract))

            def f3b(t):
                done(dve, "rem_ps", t)
                if not t.fast:
                    dve.wait_ge(s["selfN"], t.g + 1)
                    own(V.scalar_tensor_tensor(out=flat(validN[:, :, :]), in0=PB[:, :], scalar=0.0,
                                               in1=flat(selfN[:, :, :]), op0=ALU.is_equal, op1=ALU.mult))
                done(dve, "selfT", t)
                V.scalar_tensor_tensor(out=flat(validT[:, :, :]), in0=PB[:, :], scalar=0.0,
                                       in1=flat(selfT[:, :, :]), op0=ALU.is_equal,
                                       op1=ALU.mult).then_inc(s["validT"], 1)
                done(dve, "stt", t)
                own(V.tensor_tensor(vr[:, :, :], vr[:, :, :], wpt[:, 1, :, :], ALU.add))
                V.tensor_scalar(vr[:, :, :], vr[:, :, :], 0.0, None, ALU.max).then_inc(s["vsum"], 1)

            def f4(t):
                done(dve, "pos2_ps", t)
                done(dve, "validT", t)
                V.tensor_tensor(flat(key2[:, :, :]), PB[:, :], flat(validT[:, :, :]), ALU.mult).then_inc(s["key2"], 1)
                done(dve, "key2", t)
                done(dve, "cnt2s", t)
                own(V.tensor_reduce(mostn[:, :], cnt[:, 1:3, :], AX.X, ALU.max))
                own(V.tensor_tensor(most[:, :], most[:, :], mostn[:, :], ALU.max))

            def f5(t):
                hots(t, RING, K0)

            def tree(buf, op, name, t):
                done(dve, name, t, K0B)
                own(V.tensor_tensor(buf[:, 0:6, :], buf[:, 0:6, :], buf[:, 6:12, :], op))
                own(V.tensor_tensor(buf[:, 0:3, :], buf[:, 0:3, :], buf[:, 3:6, :], op))
                own(V.tensor_tensor(buf[:, 0:2, :], buf[:, 0:2, :], buf[:, 2:13:10, :], op))
                own(V.tensor_tensor(buf[:, 0, :], buf[:, 0, :], buf[:, 1, :], op))

            def f6(t):
                tree(slotP, ALU.min, "slotP", t)
                done(dve, "ps", t)
                V.tensor_tensor(m4[:, :, 2, :], slotP[:, 0, :].rearrange("p (g d) -> p g d", g=G), pS[:, :, :], ALU.add)
                tree(slotM, ALU.max, "slotM", t)
                V.tensor_tensor(m4[:, :, 1, :], slotM[:, 0, :].rearrange("p (g d) -> p g d", g=G), pS[:, :, :],
                                ALU.add).then_inc(s["extremes"], 1)
                hots(t, K0, K0 + RING)

            def norm(t, z, sq, st, squared, var, root, dst, signal):
                done(dve, squared, t)
                V.tensor_reduce(st[:, 0, :], sq[:, :].rearrange("p (g d) -> p g d", g=G), AX.X,
                                ALU.add).then_inc(s[var], 1)
                done(dve, root, t)
                own(V.reciprocal(st[:, 2, :], st[:, 1, :]))
                V.tensor_tensor(dst, z, per_row(st[:, 2, :]), ALU.mult).then_inc(s[signal], 1)

            def f7(t):
                done(dve, "yss", t)
                own(V.tensor_tensor(zf[:, :, :], ys[:, 0, :, :], ys[:, 1, :, :], ALU.add))
                for p in range(G // 2):
                    y = (PB, PB2)[p][:, 0:6 * D].rearrange("p (a f d) -> p a f d", a=2, f=3)[:, :, 0, :]
                    last = V.tensor_tensor(zf[:, 2 * p:2 * p + 2, :], y, zf[:, 2 * p:2 * p + 2, :], ALU.add)
                last.then_inc(s["ysum"], 1)
                norm(t, zf[:, :, :], sqf, stf, "sqf", "varf", "sdf", x1[:, :, :], "x1")

            def f9(t):
                norm(t, PB2[:, 0:C].rearrange("p (g d) -> p g d", g=G), sqf, stf, "sq1", "var1", "sd1",
                     x2[t.u][:, :, :], "x2")

            def f10(t):
                hots(t, K0 + RING, HOTS)

            def b3(t):
                own(V.tensor_copy(rowb[:, :, :], rows[:, RDEN:MASK + 1, bass.ds(t.g * G, G)]))
                done(dve, "y2_ps", t)
                own(V.tensor_tensor(yb[:, :, :], PX[:, 0:C].rearrange("p (g d) -> p g d", g=G),
                                    per_row(rowb[:, MASK - RDEN, :]), ALU.mult))
                V.tensor_tensor(flat(zb[:, :, :]), PX[:, C:2 * C], flat(yb[:, :, :]), ALU.add).then_inc(s["y2sum"], 1)
                norm(t, zb[:, :, :], sqb, stb, "sq2", "var2", "sd2", x3[:, :, :], "x3")

            def b6(t):
                done(dve, "z3_ps", t)
                done(dve, "x3cs", t)
                own(V.tensor_tensor(flat(yb[:, :, :]), PX[:, 0:C], flat(x3c[:, :, :]), ALU.add))
                own(V.tensor_tensor(yb[:, :, :], yb[:, :, :], per_row(rowb[:, 0, :]), ALU.mult))
                V.tensor_tensor(zb[:, :, :], yb[:, :, :], x3c[:, :, :], ALU.add).then_inc(s["z3sum"], 1)
                if t.least >= 2:
                    dve.wait_ge(stored[t.u], t.half * 16)
                norm(t, zb[:, :, :], sqb, stb, "sq3", "var3", "sd3", xo[t.u][:, :, :], "xo")

            def sort_layer(t, k):
                if k == 0:
                    done(dve, "slot2", t, K2B)
                buffers = (slot2[t.u], swap)
                for is_min, in0, in1, dst in plan[k]:
                    last = V.tensor_tensor(slots(buffers, dst), slots(buffers, in0), slots(buffers, in1),
                                           ALU.min if is_min else ALU.max)
                own(last)

            def quantiles(t):
                buffers = (slot2[t.u], swap)
                done(dve, "rankw", t)
                at = 0
                for run in ends:
                    _, first, stride, n = run
                    w = rankw[t.u][:, first:first + stride * (n - 1) + 1:stride, :]
                    for k in range(n):
                        src = buffers[run[0]][:, first + k * stride, :].rearrange("p (g d) -> p g d", g=G)
                        last = V.tensor_tensor(prod[:, at, :].rearrange("p (g d) -> p g d", g=G), src,
                                               per_row(rankw[t.u][:, first + k * stride, :]), ALU.mult)
                        at += 1
                own(last)
                assert at == RANKS == 9
                own(V.tensor_tensor(prod[:, 0:4, :], prod[:, 0:4, :], prod[:, 4:8, :], ALU.add))
                own(V.tensor_tensor(prod[:, 0:2, :], prod[:, 0:2, :], prod[:, 2:4, :], ALU.add))
                own(V.tensor_tensor(prod[:, 0, :], prod[:, 0, :], prod[:, 1, :], ALU.add))
                own(V.tensor_tensor(prod[:, 0, :], prod[:, 0, :], prod[:, 8, :], ALU.add))
                V.tensor_tensor(flat(o2[:, :, :]), prod[:, 0, :], flat(x2[t.u][:, :, :]), ALU.add).then_inc(s["o2"], 1)

            def restart():
                dve.sem_clear(s["chain_dve"])
                count[0] = 0

            def node(ap, m):
                return ap[:, :, bass.ds(m, 1)].broadcast_to([128, G, D])

            def pick_node(m):
                V.tensor_copy(pick, identb[:, bass.ds(m, 1)].broadcast_to([128, 128])).then_inc(s["pick"], 1)

            def general0(t):
                own(V.tensor_scalar(off[:, :, :], adj_all[:, bass.ds(t.g * G, G), :], 0.0, NEG_BIG,
                                    ALU.is_gt, ALU.mult))
                own(V.tensor_scalar(off[:, :, :], off[:, :, :], -NEG_BIG, None, ALU.add))
                own(V.memset(gmax[:, :, :], -FLT_MAX))
                own(V.memset(gmin[:, :, :], FLT_MAX))
                row = RG0[:, 0:C].rearrange("p (g d) -> p g d", g=G)
                with dve.Fori(0, N) as m:
                    restart()
                    pick_node(m)
                    dve.wait_ge(s["row_ps"], t.g * (2 * N) + m + 1)
                    own(V.tensor_tensor(gtmp[:, 0, :, :], row, node(off, m), ALU.add))
                    own(V.tensor_tensor(gmax[:, :, :], gmax[:, :, :], gtmp[:, 0, :, :], ALU.max))
                    own(V.tensor_tensor(gtmp[:, 0, :, :], row, node(off, m), ALU.subtract))
                    own(V.tensor_tensor(gmin[:, :, :], gmin[:, :, :], gtmp[:, 0, :, :], ALU.min))
                done(dve, "ps", t)
                own(V.tensor_tensor(m4[:, :, 2, :], gmin[:, :, :], pS[:, :, :], ALU.add))
                V.tensor_tensor(m4[:, :, 1, :], gmax[:, :, :], pS[:, :, :], ALU.add).then_inc(s["extremes"], 1)

            def general2(t):
                own(V.tensor_tensor(earlier, upto[:, :], identb[:, :], ALU.subtract))
                own(V.memset(gmax[:, :, :], 0.0))
                done(dve, "rankw", t)
                row = RG0[:, 0:C].rearrange("p (g d) -> p g d", g=G)
                rank = RG1[:, 0:C].rearrange("p (g d) -> p g d", g=G)
                with dve.Fori(0, N) as m:
                    restart()
                    pick_node(m)
                    dve.wait_ge(s["row_ps"], t.g * (2 * N) + m + N + 1)
                    own(V.tensor_tensor(gtmp[:, 0, :, :], x2[t.u][:, :, :], row, ALU.is_lt))
                    own(V.tensor_tensor(gtmp[:, 1, :, :], x2[t.u][:, :, :], row, ALU.is_le))
                    own(V.tensor_tensor(gtmp[:, 1, :, :], gtmp[:, 1, :, :], gtmp[:, 0, :, :], ALU.subtract))
                    own(V.tensor_tensor(gtmp[:, 1, :, :], gtmp[:, 1, :, :],
                                        slotP[:, 6, bass.ds(m, 1)].unsqueeze(1).broadcast_to([128, G, D]), ALU.mult))
                    V.tensor_tensor(below[:, :, :], gtmp[:, 1, :, :], gtmp[:, 0, :, :],
                                    ALU.add).then_inc(s["below"], 1)
                    dve.wait_ge(s["below_ps"], t.g * N + m + 1)
                    for k in range(3):
                        own(V.tensor_tensor(gtmp[:, 0, :, :], rank, per_row(post[:, k, :]), ALU.subtract))
                        own(V.tensor_scalar(gtmp[:, 1, :, :], gtmp[:, 0, :, :], -1.0, None, ALU.mult))
                        own(V.tensor_tensor(gtmp[:, 0, :, :], gtmp[:, 0, :, :], gtmp[:, 1, :, :], ALU.max))
                        own(V.tensor_scalar(gtmp[:, 0, :, :], gtmp[:, 0, :, :], -1.0, 1.0, ALU.mult, ALU.add))
                        own(V.tensor_scalar(gtmp[:, 0, :, :], gtmp[:, 0, :, :], 0.0, QUANTILE_WEIGHTS[k],
                                            ALU.max, ALU.mult))
                        if k == 0:
                            own(V.tensor_copy(gmin[:, :, :], gtmp[:, 0, :, :]))
                        else:
                            own(V.tensor_tensor(gmin[:, :, :], gmin[:, :, :], gtmp[:, 0, :, :], ALU.add))
                    own(V.tensor_tensor(gmin[:, :, :], gmin[:, :, :], node(validN, m), ALU.mult))
                    own(V.tensor_tensor(gmin[:, :, :], gmin[:, :, :], row, ALU.mult))
                    own(V.tensor_tensor(gmax[:, :, :], gmax[:, :, :], gmin[:, :, :], ALU.add))
                V.tensor_tensor(o2[:, :, :], gmax[:, :, :], x2[t.u][:, :, :], ALU.add).then_inc(s["o2"], 1)

            def check_counts():
                own(V.tensor_scalar(excess[:, 0:1], most[:, 0:1], float(K0), None, ALU.is_gt))
                own(V.tensor_scalar(excess[:, 1:2], most[:, 1:2], float(K2), None, ALU.is_gt))
                V.tensor_tensor(excess[:, 2:3], excess[:, 0:1], excess[:, 1:2], ALU.max).then_inc(over_a, 1)
                dve.wait_ge(over_b, 1)
                own(V.tensor_reduce(over[0:1, :], PX[0:1, 0:128], AX.X, ALU.max))
                V.tensor_copy(overi[0:1, :], over[0:1, :]).then_inc(over_c, 1)

            return dict(prepare=prepare, restart=restart, sort_layer=sort_layer, quantiles=quantiles,
                        f1=f1, f1b=f1b, f3=f3, f3b=f3b, f4=f4, f5=f5, f6=f6, f7=f7, f9=f9, f10=f10,
                        b3=b3, b6=b6, general0=general0, general2=general2, check_counts=check_counts)

        def vector_fast(dve):
            part = vector_steps(dve)
            sort_layer, quantiles = part["sort_layer"], part["quantiles"]

            def slot(t, back, front):
                part["restart"]()

                def go(step):
                    group = back if step[0] == "b" else front
                    if group is not None:
                        part[step](group)
                go("f1")
                sort_layer(t, 0)
                go("f1b")
                sort_layer(t, 1)
                go("f3")
                go("b3")
                sort_layer(t, 2)
                go("f3b")
                go("f4")
                sort_layer(t, 3)
                go("b6")
                sort_layer(t, 4)
                go("f5")
                sort_layer(t, 5)
                go("f6")
                sort_layer(t, 6)
                go("f7")
                sort_layer(t, 7)
                go("f9")
                quantiles(t)
                go("f10")

            part["prepare"]()
            for step in ("f1", "f1b", "f3", "f3b", "f4", "f5", "f6", "f7", "f9", "f10"):
                part[step](Turn(None, 0))
            slot(Turn(None, 0), None, Turn(None, 1))
            with dve.Fori(0, NG // 2 - 1) as i:
                slot(Turn(i, 1), Turn(i, 0), Turn(i, 2))
                slot(Turn(i, 2), Turn(i, 1), Turn(i, 3))
            slot(Turn(None, NG - 1), Turn(None, NG - 2), None)
            part["b3"](Turn(None, NG - 1))
            part["b6"](Turn(None, NG - 1))
            part["check_counts"]()

        with nc.Block() as block:
            block.sync(sync_fast)
            block.tensor(tensor_fast)
            block.scalar(scalar_fast)
            block.gpsimd(gpsimd_fast)
            block.vector(vector_fast)

        GENERAL = {
            "sync": (),
            "tensor": ("f1", "f2", "f3", "f4", "general0", "f6", "f7", "f8", "f9", "general2",
                       "b1", "b2", "b3", "b4", "b5", "b6"),
            "scalar": ("f1", "f2", "f3", "f4", "f6", "f7", "f8", "f9", "f10a", "b1", "b2", "b3", "b4", "b5", "b6"),
            "gpsimd": ("f1", "f2", "f3", "f4", "f10"),
            "vector": ("f1", "f1b", "f3", "f3b", "f4", "general0", "f7", "f9", "general2", "b3", "b6"),
        }

        def general(eng, part, order):
            with eng.Fori(0, NG // 2) as i:
                for u in range(2):
                    if "restart" in part:
                        part["restart"]()
                    for step in order:
                        part[step](Turn(i, u, NG))

        any_over = nc.values_load(overi[0:1, 0:1], min_val=0, max_val=1)
        with nc.If(any_over > 0):
            with nc.Block() as block:
                @block.sync
                def _(sp):
                    with sp.Fori(0, NG // 2) as i:
                        for u in range(2):
                            load_group(sp, Turn(i, u, NG))
                            load_back(sp, Turn(i, u, NG))
                            store_group(sp, Turn(i, u, NG))
                    for u in range(2):
                        sp.wait_ge(stored[u], 16 * NG)

                @block.tensor
                def _(pe):
                    general(pe, tensor_steps(pe), GENERAL["tensor"])

                @block.scalar
                def _(act):
                    general(act, scalar_steps(act), GENERAL["scalar"])

                @block.gpsimd
                def _(pool):
                    general(pool, gpsimd_steps(pool), GENERAL["gpsimd"])

                @block.vector
                def _(dve):
                    general(dve, vector_steps(dve), GENERAL["vector"])


def kernel(**inputs):
    import concourse.bacc as bacc
    from concourse.bass_utils import run_bass_kernel_spmd

    a = {k: np.asarray(v) for k, v in inputs.items()}
    x, adj = a["x"], a["adj"]
    laid = {
        "x_pairs": x.reshape(B // 2, 2, N, D).transpose(1, 3, 0, 2).reshape(2 * D, B // 2, N),
        "adj_rows": adj.transpose(1, 0, 2),
        "adj_cols": adj.transpose(2, 0, 1),
        "node_mask": a["nodemask"].view(np.uint8).T,
        "w_pre": a["L0_gnn_W_pre"], "b_pre": a["L0_gnn_b_pre"],
        "w_post": a["L0_gnn_W_post"], "b_post": a["L0_gnn_b_post"],
        "w_l1": a["L1_gnn_weight"], "b_l1": a["L1_gnn_bias"],
        "w1": a["L2_gnn_W1"], "b1": a["L2_gnn_b1"], "w2": a["L2_gnn_W2"], "b2": a["L2_gnn_b2"],
    }
    nc = bacc.Bacc("TRN2", target_bir_lowering=False, num_devices=1)
    arrays, args = {}, []
    for name, v in laid.items():
        v = np.ascontiguousarray(v)
        arrays[f"{name}_dram"] = v
        args.append(nc.dram_tensor(f"{name}_dram", v.shape, mybir.dt.from_np(v.dtype), kind="ExternalInput").ap())
    args.append(nc.dram_tensor("out_dram", (N, B, D), F32, kind="ExternalOutput").ap())
    adj_kernel(nc, *args)
    got = run_bass_kernel_spmd(nc, [arrays], core_ids=[0]).results[0]["out_dram"]
    return np.ascontiguousarray(np.transpose(got, (1, 0, 2)))
```

```python
from contextlib import ExitStack

import numpy as np

import concourse.bass as bass
from concourse import mybir

ALU = mybir.AluOpType
ACT = mybir.ActivationFunctionType
AX = mybir.AxisListType
F32 = mybir.dt.float32
BF16 = mybir.dt.bfloat16
I32 = mybir.dt.int32
U8 = mybir.dt.uint8

B, N, D, H = 64, 128, 64, 128
G = 4
NG = B // G
C = G * D
HC = 64
LN_EPS = 1e-5
PNA_EPS = 1e-5
AVG_D_LOG = 4.86
DILATE_ABOVE = 10.0
TAUS = (0.25, 0.5, 0.75)
QUANTILE_WEIGHTS = (0.25, 0.5, 0.25)
NEG_BIG = 1.0e9
EMPTY = 2.0 ** 30
ROUND = 8388608.0
FLT_MAX = 3.4028234e38
K0 = 13
K2 = 11
K0B = (K0 + 1) // 2
K2B = (K2 + 1) // 2
RING0 = 7
RING2 = 11
KP = K0 * G

NETWORK = (
    ((0, 9), (1, 6), (2, 4), (3, 7), (5, 8)),
    ((0, 1), (3, 5), (4, 10), (6, 9), (7, 8)),
    ((1, 3), (2, 5), (4, 7), (8, 10)),
    ((0, 4), (1, 2), (3, 7), (5, 9), (6, 8)),
    ((0, 1), (2, 6), (4, 5), (7, 8), (9, 10)),
    ((2, 4), (3, 6), (5, 7), (8, 9)),
    ((1, 2), (3, 4), (5, 6), (7, 8)),
    ((2, 3), (4, 5), (6, 7)),
)
PLACE = (10, 9, 8, 6, 2, 7, 3, 0, 1, 4, 5)
assert sorted(PLACE[:9]) == [0, 1, 2, 3, 6, 7, 8, 9, 10]
RANKS = int(np.ceil(max(TAUS) * (K2 - 1))) + 1


def plan_sort():
    live = set(range(RANKS))
    layers = []
    for layer in reversed(NETWORK):
        kept = [(a, b, a in live, b in live) for a, b in layer if a in live or b in live]
        for a, b, _, _ in kept:
            live |= {a, b}
        layers.append(kept)
    layers.reverse()
    side = [0] * K2
    plan = []
    for layer in layers:
        steps = []
        for is_min in (True, False):
            todo = []
            for a, b, low, high in layer:
                if low if is_min else high:
                    x, y = (a, b) if PLACE[a] < PLACE[b] else (b, a)
                    out = a if is_min else b
                    todo.append((PLACE[x], PLACE[y], side[x], side[y], out == x))
            todo.sort()
            while todo:
                first = todo[0]
                best = [first]
                for second in todo[1:]:
                    dx, dy = second[0] - first[0], second[1] - first[1]
                    if dx <= 0 or dy <= 0 or second[2:] != first[2:]:
                        continue
                    run = [first]
                    while (first[0] + len(run) * dx, first[1] + len(run) * dy) + first[2:] in todo:
                        run.append((first[0] + len(run) * dx, first[1] + len(run) * dy) + first[2:])
                    if len(run) > len(best):
                        best = run
                for x in best:
                    todo.remove(x)
                n = len(best)
                dx = best[1][0] - first[0] if n > 1 else 1
                dy = best[1][1] - first[1] if n > 1 else 1
                in0, in1 = (first[2], first[0], dx, n), (first[3], first[1], dy, n)
                src = in0 if first[4] else in1
                steps.append((is_min, in0, in1, (1 - src[0],) + src[1:]))
        for a, b, _, _ in layer:
            side[a] ^= 1
            side[b] ^= 1
        plan.append(steps)
    ends = []
    todo = sorted((PLACE[r], side[r]) for r in range(RANKS))
    while todo:
        p, s = todo[0]
        best = [(p, s)]
        for q, z in todo[1:]:
            run = [(p, s)]
            while z == s and (p + len(run) * (q - p), s) in todo:
                run.append((p + len(run) * (q - p), s))
            if len(run) > len(best):
                best = run
        for x in best:
            todo.remove(x)
        ends.append((s, p, best[1][0] - p if len(best) > 1 else 1, len(best)))
    assert RANKS == 9 == sum(run[3] for run in ends)
    return plan, ends


class Turn:

    def __init__(self, i, offset, past=0):
        self.g = offset if i is None else i * 2 + offset
        self.n = self.g + past
        self.u = offset % 2
        self.half = past // 2 + (offset // 2 if i is None else i + offset // 2)
        self.least = offset + past
        self.fast = past == 0
        self.offset, self.past = offset, past
        self.i = i

    @property
    def next(self):
        if self.i is None and self.g == NG - 1:
            return None
        return Turn(self.i, self.offset + 1, self.past)


def adj_kernel(nc, x_pairs, adj_rows, adj_cols, node_mask, w_pre, b_pre, w_post, b_post,
               w_l1, b_l1, w1, b1, w2, b2, out):
    with ExitStack() as ctx:
        def sb(name, shape, dt=F32):
            return ctx.enter_context(nc.sbuf_tensor(name, shape, dt))

        def sem(name):
            return ctx.enter_context(nc.semaphore(name))

        bank = [ctx.enter_context(nc.psum_tensor(f"bank{k}", [128, 512], F32)) for k in range(8)]
        POS, STAT, MB, MB2, RG0, RG1, PX, PX2 = bank
        GATHER = (RG0, RG1)

        ident = sb("ident", [128, 128])
        identb = sb("identb", [128, 128], BF16)
        upto = sb("upto", [128, 128], BF16)
        onesf = sb("onesf", [128, 128])
        onesb = sb("onesb", [128, 1], BF16)
        column = sb("column", [128, G, KP], BF16)
        fill = sb("fill", [KP, K0, G, D], BF16)
        slot_no = sb("slot_no", [KP, 1])
        sqrt_eps = sb("sqrt_eps", [128, 2])
        raw = sb("raw", [128, 10, D])
        rawmean = sb("rawmean", [128, 10])
        bd = sb("bd", [128, 5, 2, D])
        wpost = sb("wpost", [128, 2, 3, D])
        w1t = sb("w1t", [128, 2, H])
        b1t = sb("b1t", [128, 1])
        biasr = sb("biasr", [1, 4, D])
        biasm = sb("biasm", [1, 4])
        biast = sb("biast", [1, 4, G, D])
        rank_of = sb("rank_of", [128, 3, K2, G])
        tau_w = sb("tau_w", [128, 3, K2, G])
        mask8 = sb("mask8", [128, B], U8)

        adj_all = sb("adj_all", [128, B, N])
        deg = sb("deg", [128, B])
        rows = sb("rows", [128, 6, B])
        rtmp = sb("rtmp", [128, 2, B])
        INV, RATIO, AMP, ATT, RDEN, MASK = range(6)
        mostn = sb("mostn", [128, 2])
        most = sb("most", [128, 2, G])
        over = sb("over", [1, 1])
        overi = sb("overi", [1, 1], I32)

        adjA, adjB, adjC = (sb(f"adj{k}", [128, G, N]) for k in "ABC")
        xT0 = [sb(f"xT0_{u}", [128, G // 2, N]) for u in range(2)]
        rowc = [sb(f"rowc{u}", [128, 6, G]) for u in range(2)]
        rowb = sb("rowb", [128, 2, G])
        maskT = sb("maskT", [128, G, N], BF16)
        nbN = sb("nbN", [128, G, N], BF16)
        nbT = sb("nbT", [128, G, N], BF16)
        selfT = sb("selfT", [128, G, N], BF16)
        keyN = sb("keyN", [128, G, N], BF16)
        drop = sb("drop", [128, G, N], BF16)
        drop2 = sb("drop2", [128, G, N], BF16)
        validT = sb("validT", [128, G, N], BF16)
        key1 = sb("key1", [128, G, N], BF16)
        key2 = [sb(f"key2_{u}", [128, G, N], BF16) for u in range(2)]
        hot0 = sb("hot0", [128, RING0, G, N], BF16)
        hot2 = sb("hot2", [128, RING2, G, N], BF16)
        cnt = sb("cnt", [128, 2, G])
        cnt2 = [sb(f"cnt2_{u}", [128, G]) for u in range(2)]
        cntT1 = sb("cntT1", [KP, N])
        cntT2 = sb("cntT2", [KP, N])
        empty1 = sb("empty1", [KP, 2, N], BF16)
        empty2 = [sb(f"empty2_{u}", [KP, N], BF16) for u in range(2)]
        skp = sb("skp", [128, 6, G])
        QQ = sb("QQ", [128, G, 2, D])
        pS = sb("pS", [128, G, D])
        rp = sb("rp", [128, G, D])
        qparts = sb("qparts", [128, 3, G, D], BF16)
        xparts = sb("xparts", [128, 3, G, D], BF16)
        rest = sb("rest", [128, G, D])
        ac = sb("ac", [128, G, 2, D])
        asq = sb("asq", [128, G, D])
        wpt = sb("wpt", [128, 2, G, D])
        vr = sb("vr", [128, G, D])
        m4 = sb("m4", [128, G, 4, D])
        mT = sb("mT", [128, 2, G, N])
        slotP = sb("slotP", [128, K0, C])
        slotM = sb("slotM", [128, K0, C])
        ys = sb("ys", [128, 2, G, D])
        off = slotP[:, 0:2, :].rearrange("p k c -> p (k c)").rearrange("p (g n) -> p g n", g=G)
        gmax = slotP[:, 2, :].rearrange("p (g d) -> p g d", g=G)
        gmin = slotP[:, 3, :].rearrange("p (g d) -> p g d", g=G)
        gtmp = slotP[:, 4:6, :].rearrange("p k (g d) -> p k g d", g=G)
        earlier = slotP[:, 6, 0:128]
        validN = hot0[:, 0, :, :]
        selfN = hot0[:, 1, :, :]
        below = hot0[:, 2:4, :, :].rearrange("p k g n -> p (k g n)")[:, 0:C].rearrange("p (g d) -> p g d", g=G)
        pick = hot0[:, 4, 0, :]
        excess = sb("excess", [128, 3])
        zf = sb("zf", [128, G, D])
        sqf = sb("sqf", [128, C])
        stf = sb("stf", [128, 3, G])
        x1 = sb("x1", [128, G, D])
        x1T = sb("x1T", [128, G // 2, N])
        h1 = sb("h1", [128, G, D])
        x2 = [sb(f"x2_{u}", [128, G, D]) for u in range(2)]
        slot2 = [sb(f"slot2_{u}", [128, K2, C]) for u in range(2)]
        swap = sb("swap", [128, K2, C])
        hatd = sb("hatd", [128, 3, K2, G])
        hatn = sb("hatn", [128, 3, K2, G])
        post = sb("post", [128, 3, G])
        rankw = [sb(f"rankw{u}", [128, K2, G]) for u in range(2)]
        o2 = sb("o2", [128, G, D])
        o2T = sb("o2T", [128, G // 2, N])
        x2T = sb("x2T", [128, G // 2, N])
        hT = sb("hT", [128, G, N])
        yb = sb("yb", [128, G, D])
        zb = sb("zb", [128, G, D])
        sqb = sb("sqb", [128, C])
        stb = sb("stb", [128, 3, G])
        x3 = sb("x3", [128, G, D])
        x3T = sb("x3T", [128, G // 2, N])
        x3c = sb("x3c", [128, G, D])
        xo = [sb(f"xo{u}", [128, G, D]) for u in range(2)]

        plan, ends = plan_sort()

        def slots(buffers, run):
            s, first, stride, n = run
            return buffers[s][:, first:first + stride * (n - 1) + 1:stride, :]

        w_in = sem("w_in")
        deg_in = [sem(f"deg_in{k}") for k in range(4)]
        made_pool = sem("made_pool")
        made_dve = sem("made_dve")
        logs_in = sem("logs_in")
        logs = sem("logs")
        over_a, over_b, over_c = (sem(f"over_{k}") for k in "abc")

        names = """maskT nbN0 nbN nbT selfT rowc pos1_ps key1 cnt_ps cnts posN_ps keyN drop rem_ps
            validT qp_ps qs qh ps rpS rest1 qm parts1 ac_ps acs asq mean stt vsum std pos2_ps key2 cnt2_ps
            cnt2s empty1 empty2 hot0 hot2 slot_ps slotP minus_ps slotM extremes mT_ps mTs y_ps yss ysum sqf
            varf sdf x1 x1T_ps x1Ts h1_ps h1s z1_ps sq1 var1 sd1 x2 xh xrest1 xm parts2 slot2_ps slot2
            rankw o2 o2T_ps o2Ts hT_ps hTs y2_ps y2sum sq2 var2 sd2 x3 x3T_ps x3Ts x3c_ps x3cs z3_ps
            z3sum sq3 var3 sd3 xo selfN pick row_ps below below_ps seen_pool chain_dve chain_pool""".split()
        s = {n: sem(n) for n in names}
        adjA_in, adjB_in, adjC_in = (sem(f"adj{k}_in") for k in "ABC")
        x_in = [sem(f"x_in{u}") for u in range(2)]
        stored = [sem(f"stored{u}") for u in range(2)]

        def given(t, per=1, k=None):
            return t.n * per + (per if k is None else k)

        def before(eng, name, t, back=1, per=1, k=None):
            if t.least >= back:
                eng.wait_ge(s[name], (t.n - back) * per + (per if k is None else k))

        WEIGHT_LOADS = 23
        MADE_POOL = 3

        TENSOR_ORDER = """
            b2@1 gather2:5@0 gather0:0@2 gather0:1@2 a3@2 gather0:2@2 b3@1 a5@2 b4@1 c1@-1 c2@-1 c3@-1
            gather0:3@2 a6@2 gather0:4@2 c4@-1 c5@-1 gather0:5@2 c6@-1 gather0:6@2 gather0:7@2 gather2:0@1
            gather2:1@1 a2@3 gather2:2@1 a1@3 gather2:3@1 b1@2 gather2:4@1 a1c@3 a1n@3""".split()
        SCALAR_ORDER = """
            gather2:4@0 a1c@2 gather2:5@0 b2@1 gather0:0@2 gather0:1@2 b2s@1 a3@2 b3@1 c1@-1 gather0:2@2 b4@1
            c2@-1 c3@-1 gather0:3@2 a6@2 gather0:4@2 c4@-1 c5@-1 gather0:5@2 b5@1 gather0:6@2 gather0:7@2 c6@-1
            a3s@2 gather2:0@1 gather2:1@1 gather2:2@1 a2@3 b1@2 gather2:3@1""".split()
        GPSIMD_ORDER = """
            a3@0 b5@-1 b0@-1 a6@0 a1@1 a2@1 a4@1""".split()
        VECTOR_ORDER = """
            sort:11-12@0 a1@3 hots0:12-13@2 sort:12-14@0 hots2:4-7@1 c6a@-1 hots2:7-10@1 sort:14-16@0 c6b@-1
            a7@2 a1b@3 sort:16-19@0 hots0:0-1@3 sort:19-22@0 hots0:1-2@3 c6c@-1 sort:22-27@0 hots0:2-3@3
            hots2:10-11@1 a1n@3 sort:27-31@0 hots0:3-5@3 sort:31-34@0 hots0:5-6@3 sort:34-37@0 hots0:6-8@3
            b2a@2 sort:37-38@0 hots0:8-9@3 sort:38-42@0 b2b@2 sort:42-44@0 b2c@2 sort:44-48@0 quantiles@0
            sort:0-1@1 a5@3 hots2:0-1@2 sort:1-2@1 b4b@2 a3@3 b4c@2 hots2:1-2@2 sort:2-4@1 c3a@0 sort:4-5@1
            hots0:9-10@3 c3b@0 sort:5-7@1 a6@3 hots0:10-11@3 hots2:2-3@2 c3c@0 sort:7-11@1 hots0:11-12@3 a3b@3
            hots2:3-4@2""".split()
        SYNC_ORDER = "load_x@3 load_a@3 load_b@2 load_c@0 store@-1".split()

        def pipeline(eng, part, order):
            steps = []
            for entry in order:
                name, lag = entry.split("@")
                name, _, which = name.partition(":")
                steps.append((name, [int(k) for k in which.split("-") if k], int(lag)))
            low, high = min(x[2] for x in steps), max(x[2] for x in steps)

            def slot(i, number):
                if "restart" in part:
                    part["restart"]()
                for name, which, lag in steps:
                    if i is not None or 0 <= number + lag < NG:
                        part[name](Turn(i, number + lag), *which)

            turns = (NG - high + low) // 2
            for number in range(-high, -low):
                slot(None, number)
            with eng.Fori(0, turns) as i:
                slot(i, -low)
                slot(i, -low + 1)
            for number in range(-low + 2 * turns, NG - low):
                slot(None, number)

        def load_adj(eng, t, dst, signal, used):
            before(eng, used, t)
            eng.dma_start(dst[:], adj_cols[:, bass.ds(t.g * G, G), :]).then_inc(signal, 16)

        def load_a(eng, t):
            load_adj(eng, t, adjA, adjA_in, "ac_ps")

        def load_b(eng, t):
            load_adj(eng, t, adjB, adjB_in, "z1_ps")

        def load_c(eng, t):
            load_adj(eng, t, adjC, adjC_in, "z3_ps")

        def load_x(eng, t):
            before(eng, "y_ps", t, 2)
            eng.dma_start(xT0[t.u][:], x_pairs[:, bass.ds(t.g * (G // 2), G // 2), :]).then_inc(x_in[t.u], 16)

        def store_group(eng, t):
            eng.wait_ge(s["xo"], given(t))
            eng.dma_start(out[:, bass.ds(t.g * G, G), :], xo[t.u][:]).then_inc(stored[t.u], 16)

        def sync_fast(sp):
            small = [(raw[0:64, 0, :], w_post[0:64, :]), (raw[64:128, 0, :], w_post[0:64, :]),
                     (raw[0:64, 1, :], w_l1), (raw[64:128, 1, :], w_l1), (raw[:, 9, :], w2),
                     (bd[0:64, 0, 0, :], w_pre[64:128, :]), (bd[64:128, 0, 1, :], w_pre[64:128, :]),
                     (bd[0:64, 1, 0, :], w_pre[0:64, :]), (bd[64:128, 1, 1, :], w_pre[0:64, :]),
                     (w1t[0:64, 0, :], w1), (w1t[64:128, 1, :], w1),
                     (b1t[:, :], b1.rearrange("(h a) -> h a", a=1)), (mask8[:, :], node_mask)]
            for k in range(2):
                for f in range(3):
                    r = D + f * 4 * D + k * 2 * D
                    small.append((raw[:, 3 + 3 * k + f, :], w_post[r:r + 128, :]))
            for k, b in enumerate((b_pre, b_post, b_l1, b2)):
                small.append((biasr[0:1, k, :], b.rearrange("(a d) -> a d", a=1)))
            assert len(small) == WEIGHT_LOADS
            sp.wait_ge(made_pool, 1)
            for k in range(4):
                sp.dma_start(adj_all[:, k * 16:(k + 1) * 16, :],
                             adj_rows[:, k * 16:(k + 1) * 16, :]).then_inc(deg_in[k], 16)
                if k == 0:
                    for dst, src in small:
                        sp.dma_start(dst, src).then_inc(w_in, 16)
                    load_x(sp, Turn(None, 0))
                    load_a(sp, Turn(None, 0))

            def later(load):
                return lambda t: None if t.i is None and t.g == 0 else load(sp, t)

            pipeline(sp, dict(load_x=later(load_x), load_a=later(load_a), load_b=lambda t: load_b(sp, t),
                              load_c=lambda t: load_c(sp, t), store=lambda t: store_group(sp, t)), SYNC_ORDER)
            for u in range(2):
                sp.wait_ge(stored[u], 16 * (NG // 2))

        def tensor_steps(pe):
            mm = nc.tensor.matmul

            def pair(k):
                return bd[:, k, :, :].rearrange("p a d -> p (a d)")

            def flat(ap):
                return ap.rearrange("p g n -> p (g n)")

            def bias(k):
                return biast[0:1, k, :, :].rearrange("a g d -> a (g d)")

            def two(ps, p):
                return ps[:, p * 128:(p + 1) * 128]

            def a1(t):
                pe.wait_ge(s["maskT"], given(t))
                before(pe, "key2", t)
                mm(POS[:, :], upto[:, :], flat(maskT[:, :, :]), start=True, stop=True).then_inc(s["pos1_ps"], 1)

            def a2(t):
                pe.wait_ge(x_in[t.u], t.half * 16 + 16)
                before(pe, "cnt2s", t)
                for p in range(G // 2):
                    mm(two(STAT, p), xT0[t.u][:, p, :], pair(0), start=True, stop=True)
                mm(STAT[:, C:2 * C], onesf[0:1, :], bias(0), start=True, stop=False, skip_group_check=True)
                for p in range(G // 2):
                    last = mm(two(STAT, p + G // 2), xT0[t.u][:, p, :], pair(1),
                              start=False, stop=True, skip_group_check=True)
                last.then_inc(s["qp_ps"], 1)

            def a1c(t):
                pe.wait_ge(s["rpS"], given(t))
                pe.wait_ge(s["nbT"], given(t))
                for g in range(G):
                    mm(STAT[:, g:g + 1], nbT[:, g, :], onesb[:, :], start=True, stop=True)
                    mm(STAT[:, 8 + g:9 + g], maskT[:, g, :], onesb[:, :], start=True, stop=True)
                for g in range(G):
                    last = mm(STAT[0:KP, 128:256], column[:, g, :], maskT[:, g, :], start=g == 0, stop=g == G - 1)
                last.then_inc(s["cnt_ps"], 1)

            def a1n(t):
                pe.wait_ge(s["key1"], given(t))
                pe.wait_ge(s["nbT"], given(t))
                for g in range(G):
                    last = mm(POS[:, g * N:(g + 1) * N], nbT[:, g, :], upto[:, :], start=True, stop=True)
                last.then_inc(s["posN_ps"], 1)

            def a3(t):
                pe.wait_ge(s["qs"], given(t))
                pe.wait_ge(s["cnts"], given(t))
                pe.wait_ge(adjA_in, 16 * given(t))
                for g in range(G):
                    last = mm(two(STAT, g), adjA[:, g, :], QQ[:, g, :, :].rearrange("p a d -> p (a d)"),
                              start=True, stop=True)
                last.then_inc(s["ac_ps"], 1)

            def a5(t):
                pe.wait_ge(s["drop"], given(t))
                pe.wait_ge(s["keyN"], given(t))
                for g in range(G):
                    mm(two(POS, g), drop[:, g, :], identb[:, :], start=True, stop=False)
                    last = mm(two(POS, g), identb[:, :], drop[:, g, :], start=False, stop=True)
                last.then_inc(s["rem_ps"], 1)

            def a6(t):
                pe.wait_ge(s["validT"], given(t))
                mm(POS[:, :], upto[:, :], flat(validT[:, :, :]), start=True, stop=True).then_inc(s["pos2_ps"], 1)
                pe.wait_ge(s["acs"], given(t))
                for g in range(G):
                    mm(STAT[:, g:g + 1], validT[:, g, :], onesb[:, :], start=True, stop=True)
                for g in range(G):
                    last = mm(STAT[0:KP, 128:256], column[:, g, :], validT[:, g, :], start=g == 0, stop=g == G - 1)
                last.then_inc(s["cnt2_ps"], 1)

            def gather_bank(t, b, slots_in, ready, hot, parts, empty):
                ps = GATHER[b % 2]
                both = range(2 * b, min(2 * b + 2, slots_in))
                mm(ps[:, 0:len(both) * C], empty, fill[:, 2 * b:2 * b + len(both), :, :].rearrange(
                    "k s g d -> k (s g d)"), start=True, stop=False, skip_group_check=True)
                for slot in both:
                    pe.wait_ge(s[ready], given(t, slots_in, slot + 1))
                    for g in range(G):
                        at = (slot % 2) * C + g * D
                        for part in range(3):
                            last = mm(ps[:, at:at + D], hot[:, slot % hot.shape[1], g, :], parts[:, part, g, :],
                                      start=False, stop=True, skip_group_check=True)
                return last

            def gather0(t, b):
                if b == 0:
                    pe.wait_ge(s["parts1"], given(t))
                    pe.wait_ge(s["empty1"], given(t))
                    before(pe, "slot2", t, 2, K2B)
                if b < K0B:
                    if b >= 2:
                        pe.wait_ge(s["slotM"], given(t, K0B, b - 1))
                    gather_bank(t, b, K0, "hot0", hot0, qparts, empty1[:, 0, :]).then_inc(s["slot_ps"], 1)
                if b >= 1:
                    pe.wait_ge(s["slotP"], given(t, K0B, b))
                    n = min(2, K0 - 2 * (b - 1))
                    mm(GATHER[(b - 1) % 2][:, 0:n * C], empty1[:, 1, :],
                       fill[:, 2 * b - 2:2 * b - 2 + n, :, :].rearrange("k s g d -> k (s g d)"),
                       start=False, stop=True, skip_group_check=True).then_inc(s["minus_ps"], 1)

            def gather2(t, b):
                if b == 0:
                    pe.wait_ge(s["parts2"], given(t))
                    pe.wait_ge(s["empty2"], given(t))
                    if t.next is not None:
                        pe.wait_ge(s["slotM"], given(t.next, K0B))
                    before(pe, "slot2", t, 1, K2B)
                if b >= 2:
                    pe.wait_ge(s["slot2"], given(t, K2B, b - 1))
                gather_bank(t, b, K2, "hot2", hot2, xparts, empty2[t.u][:, :]).then_inc(s["slot2_ps"], 1)

            def b1(t):
                pe.wait_ge(s["extremes"], given(t))
                pe.wait_ge(s["std"], given(t))
                before(pe, "h1s", t)
                before(pe, "x2", t)
                for k in range(2):
                    for g in range(G):
                        last = nc.tensor.transpose(two((MB, MB2)[k], g),
                                                   m4[:, g, 2 * k:2 * k + 2, :].rearrange("p a d -> p (a d)"),
                                                   ident[:, :])
                    last.then_inc(s["mT_ps"], 1)

            def b2(t):
                pe.wait_ge(s["mTs"], given(t, 2))
                for p in range(G // 2):
                    both = (MB, MB2)[p][:, 0:6 * D].rearrange("p (a f d) -> p a f d", a=2, f=3)
                    mm(both[:, :, 0, :], onesf[0:1, :], biast[0:1, 1, 0:2, :], start=True, stop=False,
                       skip_group_check=True)
                    mm(both[:, :, 0, :], xT0[t.u][:, p, :], bd[:, 2, :, :], start=False, stop=False,
                       skip_group_check=True)
                    for a in range(2):
                        for k in range(2):
                            last = mm(both[:, a, :, :], mT[:, k, 2 * p + a, :], wpost[:, k, :, :],
                                      start=False, stop=True, skip_group_check=True)
                last.then_inc(s["y_ps"], 1)

            def b3(t):
                pe.wait_ge(s["x1"], given(t))
                for p in range(G // 2):
                    last = nc.tensor.transpose(two(MB, p), x1[:, 2 * p:2 * p + 2, :].rearrange("p a d -> p (a d)"),
                                               ident[:, :])
                last.then_inc(s["x1T_ps"], 1)
                pe.wait_ge(s["x1Ts"], given(t))
                for p in range(G // 2):
                    last = mm(two(MB, p + G // 2), x1T[:, p, :], pair(3), start=True, stop=True)
                last.then_inc(s["h1_ps"], 1)

            def b4(t):
                pe.wait_ge(s["ysum"], given(t))
                mm(MB2[:, 0:C], onesf[0:1, :], bias(2), start=True, stop=False, skip_group_check=True)
                for p in range(G // 2):
                    mm(two(MB2, p), x1T[:, p, :], pair(4), start=False, stop=False, skip_group_check=True)
                pe.wait_ge(s["h1s"], given(t))
                pe.wait_ge(adjB_in, 16 * given(t))
                for g in range(G):
                    last = mm(MB2[:, g * D:(g + 1) * D], adjB[:, g, :], h1[:, g, :],
                              start=False, stop=True, skip_group_check=True)
                last.then_inc(s["z1_ps"], 1)

            def c1(t):
                pe.wait_ge(s["o2"], given(t))
                before(pe, "z3sum", t)
                for p in range(G // 2):
                    nc.tensor.transpose(two(PX, p + G // 2),
                                        x2[t.u][:, 2 * p:2 * p + 2, :].rearrange("p a d -> p (a d)"), ident[:, :])
                for p in range(G // 2):
                    last = nc.tensor.transpose(two(PX, p), o2[:, 2 * p:2 * p + 2, :].rearrange("p a d -> p (a d)"),
                                               ident[:, :])
                last.then_inc(s["o2T_ps"], 1)

            def c2(t):
                pe.wait_ge(s["o2Ts"], given(t))
                before(pe, "x3cs", t)
                for a in range(2):
                    last = mm(PX2[:, a * C:(a + 1) * C], w1t[:, a, :], flat(o2T[:, :, :]), start=True, stop=True)
                last.then_inc(s["hT_ps"], 1)

            def c3(t):
                mm(PX[:, 0:C], onesf[0:1, :], bias(3), start=True, stop=False, skip_group_check=True)
                for p in range(G // 2):
                    mm(two(PX, p + G // 2), x2T[:, p, :], pair(4), start=False, stop=True, skip_group_check=True)
                pe.wait_ge(s["hTs"], given(t))
                for g in range(G):
                    last = mm(PX[:, g * D:(g + 1) * D], hT[:, (g % 2) * (G // 2) + g // 2, :], raw[:, 9, :],
                              start=False, stop=True, skip_group_check=True)
                last.then_inc(s["y2_ps"], 1)

            def c4(t):
                pe.wait_ge(s["x3"], given(t))
                for p in range(G // 2):
                    last = nc.tensor.transpose(two(PX, p), x3[:, 2 * p:2 * p + 2, :].rearrange("p a d -> p (a d)"),
                                               ident[:, :])
                last.then_inc(s["x3T_ps"], 1)

            def c5(t):
                pe.wait_ge(s["x3Ts"], given(t))
                for p in range(G // 2):
                    last = mm(two(PX2, p), x3T[:, p, :], pair(4), start=True, stop=True)
                last.then_inc(s["x3c_ps"], 1)

            def c6(t):
                pe.wait_ge(s["x3cs"], given(t))
                pe.wait_ge(adjC_in, 16 * given(t))
                for g in range(G):
                    last = mm(PX[:, g * D:(g + 1) * D], adjC[:, g, :], x3c[:, g, :], start=True, stop=True)
                last.then_inc(s["z3_ps"], 1)

            def general0(t):
                with pe.Fori(0, N) as m:
                    pe.wait_ge(s["parts1"], given(t))
                    node_row(t, m, 0, qparts)

            def general2(t):
                with pe.Fori(0, N) as m:
                    pe.wait_ge(s["parts2"], given(t))
                    node_row(t, m, N, xparts)
                    pe.wait_ge(s["below"], t.g * N + m + 1)
                    for g in range(G):
                        last = mm(RG1[:, g * D:(g + 1) * D], validT[:, g, :], below[:, g, :], start=True, stop=True)
                    last.then_inc(s["below_ps"], 1)

            def node_row(t, m, offset, parts):
                pe.wait_ge(s["pick"], t.g * (2 * N) + m + offset + 1)
                for part in range(3):
                    last = mm(RG0[:, 0:C], pick, flat(parts[:, part, :, :]), start=part == 0, stop=part == 2)
                last.then_inc(s["row_ps"], 1)

            return dict(a1=a1, a1c=a1c, a1n=a1n, a2=a2, a3=a3, a5=a5, a6=a6, gather0=gather0, b1=b1, b2=b2, b3=b3,
                        b4=b4, gather2=gather2, c1=c1, c2=c2, c3=c3, c4=c4, c5=c5, c6=c6, general0=general0,
                        general2=general2)

        def tensor_fast(pe):
            part = tensor_steps(pe)
            pe.wait_ge(made_pool, MADE_POOL)
            pe.wait_ge(made_dve, 1)
            pipeline(pe, part, TENSOR_ORDER)
            pe.wait_ge(over_a, 1)
            nc.tensor.transpose(PX[0:1, 0:128], excess[:, 2:3], ident[:, :]).then_inc(over_b, 1)

        def scalar_steps(act):
            A = nc.scalar.activation

            def flat(ap):
                return ap.rearrange("p g d -> p (g d)")

            def root(t, st, ready, signal):
                act.wait_ge(s[ready], given(t))
                A(st[:, 1, :], st[:, 0, :], ACT.Sqrt, bias=sqrt_eps[:, 1:2], scale=1.0 / D).then_inc(s[signal], 1)

            def a1c(t):
                act.wait_ge(s["cnt_ps"], given(t))
                A(cnt[:, 0, :], STAT[:, 0:G], ACT.Copy)
                A(cnt[:, 1, :], STAT[:, 8:8 + G], ACT.Copy)
                A(cntT1[:, :], STAT[0:KP, 128:256], ACT.Copy).then_inc(s["cnts"], 1)

            def a2(t):
                q = STAT[:, 0:C].rearrange("p (g d) -> p g d", g=G)
                act.wait_ge(s["qp_ps"], given(t))
                if t.fast:
                    before(act, "slot_ps", t, 1, K0B)
                before(act, "extremes", t)
                A(QQ[:, :, 0, :], q, ACT.Copy)
                A(QQ[:, :, 1, :], q, ACT.Square).then_inc(s["qs"], 1)
                A(flat(qparts[:, 0, :, :]), STAT[:, 0:C], ACT.Copy).then_inc(s["qh"], 1)
                A(flat(pS[:, :, :]), STAT[:, C:2 * C], ACT.Copy).then_inc(s["ps"], 1)
                act.wait_ge(s["rowc"], given(t))
                for g in range(G):
                    last = A(rp[:, g, :], STAT[:, C + g * D:C + (g + 1) * D], ACT.Copy,
                             scale=rowc[t.u][:, RATIO, g:g + 1])
                last.then_inc(s["rpS"], 1)
                act.wait_ge(s["rest1"], given(t))
                A(flat(qparts[:, 1, :, :]), flat(rest[:, :, :]), ACT.Copy).then_inc(s["qm"], 1)

            def a3(t):
                act.wait_ge(s["ac_ps"], given(t))
                for g in range(G):
                    last = A(ac[:, g, :, :].rearrange("p a d -> p (a d)"), STAT[:, g * 128:(g + 1) * 128], ACT.Copy,
                             scale=rowc[t.u][:, INV, g:g + 1])
                last.then_inc(s["acs"], 1)
                act.wait_ge(s["acs"], given(t))
                A(asq[:, :, :], ac[:, :, 0, :], ACT.Square).then_inc(s["asq"], 1)

            def a6(t):
                act.wait_ge(s["cnt2_ps"], given(t))
                before(act, "rankw", t, 2)
                A(cnt2[t.u][:, :], STAT[:, 0:G], ACT.Copy)
                A(cntT2[:, :], STAT[0:KP, 128:256], ACT.Copy).then_inc(s["cnt2s"], 1)

            def a3s(t):
                act.wait_ge(s["vsum"], given(t))
                before(act, "mT_ps", t, 1, 2)
                A(m4[:, :, 3, :], vr[:, :, :], ACT.Sqrt, bias=sqrt_eps[:, 0:1]).then_inc(s["std"], 1)

            def gather0(t, b):
                if b == 0:
                    before(act, "extremes", t)
                if b < K0B:
                    n = min(2, K0 - 2 * b)
                    act.wait_ge(s["slot_ps"], given(t, K0B, b + 1))
                    A(flat(slotP[:, 2 * b:2 * b + n, :]), GATHER[b % 2][:, 0:n * C],
                      ACT.Copy).then_inc(s["slotP"], 1)
                if b >= 1:
                    n = min(2, K0 - 2 * (b - 1))
                    act.wait_ge(s["minus_ps"], given(t, K0B, b))
                    A(flat(slotM[:, 2 * b - 2:2 * b - 2 + n, :]), GATHER[(b - 1) % 2][:, 0:n * C],
                      ACT.Copy).then_inc(s["slotM"], 1)

            def b1(t):
                for k in range(2):
                    act.wait_ge(s["mT_ps"], given(t, 2, k + 1))
                    A(flat(mT[:, k, :, :]), (MB, MB2)[k][:, :], ACT.Copy).then_inc(s["mTs"], 1)

            def b2(t):
                act.wait_ge(s["y_ps"], given(t))
                for f, which in ((1, AMP), (2, ATT)):
                    for g in range(G):
                        o = (g % 2) * 3 * D + f * D
                        last = A(ys[:, f - 1, g, :], (MB, MB2)[g // 2][:, o:o + D], ACT.Copy,
                                 scale=rowc[t.u][:, which, g:g + 1])
                last.then_inc(s["yss"], 1)

            def b2s(t):
                act.wait_ge(s["ysum"], given(t))
                A(sqf[:, :], flat(zf[:, :, :]), ACT.Square).then_inc(s["sqf"], 1)
                root(t, stf, "varf", "sdf")

            def b3(t):
                act.wait_ge(s["x1T_ps"], given(t))
                A(flat(x1T[:, :, :]), MB[:, 0:C], ACT.Copy).then_inc(s["x1Ts"], 1)
                act.wait_ge(s["h1_ps"], given(t))
                A(flat(h1[:, :, :]), MB[:, C:2 * C], ACT.Copy).then_inc(s["h1s"], 1)

            def b4(t):
                act.wait_ge(s["z1_ps"], given(t))
                A(sqf[:, :], MB2[:, 0:C], ACT.Square).then_inc(s["sq1"], 1)
                root(t, stf, "var1", "sd1")

            def b5(t):
                act.wait_ge(s["x2"], given(t))
                if t.fast:
                    before(act, "slot2_ps", t, 1, K2B)
                A(flat(xparts[:, 0, :, :]), flat(x2[t.u][:, :, :]), ACT.Copy).then_inc(s["xh"], 1)
                act.wait_ge(s["xrest1"], given(t))
                A(flat(xparts[:, 1, :, :]), flat(rest[:, :, :]), ACT.Copy).then_inc(s["xm"], 1)

            def gather2(t, b):
                n = min(2, K2 - 2 * b)
                act.wait_ge(s["slot2_ps"], given(t, K2B, b + 1))
                A(flat(slot2[t.u][:, 2 * b:2 * b + n, :]), GATHER[b % 2][:, 0:n * C],
                  ACT.Copy).then_inc(s["slot2"], 1)

            def c1(t):
                act.wait_ge(s["o2T_ps"], given(t))
                A(flat(x2T[:, :, :]), PX[:, C:2 * C], ACT.Copy)
                A(flat(o2T[:, :, :]), PX[:, 0:C], ACT.Copy).then_inc(s["o2Ts"], 1)

            def c2(t):
                act.wait_ge(s["hT_ps"], given(t))
                A(flat(hT[:, :, :]), PX2[:, :], ACT.Relu, bias=b1t[:, 0:1]).then_inc(s["hTs"], 1)

            def c3(t):
                act.wait_ge(s["y2sum"], given(t))
                A(sqb[:, :], flat(zb[:, :, :]), ACT.Square).then_inc(s["sq2"], 1)
                root(t, stb, "var2", "sd2")

            def c4(t):
                act.wait_ge(s["x3T_ps"], given(t))
                A(flat(x3T[:, :, :]), PX[:, 0:C], ACT.Copy).then_inc(s["x3Ts"], 1)

            def c5(t):
                act.wait_ge(s["x3c_ps"], given(t))
                A(flat(x3c[:, :, :]), PX2[:, 0:C], ACT.Copy).then_inc(s["x3cs"], 1)

            def c6(t):
                act.wait_ge(s["z3sum"], given(t))
                A(sqb[:, :], flat(zb[:, :, :]), ACT.Square).then_inc(s["sq3"], 1)
                root(t, stb, "var3", "sd3")

            return dict(a1c=a1c, a2=a2, a3=a3, a6=a6, a3s=a3s, gather0=gather0, b1=b1, b2=b2, b2s=b2s, b3=b3, b4=b4,
                        b5=b5, gather2=gather2, c1=c1, c2=c2, c3=c3, c4=c4, c5=c5, c6=c6)

        def scalar_fast(act):
            part = scalar_steps(act)
            act.wait_ge(logs_in, 1)
            nc.scalar.activation(rtmp[:, 1, :], rtmp[:, 0, :], ACT.Ln).then_inc(logs, 1)
            act.wait_ge(made_dve, 1)
            pipeline(act, part, SCALAR_ORDER)

        def gpsimd_steps(pool):
            P = nc.gpsimd
            count = [0]

            def own(ins):
                count[0] += 1
                ins.then_inc(s["chain_pool"], 1)
                pool.wait_ge(s["chain_pool"], count[0])

            def ready(name, t):
                pool.wait_ge(s[name], given(t))
                pool.sem_inc(s["seen_pool"], 1)

            def per_row(ap, n):
                return ap.unsqueeze(2).broadcast_to([128, G, n])

            def constants():
                own(P.memset(w1t[:, :, :], 0.0))
                P.memset(bd[:, :, :, :], 0.0).then_inc(made_pool, 1)
                own(P.memset(ident[:, :], 0.0))
                own(P.affine_select(out=ident[:, :], in_=ident[:, :], compare_op=ALU.not_equal, fill=1.0,
                                    base=0, pattern=[[-1, 128]], channel_multiplier=1))
                P.tensor_copy(identb[:, :], ident[:, :])
                own(P.memset(onesf[:, :], 1.0))
                P.memset(onesb[:, :], 1.0)
                P.affine_select(out=upto[:, :], in_=onesf[:, :], compare_op=ALU.is_ge, fill=0.0,
                                base=0, pattern=[[1, 128]], channel_multiplier=-1)
                own(P.memset(column[:, :, :], 0.0))
                for g in range(G):
                    P.memset(column[:, g, g::G], 1.0)
                own(P.memset(fill[:, :, :, :], 0.0))
                own(P.affine_select(out=fill[:, :, :, :], in_=fill[:, :, :, :], compare_op=ALU.not_equal, fill=EMPTY,
                                    base=0, pattern=[[-G, K0], [-1, G], [0, D]], channel_multiplier=1))
                own(P.memset(slot_no[:, :], float(K0)))
                for k in range(K0 - 1, 0, -1):
                    own(P.affine_select(out=slot_no[:, :], in_=slot_no[:, :], compare_op=ALU.is_ge, fill=float(k),
                                        base=-G * k, pattern=[[0, 1]], channel_multiplier=1))
                P.memset(sqrt_eps[:, 0:1], PNA_EPS)
                P.memset(sqrt_eps[:, 1:2], LN_EPS)
                for r in range(K2):
                    P.memset(rank_of[:, :, PLACE[r], :], float(r))
                for k in range(3):
                    P.memset(tau_w[:, k, :, :], QUANTILE_WEIGHTS[k])
                own(P.memset(most[:, :, :], 0.0))
                P.sem_inc(made_pool, MADE_POOL - 1)

            def a1(t):
                ready("nbN0", t)
                P.affine_select(out=nbN[:, :, :], in_=nbN[:, :, :], compare_op=ALU.not_equal, fill=0.0,
                                base=0, pattern=[[0, G], [-1, N]], channel_multiplier=1).then_inc(s["nbN"], 1)
                if not t.fast:
                    ready("nbN", t)
                    P.affine_select(out=selfN[:, :, :], in_=nbN[:, :, :], compare_op=ALU.not_equal, fill=1.0,
                                    base=0, pattern=[[0, G], [-1, N]], channel_multiplier=1).then_inc(s["selfN"], 1)
                ready("maskT", t)
                P.affine_select(out=nbT[:, :, :], in_=maskT[:, :, :], compare_op=ALU.not_equal, fill=0.0,
                                base=0, pattern=[[0, G], [-1, N]], channel_multiplier=1).then_inc(s["nbT"], 1)
                P.affine_select(out=selfT[:, :, :], in_=maskT[:, :, :], compare_op=ALU.not_equal, fill=1.0,
                                base=0, pattern=[[0, G], [-1, N]], channel_multiplier=1).then_inc(s["selfT"], 1)

            def a2(t):
                ready("qh", t)
                P.tensor_tensor(rest[:, :, :], QQ[:, :, 0, :], qparts[:, 0, :, :], ALU.subtract).then_inc(s["rest1"], 1)
                ready("qm", t)
                P.tensor_tensor(qparts[:, 2, :, :], rest[:, :, :], qparts[:, 1, :, :],
                                ALU.subtract).then_inc(s["parts1"], 1)
                ready("cnts", t)
                P.tensor_scalar(empty1[:, 0, :], cntT1[:, :], slot_no[:, 0:1], None, ALU.is_lt)
                P.tensor_scalar(empty1[:, 1, :], cntT1[:, :], slot_no[:, 0:1], -2.0, ALU.is_lt,
                                ALU.mult).then_inc(s["empty1"], 1)

            def a3(t):
                ready("rpS", t)
                P.tensor_tensor(wpt[:, 0, :, :], pS[:, :, :], rp[:, :, :], ALU.subtract)
                ready("mean", t)
                own(P.tensor_tensor(wpt[:, 1, :, :], m4[:, :, 0, :], ac[:, :, 0, :], ALU.add))
                P.tensor_tensor(wpt[:, 1, :, :], wpt[:, 1, :, :], wpt[:, 0, :, :], ALU.mult).then_inc(s["stt"], 1)

            def a4(t):
                own(P.tensor_scalar(skp[:, 0, :], cnt[:, 0, :], 0.5, 0.25, ALU.mult, ALU.add))
                own(P.tensor_scalar(skp[:, 1, :], skp[:, 0, :], ROUND, None, ALU.add))
                own(P.tensor_scalar(skp[:, 0, :], skp[:, 1, :], -ROUND, None, ALU.add))
                own(P.tensor_scalar(skp[:, 1, :], cnt[:, 0, :], DILATE_ABOVE, None, ALU.is_gt))
                ready("rowc", t)
                own(P.tensor_tensor(skp[:, 2, :], skp[:, 1, :], rowc[t.u][:, MASK, :], ALU.mult))
                own(P.tensor_tensor(skp[:, 3, :], skp[:, 0, :], skp[:, 2, :], ALU.mult))
                own(P.tensor_tensor(skp[:, 4, :], skp[:, 3, :], skp[:, 2, :], ALU.add))
                own(P.tensor_scalar(skp[:, 4, :], skp[:, 4, :], -1.0, None, ALU.add))
                own(P.tensor_tensor(skp[:, 5, :], skp[:, 4, :], skp[:, 3, :], ALU.add))
                ready("keyN", t)
                own(P.tensor_tensor(drop[:, :, :], keyN[:, :, :], per_row(skp[:, 4, :], N), ALU.subtract))
                own(P.tensor_tensor(drop2[:, :, :], keyN[:, :, :], per_row(skp[:, 5, :], N), ALU.subtract))
                own(P.tensor_tensor(drop[:, :, :], drop[:, :, :], drop2[:, :, :], ALU.mult))
                P.tensor_scalar(drop[:, :, :], drop[:, :, :], 0.0, None, ALU.is_equal).then_inc(s["drop"], 1)

            def a6(t):
                ready("cnt2s", t)
                P.tensor_scalar(empty2[t.u][:, :], cntT2[:, :], slot_no[:, 0:1], None, ALU.is_lt).then_inc(s["empty2"], 1)

            def b0(t):
                before(pool, "o2", t, 2)
                pool.sem_inc(s["seen_pool"], 1)
                for k in range(3):
                    own(P.tensor_scalar(post[:, k, :], cnt2[t.u][:, :], -1.0, TAUS[k], ALU.add, ALU.mult))
                own(P.tensor_tensor(hatd[:, :, :, :], rank_of[:, :, :, :],
                                    post[:, :, :].unsqueeze(2).broadcast_to([128, 3, K2, G]), ALU.subtract))
                own(P.tensor_scalar(hatn[:, :, :, :], hatd[:, :, :, :], 0.0, 2.0, ALU.max, ALU.mult))
                own(P.tensor_tensor(hatd[:, :, :, :], hatn[:, :, :, :], hatd[:, :, :, :], ALU.subtract))
                own(P.tensor_scalar(hatd[:, :, :, :], hatd[:, :, :, :], -1.0, 1.0, ALU.mult, ALU.add))
                own(P.tensor_scalar(hatd[:, :, :, :], hatd[:, :, :, :], 0.0, None, ALU.max))
                own(P.tensor_tensor(hatd[:, :, :, :], hatd[:, :, :, :], tau_w[:, :, :, :], ALU.mult))
                own(P.tensor_tensor(hatn[:, 0, :, :], hatd[:, 0, :, :], hatd[:, 1, :, :], ALU.add))
                P.tensor_tensor(rankw[t.u][:, :, :], hatn[:, 0, :, :], hatd[:, 2, :, :],
                                ALU.add).then_inc(s["rankw"], 1)

            def b5(t):
                ready("xh", t)
                P.tensor_tensor(rest[:, :, :], x2[t.u][:, :, :], xparts[:, 0, :, :],
                                ALU.subtract).then_inc(s["xrest1"], 1)
                ready("xm", t)
                P.tensor_tensor(xparts[:, 2, :, :], rest[:, :, :], xparts[:, 1, :, :],
                                ALU.subtract).then_inc(s["parts2"], 1)

            def restart():
                pool.sem_clear(s["chain_pool"])
                count[0] = 0

            return dict(constants=constants, restart=restart, a1=a1, a2=a2, a3=a3, a4=a4, a6=a6, b0=b0, b5=b5)

        def gpsimd_fast(pool):
            part = gpsimd_steps(pool)
            part["constants"]()

            pipeline(pool, part, GPSIMD_ORDER)

        def vector_steps(dve):
            V = nc.vector
            count = [0]

            def own(ins):
                count[0] += 1
                ins.then_inc(s["chain_dve"], 1)
                dve.wait_ge(s["chain_dve"], count[0])

            marks = {}

            def mark(what, ins):
                count[0] += 1
                ins.then_inc(s["chain_dve"], 1)
                marks.setdefault(what, []).append(count[0])

            def need(what, back):
                if what in marks:
                    dve.wait_ge(s["chain_dve"], marks[what][-1 - back])

            def per_row(ap, n=D):
                return ap.unsqueeze(2).broadcast_to([128, ap.shape[1], n])

            def flat(ap):
                return ap.rearrange("p g d -> p (g d)")

            def prepare():
                for k in range(4):
                    dve.wait_ge(deg_in[k], 16)
                    own(V.tensor_reduce(deg[:, k * 16:(k + 1) * 16], adj_all[:, k * 16:(k + 1) * 16, :], AX.X, ALU.add))
                V.tensor_scalar(rtmp[:, 0, :], deg[:, :], 1.0, None, ALU.add).then_inc(logs_in, 1)
                dve.wait_ge(logs_in, 1)
                own(V.reciprocal(rows[:, RDEN, :], rtmp[:, 0, :]))
                own(V.tensor_scalar(rows[:, RDEN, :], rows[:, RDEN, :], FLT_MAX, None, ALU.min))
                own(V.tensor_scalar(rows[:, RATIO, :], deg[:, :], 1.0, None, ALU.max))
                own(V.reciprocal(rows[:, INV, :], rows[:, RATIO, :]))
                own(V.tensor_tensor(rows[:, RATIO, :], deg[:, :], rows[:, INV, :], ALU.mult))
                dve.wait_ge(w_in, 16 * WEIGHT_LOADS)
                own(V.tensor_copy(rows[:, MASK, :], mask8[:, :]))
                dve.wait_ge(logs, 1)
                own(V.tensor_scalar(rows[:, AMP, :], rtmp[:, 1, :], 1.0 / AVG_D_LOG, None, ALU.mult))
                own(V.tensor_scalar(rtmp[:, 0, :], rtmp[:, 1, :], PNA_EPS, None, ALU.max))
                own(V.reciprocal(rtmp[:, 1, :], rtmp[:, 0, :]))
                own(V.tensor_scalar(rows[:, ATT, :], rtmp[:, 1, :], AVG_D_LOG, None, ALU.mult))

                dve.wait_ge(made_pool, MADE_POOL)
                own(V.tensor_copy(raw[0:64, 2, :], ident[0:64, 0:64]))
                own(V.tensor_copy(raw[64:128, 2, :], ident[64:128, 64:128]))
                own(V.tensor_tensor(raw[:, 0, :], raw[:, 0, :], raw[:, 2, :], ALU.add))
                own(V.tensor_reduce(rawmean[:, :], raw[:, :, :], AX.X, ALU.add))
                own(V.tensor_scalar(rawmean[:, :], rawmean[:, :], 1.0 / D, None, ALU.mult))
                own(V.tensor_tensor(raw[:, :, :], raw[:, :, :], per_row(rawmean[:, :]), ALU.subtract))
                for block_of, k in ((0, 2), (1, 3), (2, 4)):
                    V.tensor_copy(bd[0:64, k, 0, :], raw[0:64, block_of, :])
                    V.tensor_copy(bd[64:128, k, 1, :], raw[64:128, block_of, :])
                own(V.tensor_copy(wpost[:, :, :, :].rearrange("p k f d -> p (k f) d"), raw[:, 3:9, :]))
                own(V.tensor_reduce(biasm[0:1, :], biasr[0:1, :, :], AX.X, ALU.add))
                own(V.tensor_scalar(biasm[0:1, :], biasm[0:1, :], 1.0 / D, None, ALU.mult))
                own(V.memset(biasm[0:1, 0:1], 0.0))
                own(V.tensor_tensor(biasr[0:1, :, :], biasr[0:1, :, :],
                                    biasm[0:1, :].unsqueeze(2).broadcast_to([1, 4, D]), ALU.subtract))
                own(V.tensor_copy(biast[0:1, :, :, :], biasr[0:1, :, :].unsqueeze(2).broadcast_to([1, 4, G, D])))
                dve.sem_inc(made_dve, 1)

            def hots(t, lo, hi, slots_in, hot, key, signal, used):
                ring, banks = hot.shape[1], (slots_in + 1) // 2
                for k in range(lo, hi):
                    if k >= ring:
                        dve.wait_ge(s[used], given(t, banks, (k - ring) // 2 + 1))
                    else:
                        last = k + (slots_in - 1 - k) // ring * ring
                        before(dve, used, t, 1, banks, last // 2 + 1)
                    V.tensor_scalar(hot[:, k % ring, :, :], key, k + 1.0, None, ALU.is_equal).then_inc(s[signal], 1)

            def hots0(t, lo, hi):
                dve.wait_ge(s["key1"], given(t))
                hots(t, lo, hi, K0, hot0, key1[:, :, :], "hot0", "slot_ps")

            def hots2(t, lo, hi):
                dve.wait_ge(s["key2"], given(t))
                hots(t, lo, hi, K2, hot2, key2[t.u][:, :, :], "hot2", "slot2_ps")

            def a1(t):
                dve.wait_ge(adjA_in, 16 * given(t))
                V.tensor_scalar(maskT[:, :, :], adjA[:, :, :], 0.0, None, ALU.is_gt).then_inc(s["maskT"], 1)
                V.tensor_scalar(nbN[:, :, :], adj_all[:, bass.ds(t.g * G, G), :], 0.0, None,
                                ALU.is_gt).then_inc(s["nbN0"], 1)
                V.tensor_copy(rowc[t.u][:, :, :], rows[:, :, bass.ds(t.g * G, G)]).then_inc(s["rowc"], 1)

            def a1b(t):
                dve.wait_ge(s["pos1_ps"], given(t))
                dve.wait_ge(s["maskT"], given(t))
                V.tensor_tensor(flat(key1[:, :, :]), POS[:, :], flat(maskT[:, :, :]), ALU.mult).then_inc(s["key1"], 1)

            def a1n(t):
                dve.wait_ge(s["posN_ps"], given(t))
                dve.wait_ge(s["nbN"], given(t))
                V.tensor_tensor(flat(keyN[:, :, :]), POS[:, :], flat(nbN[:, :, :]), ALU.mult).then_inc(s["keyN"], 1)

            def a3(t):
                dve.wait_ge(s["acs"], given(t))
                dve.wait_ge(s["rpS"], given(t))
                before(dve, "mT_ps", t, 1, 2)
                V.tensor_tensor(m4[:, :, 0, :], rp[:, :, :], ac[:, :, 0, :], ALU.add).then_inc(s["mean"], 1)
                dve.wait_ge(s["asq"], given(t))
                own(V.tensor_tensor(vr[:, :, :], ac[:, :, 1, :], asq[:, :, :], ALU.subtract))

            def a3b(t):
                dve.wait_ge(s["stt"], given(t))
                own(V.tensor_tensor(vr[:, :, :], vr[:, :, :], wpt[:, 1, :, :], ALU.add))
                V.tensor_scalar(vr[:, :, :], vr[:, :, :], 0.0, None, ALU.max).then_inc(s["vsum"], 1)

            def a5(t):
                dve.wait_ge(s["rem_ps"], given(t))
                if not t.fast:
                    dve.wait_ge(s["selfN"], t.g + 1)
                    own(V.scalar_tensor_tensor(out=flat(validN[:, :, :]), in0=POS[:, :], scalar=0.0,
                                               in1=flat(selfN[:, :, :]), op0=ALU.is_equal, op1=ALU.mult))
                dve.wait_ge(s["selfT"], given(t))
                V.scalar_tensor_tensor(out=flat(validT[:, :, :]), in0=POS[:, :], scalar=0.0,
                                       in1=flat(selfT[:, :, :]), op0=ALU.is_equal,
                                       op1=ALU.mult).then_inc(s["validT"], 1)

            def a6(t):
                dve.wait_ge(s["pos2_ps"], given(t))
                dve.wait_ge(s["validT"], given(t))
                V.tensor_tensor(flat(key2[t.u][:, :, :]), POS[:, :], flat(validT[:, :, :]),
                                ALU.mult).then_inc(s["key2"], 1)
                dve.wait_ge(s["cnt2s"], given(t))
                V.tensor_tensor(most[:, 0, :], most[:, 0, :], cnt[:, 1, :], ALU.max)
                own(V.tensor_tensor(most[:, 1, :], most[:, 1, :], cnt2[t.u][:, :], ALU.max))

            def a7(t):
                dve.wait_ge(s["slotP"], given(t, K0B))
                dve.wait_ge(s["slotM"], given(t, K0B))
                pairs = ((slotP, ALU.min), (slotM, ALU.max))
                for buf, op in pairs:
                    mark("tree", V.tensor_tensor(buf[:, 0:6, :], buf[:, 0:6, :], buf[:, 6:12, :], op))
                for buf, op in pairs:
                    need("tree", 1)
                    mark("tree", V.tensor_tensor(buf[:, 0:3, :], buf[:, 0:3, :], buf[:, 3:6, :], op))
                for buf, op in pairs:
                    need("tree", 1)
                    mark("tree", V.tensor_tensor(buf[:, 0:2, :], buf[:, 0:2, :], buf[:, 2:13:10, :], op))
                for buf, op in pairs:
                    need("tree", 1)
                    mark("tree", V.tensor_tensor(buf[:, 0, :], buf[:, 0, :], buf[:, 1, :], op))
                dve.wait_ge(s["ps"], given(t))
                for (buf, op), k, most_of in zip(pairs, (2, 1), (NEG_BIG, -NEG_BIG)):
                    need("tree", 1 if k == 2 else 0)
                    last = V.scalar_tensor_tensor(out=m4[:, :, k, :], in0=buf[:, 0, :].rearrange(
                        "p (g d) -> p g d", g=G), scalar=most_of, in1=pS[:, :, :], op0=op, op1=ALU.add)
                last.then_inc(s["extremes"], 1)

            def norm_b(t, sq, st, squared, var):
                dve.wait_ge(s[squared], given(t))
                V.tensor_reduce(st[:, 0, :], sq[:, :].rearrange("p (g d) -> p g d", g=G), AX.X,
                                ALU.add).then_inc(s[var], 1)

            def norm_c(t, z, st, root, dst, signal):
                dve.wait_ge(s[root], given(t))
                own(V.reciprocal(st[:, 2, :], st[:, 1, :]))
                V.tensor_tensor(dst, z, per_row(st[:, 2, :]), ALU.mult).then_inc(s[signal], 1)

            def b2a(t):
                dve.wait_ge(s["yss"], given(t))
                own(V.tensor_tensor(zf[:, :, :], ys[:, 0, :, :], ys[:, 1, :, :], ALU.add))
                for p in range(G // 2):
                    y = (MB, MB2)[p][:, 0:6 * D].rearrange("p (a f d) -> p a f d", a=2, f=3)[:, :, 0, :]
                    last = V.tensor_tensor(zf[:, 2 * p:2 * p + 2, :], y, zf[:, 2 * p:2 * p + 2, :], ALU.add)
                last.then_inc(s["ysum"], 1)

            def b2b(t):
                norm_b(t, sqf, stf, "sqf", "varf")

            def b2c(t):
                norm_c(t, zf[:, :, :], stf, "sdf", x1[:, :, :], "x1")

            def b4b(t):
                norm_b(t, sqf, stf, "sq1", "var1")

            def b4c(t):
                norm_c(t, MB2[:, 0:C].rearrange("p (g d) -> p g d", g=G), stf, "sd1", x2[t.u][:, :, :], "x2")

            def c3a(t):
                own(V.tensor_copy(rowb[:, :, :], rows[:, RDEN:MASK + 1, bass.ds(t.g * G, G)]))
                dve.wait_ge(s["y2_ps"], given(t))
                own(V.tensor_tensor(yb[:, :, :], PX[:, 0:C].rearrange("p (g d) -> p g d", g=G),
                                    per_row(rowb[:, MASK - RDEN, :]), ALU.mult))
                V.tensor_tensor(flat(zb[:, :, :]), PX[:, C:2 * C], flat(yb[:, :, :]), ALU.add).then_inc(s["y2sum"], 1)

            def c3b(t):
                norm_b(t, sqb, stb, "sq2", "var2")

            def c3c(t):
                norm_c(t, zb[:, :, :], stb, "sd2", x3[:, :, :], "x3")

            def c6a(t):
                dve.wait_ge(s["z3_ps"], given(t))
                dve.wait_ge(s["x3cs"], given(t))
                own(V.tensor_tensor(flat(yb[:, :, :]), PX[:, 0:C], flat(x3c[:, :, :]), ALU.add))
                own(V.tensor_tensor(yb[:, :, :], yb[:, :, :], per_row(rowb[:, 0, :]), ALU.mult))
                V.tensor_tensor(zb[:, :, :], yb[:, :, :], x3c[:, :, :], ALU.add).then_inc(s["z3sum"], 1)

            def c6b(t):
                norm_b(t, sqb, stb, "sq3", "var3")

            def c6c(t):
                if t.least >= 2:
                    dve.wait_ge(stored[t.u], t.half * 16)
                norm_c(t, zb[:, :, :], stb, "sd3", xo[t.u][:, :, :], "xo")

            steps = [(layer, step) for layer, todo in enumerate(plan) for step in todo]

            def sort(t, lo, hi):
                buffers = (slot2[t.u], swap)
                for k in range(lo, min(hi, len(steps))):
                    layer, (is_min, in0, in1, dst) = steps[k]
                    if k == 0:
                        dve.wait_ge(s["slot2"], given(t, K2B))
                    elif steps[k - 1][0] != layer:
                        need("sort", 0)
                    mark("sort", V.tensor_tensor(slots(buffers, dst), slots(buffers, in0), slots(buffers, in1),
                                                 ALU.min if is_min else ALU.max))

            def quantiles(t):
                buffers = (slot2[t.u], swap)
                dve.wait_ge(s["rankw"], given(t))
                need("sort", 0)
                prod = slot2[t.u]
                for side, first, stride, n in ends:
                    for place in range(first, first + stride * n, stride):
                        last = V.tensor_tensor(prod[:, place, :].rearrange("p (g d) -> p g d", g=G),
                                               buffers[side][:, place, :].rearrange("p (g d) -> p g d", g=G),
                                               per_row(rankw[t.u][:, place, :]), ALU.mult)
                own(last)
                own(V.tensor_tensor(prod[:, 0:4, :], prod[:, 0:4, :], prod[:, 6:10, :], ALU.add))
                own(V.tensor_tensor(prod[:, 0:2, :], prod[:, 0:2, :], prod[:, 2:4, :], ALU.add))
                own(V.tensor_tensor(prod[:, 0, :], prod[:, 0, :], prod[:, 1, :], ALU.add))
                own(V.tensor_tensor(prod[:, 0, :], prod[:, 0, :], prod[:, 10, :], ALU.add))
                V.tensor_tensor(flat(o2[:, :, :]), prod[:, 0, :], flat(x2[t.u][:, :, :]), ALU.add).then_inc(s["o2"], 1)

            def restart():
                if marks:
                    dve.wait_ge(s["chain_dve"], count[0])
                    marks.clear()
                dve.sem_clear(s["chain_dve"])
                count[0] = 0

            def node(ap, m):
                return ap[:, :, bass.ds(m, 1)].broadcast_to([128, G, D])

            def pick_node(m):
                V.tensor_copy(pick, identb[:, bass.ds(m, 1)].broadcast_to([128, 128])).then_inc(s["pick"], 1)

            def general0(t):
                own(V.tensor_scalar(off[:, :, :], adj_all[:, bass.ds(t.g * G, G), :], 0.0, NEG_BIG,
                                    ALU.is_gt, ALU.mult))
                own(V.tensor_scalar(off[:, :, :], off[:, :, :], -NEG_BIG, None, ALU.add))
                own(V.memset(gmax[:, :, :], -FLT_MAX))
                own(V.memset(gmin[:, :, :], FLT_MAX))
                row = RG0[:, 0:C].rearrange("p (g d) -> p g d", g=G)
                with dve.Fori(0, N) as m:
                    restart()
                    pick_node(m)
                    dve.wait_ge(s["row_ps"], t.g * (2 * N) + m + 1)
                    own(V.tensor_tensor(gtmp[:, 0, :, :], row, node(off, m), ALU.add))
                    own(V.tensor_tensor(gmax[:, :, :], gmax[:, :, :], gtmp[:, 0, :, :], ALU.max))
                    own(V.tensor_tensor(gtmp[:, 0, :, :], row, node(off, m), ALU.subtract))
                    own(V.tensor_tensor(gmin[:, :, :], gmin[:, :, :], gtmp[:, 0, :, :], ALU.min))
                dve.wait_ge(s["ps"], given(t))
                own(V.tensor_tensor(m4[:, :, 2, :], gmin[:, :, :], pS[:, :, :], ALU.add))
                V.tensor_tensor(m4[:, :, 1, :], gmax[:, :, :], pS[:, :, :], ALU.add).then_inc(s["extremes"], 1)

            def general2(t):
                own(V.tensor_tensor(earlier, upto[:, :], identb[:, :], ALU.subtract))
                own(V.memset(gmax[:, :, :], 0.0))
                dve.wait_ge(s["rankw"], given(t))
                row = RG0[:, 0:C].rearrange("p (g d) -> p g d", g=G)
                rank = RG1[:, 0:C].rearrange("p (g d) -> p g d", g=G)
                with dve.Fori(0, N) as m:
                    restart()
                    pick_node(m)
                    dve.wait_ge(s["row_ps"], t.g * (2 * N) + m + N + 1)
                    own(V.tensor_tensor(gtmp[:, 0, :, :], x2[t.u][:, :, :], row, ALU.is_lt))
                    own(V.tensor_tensor(gtmp[:, 1, :, :], x2[t.u][:, :, :], row, ALU.is_le))
                    own(V.tensor_tensor(gtmp[:, 1, :, :], gtmp[:, 1, :, :], gtmp[:, 0, :, :], ALU.subtract))
                    own(V.tensor_tensor(gtmp[:, 1, :, :], gtmp[:, 1, :, :],
                                        slotP[:, 6, bass.ds(m, 1)].unsqueeze(1).broadcast_to([128, G, D]), ALU.mult))
                    V.tensor_tensor(below[:, :, :], gtmp[:, 1, :, :], gtmp[:, 0, :, :],
                                    ALU.add).then_inc(s["below"], 1)
                    dve.wait_ge(s["below_ps"], t.g * N + m + 1)
                    for k in range(3):
                        own(V.tensor_tensor(gtmp[:, 0, :, :], rank, per_row(post[:, k, :]), ALU.subtract))
                        own(V.tensor_scalar(gtmp[:, 1, :, :], gtmp[:, 0, :, :], -1.0, None, ALU.mult))
                        own(V.tensor_tensor(gtmp[:, 0, :, :], gtmp[:, 0, :, :], gtmp[:, 1, :, :], ALU.max))
                        own(V.tensor_scalar(gtmp[:, 0, :, :], gtmp[:, 0, :, :], -1.0, 1.0, ALU.mult, ALU.add))
                        own(V.tensor_scalar(gtmp[:, 0, :, :], gtmp[:, 0, :, :], 0.0, QUANTILE_WEIGHTS[k],
                                            ALU.max, ALU.mult))
                        if k == 0:
                            own(V.tensor_copy(gmin[:, :, :], gtmp[:, 0, :, :]))
                        else:
                            own(V.tensor_tensor(gmin[:, :, :], gmin[:, :, :], gtmp[:, 0, :, :], ALU.add))
                    own(V.tensor_tensor(gmin[:, :, :], gmin[:, :, :], node(validN, m), ALU.mult))
                    own(V.tensor_tensor(gmin[:, :, :], gmin[:, :, :], row, ALU.mult))
                    own(V.tensor_tensor(gmax[:, :, :], gmax[:, :, :], gmin[:, :, :], ALU.add))
                V.tensor_tensor(o2[:, :, :], gmax[:, :, :], x2[t.u][:, :, :], ALU.add).then_inc(s["o2"], 1)

            def check_counts():
                own(V.tensor_reduce(mostn[:, :], most[:, :, :], AX.X, ALU.max))
                own(V.tensor_scalar(excess[:, 0:1], mostn[:, 0:1], float(K0), None, ALU.is_gt))
                own(V.tensor_scalar(excess[:, 1:2], mostn[:, 1:2], float(K2), None, ALU.is_gt))
                V.tensor_tensor(excess[:, 2:3], excess[:, 0:1], excess[:, 1:2], ALU.max).then_inc(over_a, 1)
                dve.wait_ge(over_b, 1)
                own(V.tensor_reduce(over[0:1, :], PX[0:1, 0:128], AX.X, ALU.max))
                V.tensor_copy(overi[0:1, :], over[0:1, :]).then_inc(over_c, 1)

            return dict(prepare=prepare, restart=restart, sort=sort, quantiles=quantiles, a1=a1, a1b=a1b, a1n=a1n,
                        a3=a3, a3b=a3b, a5=a5, a6=a6, a7=a7, hots0=hots0, hots2=hots2, b2a=b2a, b2b=b2b, b2c=b2c,
                        b4b=b4b, b4c=b4c, c3a=c3a, c3b=c3b, c3c=c3c, c6a=c6a, c6b=c6b, c6c=c6c,
                        general0=general0, general2=general2, check_counts=check_counts)

        def vector_fast(dve):
            part = vector_steps(dve)
            part["prepare"]()
            pipeline(dve, part, VECTOR_ORDER)
            part["check_counts"]()

        with nc.Block() as block:
            block.sync(sync_fast)
            block.tensor(tensor_fast)
            block.scalar(scalar_fast)
            block.gpsimd(gpsimd_fast)
            block.vector(vector_fast)

        GENERAL = {
            "tensor": ("a1", "a2", "a1c", "a1n", "a3", "a5", "a6", "general0", "b1", "b2", "b3", "b4", "general2",
                       "c1", "c2", "c3", "c4", "c5", "c6"),
            "scalar": ("a2", "a1c", "a3", "a6", "a3s", "b1", "b2", "b2s", "b3", "b4", "b5",
                       "c1", "c2", "c3", "c4", "c5", "c6"),
            "gpsimd": ("a1", "a2", "a3", "a4", "a6", "b0", "b5"),
            "vector": ("a1", "a1b", "a1n", "a3", "a3b", "a5", "a6", "general0", "b2a", "b2b", "b2c", "b4b", "b4c",
                       "general2", "c3a", "c3b", "c3c", "c6a", "c6b", "c6c"),
        }

        def general(eng, part, order):
            with eng.Fori(0, NG // 2) as i:
                for u in range(2):
                    if "restart" in part:
                        part["restart"]()
                    for step in order:
                        part[step](Turn(i, u, NG))

        any_over = nc.values_load(overi[0:1, 0:1], min_val=0, max_val=1)
        with nc.If(any_over > 0):
            with nc.Block() as block:
                @block.sync
                def _(sp):
                    with sp.Fori(0, NG // 2) as i:
                        for u in range(2):
                            t = Turn(i, u, NG)
                            load_a(sp, t)
                            load_x(sp, t)
                            load_b(sp, t)
                            load_c(sp, t)
                            store_group(sp, t)
                    for u in range(2):
                        sp.wait_ge(stored[u], 16 * NG)

                @block.tensor
                def _(pe):
                    general(pe, tensor_steps(pe), GENERAL["tensor"])

                @block.scalar
                def _(act):
                    general(act, scalar_steps(act), GENERAL["scalar"])

                @block.gpsimd
                def _(pool):
                    general(pool, gpsimd_steps(pool), GENERAL["gpsimd"])

                @block.vector
                def _(dve):
                    general(dve, vector_steps(dve), GENERAL["vector"])


def kernel(**inputs):
    import concourse.bacc as bacc
    from concourse.bass_utils import run_bass_kernel_spmd

    a = {k: np.asarray(v) for k, v in inputs.items()}
    x, adj = a["x"], a["adj"]
    laid = {
        "x_pairs": x.reshape(B // 2, 2, N, D).transpose(1, 3, 0, 2).reshape(2 * D, B // 2, N),
        "adj_rows": adj.transpose(1, 0, 2),
        "adj_cols": adj.transpose(2, 0, 1),
        "node_mask": a["nodemask"].view(np.uint8).T,
        "w_pre": a["L0_gnn_W_pre"], "b_pre": a["L0_gnn_b_pre"],
        "w_post": a["L0_gnn_W_post"], "b_post": a["L0_gnn_b_post"],
        "w_l1": a["L1_gnn_weight"], "b_l1": a["L1_gnn_bias"],
        "w1": a["L2_gnn_W1"], "b1": a["L2_gnn_b1"], "w2": a["L2_gnn_W2"], "b2": a["L2_gnn_b2"],
    }
    nc = bacc.Bacc("TRN2", target_bir_lowering=False, num_devices=1)
    arrays, args = {}, []
    for name, v in laid.items():
        v = np.ascontiguousarray(v)
        arrays[f"{name}_dram"] = v
        args.append(nc.dram_tensor(f"{name}_dram", v.shape, mybir.dt.from_np(v.dtype), kind="ExternalInput").ap())
    args.append(nc.dram_tensor("out_dram", (N, B, D), F32, kind="ExternalOutput").ap())
    adj_kernel(nc, *args)
    got = run_bass_kernel_spmd(nc, [arrays], core_ids=[0]).results[0]["out_dram"]
    return np.ascontiguousarray(np.transpose(got, (1, 0, 2)))
```

```python
from contextlib import ExitStack

import numpy as np

import concourse.bass as bass
from concourse import mybir

ALU = mybir.AluOpType
ACT = mybir.ActivationFunctionType
AX = mybir.AxisListType
F32 = mybir.dt.float32
BF16 = mybir.dt.bfloat16
I32 = mybir.dt.int32
U8 = mybir.dt.uint8

B, N, D, H = 64, 128, 64, 128
G = 4
NG = B // G
C = G * D
HC = 64
LN_EPS = 1e-5
PNA_EPS = 1e-5
AVG_D_LOG = 4.86
DILATE_ABOVE = 10.0
TAUS = (0.25, 0.5, 0.75)
QUANTILE_WEIGHTS = (0.25, 0.5, 0.25)
NEG_BIG = 1.0e9
EMPTY = 2.0 ** 30
MEMBER = 256.0
ROUND = 8388608.0
FLT_MAX = 3.4028234e38
K0 = 13
K2 = 11
K0B = (K0 + 1) // 2
K2B = (K2 + 1) // 2
RING0 = 7
RING2 = 11
KP = K0 * G

NETWORK = (
    ((0, 9), (1, 6), (2, 4), (3, 7), (5, 8)),
    ((0, 1), (3, 5), (4, 10), (6, 9), (7, 8)),
    ((1, 3), (2, 5), (4, 7), (8, 10)),
    ((0, 4), (1, 2), (3, 7), (5, 9), (6, 8)),
    ((0, 1), (2, 6), (4, 5), (7, 8), (9, 10)),
    ((2, 4), (3, 6), (5, 7), (8, 9)),
    ((1, 2), (3, 4), (5, 6), (7, 8)),
    ((2, 3), (4, 5), (6, 7)),
)
PLACE = (10, 9, 8, 6, 2, 7, 3, 0, 1, 4, 5)
assert sorted(PLACE[:9]) == [0, 1, 2, 3, 6, 7, 8, 9, 10]
RANKS = int(np.ceil(max(TAUS) * (K2 - 1))) + 1


def plan_sort():
    live = set(range(RANKS))
    layers = []
    for layer in reversed(NETWORK):
        kept = [(a, b, a in live, b in live) for a, b in layer if a in live or b in live]
        for a, b, _, _ in kept:
            live |= {a, b}
        layers.append(kept)
    layers.reverse()
    side = [0] * K2
    plan = []
    for layer in layers:
        steps = []
        for is_min in (True, False):
            todo = []
            for a, b, low, high in layer:
                if low if is_min else high:
                    x, y = (a, b) if PLACE[a] < PLACE[b] else (b, a)
                    out = a if is_min else b
                    todo.append((PLACE[x], PLACE[y], side[x], side[y], out == x))
            todo.sort()
            while todo:
                first = todo[0]
                best = [first]
                for second in todo[1:]:
                    dx, dy = second[0] - first[0], second[1] - first[1]
                    if dx <= 0 or dy <= 0 or second[2:] != first[2:]:
                        continue
                    run = [first]
                    while (first[0] + len(run) * dx, first[1] + len(run) * dy) + first[2:] in todo:
                        run.append((first[0] + len(run) * dx, first[1] + len(run) * dy) + first[2:])
                    if len(run) > len(best):
                        best = run
                for x in best:
                    todo.remove(x)
                n = len(best)
                dx = best[1][0] - first[0] if n > 1 else 1
                dy = best[1][1] - first[1] if n > 1 else 1
                in0, in1 = (first[2], first[0], dx, n), (first[3], first[1], dy, n)
                src = in0 if first[4] else in1
                steps.append((is_min, in0, in1, (1 - src[0],) + src[1:]))
        for a, b, _, _ in layer:
            side[a] ^= 1
            side[b] ^= 1
        plan.append(steps)
    ends = []
    todo = sorted((PLACE[r], side[r]) for r in range(RANKS))
    while todo:
        p, s = todo[0]
        best = [(p, s)]
        for q, z in todo[1:]:
            run = [(p, s)]
            while z == s and (p + len(run) * (q - p), s) in todo:
                run.append((p + len(run) * (q - p), s))
            if len(run) > len(best):
                best = run
        for x in best:
            todo.remove(x)
        ends.append((s, p, best[1][0] - p if len(best) > 1 else 1, len(best)))
    assert RANKS == 9 == sum(run[3] for run in ends)
    return plan, ends


class Turn:

    def __init__(self, i, offset, past=0):
        self.g = offset if i is None else i * 2 + offset
        self.n = self.g + past
        self.u = offset % 2
        self.half = past // 2 + (offset // 2 if i is None else i + offset // 2)
        self.least = offset + past
        self.fast = past == 0
        self.offset, self.past = offset, past
        self.i = i

    @property
    def next(self):
        if self.i is None and self.g == NG - 1:
            return None
        return Turn(self.i, self.offset + 1, self.past)


def adj_kernel(nc, x_pairs, adj_rows, adj_cols, node_mask, w_pre, b_pre, w_post, b_post,
               w_l1, b_l1, w1, b1, w2, b2, out):
    with ExitStack() as ctx:
        def sb(name, shape, dt=F32):
            return ctx.enter_context(nc.sbuf_tensor(name, shape, dt))

        def sem(name):
            return ctx.enter_context(nc.semaphore(name))

        bank = [ctx.enter_context(nc.psum_tensor(f"bank{k}", [128, 512], F32)) for k in range(8)]
        POS, STAT, MB, MB2, RG0, RG1, PX, PX2 = bank
        GATHER = (RG0, RG1)

        ident = sb("ident", [128, 128])
        identb = sb("identb", [128, 128], BF16)
        minus_i = sb("minus_i", [128, 128], BF16)
        member_i = sb("member_i", [128, 128], BF16)
        upto = sb("upto", [128, 128], BF16)
        onesf = sb("onesf", [128, 128])
        onesb = sb("onesb", [128, 1], BF16)
        column = sb("column", [128, G, KP], BF16)
        fill = sb("fill", [KP, K0, G, D], BF16)
        slot_no = sb("slot_no", [KP, 1])
        sqrt_eps = sb("sqrt_eps", [128, 2])
        not_member = sb("not_member", [128, 1])
        raw = sb("raw", [128, 10, D])
        rawmean = sb("rawmean", [128, 10])
        bd = sb("bd", [128, 5, 2, D])
        wpost = sb("wpost", [128, 2, 3, D])
        w1t = sb("w1t", [128, 2, H])
        b1t = sb("b1t", [128, 1])
        biasr = sb("biasr", [1, 4, D])
        biasm = sb("biasm", [1, 4])
        biast = sb("biast", [1, 5, G, D])
        rank_of = sb("rank_of", [128, 3, K2, G])
        tau_w = sb("tau_w", [128, 3, K2, G])
        mask8 = sb("mask8", [128, B], U8)

        adj_all = sb("adj_all", [128, B, N])
        deg = sb("deg", [128, B])
        rows = sb("rows", [128, 6, B])
        rtmp = sb("rtmp", [128, 2, B])
        INV, RATIO, AMP, ATT, RDEN, MASK = range(6)
        mostn = sb("mostn", [128, 2])
        most = sb("most", [128, 2, G])
        over = sb("over", [1, 1])
        overi = sb("overi", [1, 1], I32)

        adjA, adjB, adjC = (sb(f"adj{k}", [128, G, N]) for k in "ABC")
        xT0 = [sb(f"xT0_{u}", [128, G // 2, N]) for u in range(2)]
        rowc = [sb(f"rowc{u}", [128, 6, G]) for u in range(2)]
        rowb = [sb(f"rowb{u}", [128, 2, G]) for u in range(2)]
        maskT = sb("maskT", [128, G, N], BF16)
        nbN = sb("nbN", [128, G, N], BF16)
        nbT = sb("nbT", [128, G, N], BF16)
        selfT = sb("selfT", [128, G, N], BF16)
        keyN = sb("keyN", [128, G, N], BF16)
        drop = sb("drop", [128, G, N], BF16)
        drop2 = sb("drop2", [128, G, N], BF16)
        validT = sb("validT", [128, G, N], BF16)
        key1 = sb("key1", [128, G, N], BF16)
        key2 = [sb(f"key2_{u}", [128, G, N], BF16) for u in range(2)]
        hot0 = sb("hot0", [128, RING0, G, N], BF16)
        hot2 = sb("hot2", [128, RING2, G, N], BF16)
        cnt = sb("cnt", [128, 2, G])
        cnt2 = [sb(f"cnt2_{u}", [128, G]) for u in range(2)]
        cntT1 = sb("cntT1", [KP, N])
        cntT2 = sb("cntT2", [KP, N])
        empty1 = sb("empty1", [KP, 2, N], BF16)
        empty2 = [sb(f"empty2_{u}", [KP, N], BF16) for u in range(2)]
        skp = sb("skp", [128, 6, G])
        QQ = sb("QQ", [128, G, 2, D])
        pS = sb("pS", [128, G, D])
        rp = sb("rp", [128, G, D])
        qparts = sb("qparts", [128, 3, G, D], BF16)
        xparts = sb("xparts", [128, 3, G, D], BF16)
        ac = sb("ac", [128, G, 2, D])
        asq = sb("asq", [128, G, D])
        wpt = sb("wpt", [128, 2, G, D])
        vr = sb("vr", [128, G, D])
        m4 = sb("m4", [128, G, 4, D])
        mT = sb("mT", [128, 2, G, N])
        slotP = sb("slotP", [128, K0, C])
        slotM = sb("slotM", [128, K0, C])
        ys = sb("ys", [128, 2, G, D])
        off = slotP[:, 0:2, :].rearrange("p k c -> p (k c)").rearrange("p (g n) -> p g n", g=G)
        gmax = slotP[:, 2, :].rearrange("p (g d) -> p g d", g=G)
        gmin = slotP[:, 3, :].rearrange("p (g d) -> p g d", g=G)
        gtmp = slotP[:, 4:6, :].rearrange("p k (g d) -> p k g d", g=G)
        earlier = slotP[:, 6, 0:128]
        validN = hot0[:, 0, :, :]
        selfN = hot0[:, 1, :, :]
        below = hot0[:, 2:4, :, :].rearrange("p k g n -> p (k g n)")[:, 0:C].rearrange("p (g d) -> p g d", g=G)
        pick = hot0[:, 4, 0, :]
        excess = sb("excess", [128, 3])
        zf = sb("zf", [128, G, D])
        sqf = sb("sqf", [128, C])
        stf = sb("stf", [128, 3, G])
        x1 = sb("x1", [128, G, D])
        x1T = sb("x1T", [128, G // 2, N])
        h1 = sb("h1", [128, G, D])
        x2 = [sb(f"x2_{u}", [128, G, D]) for u in range(2)]
        slot2 = [sb(f"slot2_{u}", [128, K2, C]) for u in range(2)]
        swap = sb("swap", [128, K2, C])
        hatd = sb("hatd", [128, 3, K2, G])
        hatn = sb("hatn", [128, 3, K2, G])
        post = sb("post", [128, 3, G])
        rankw = [sb(f"rankw{u}", [128, K2, G]) for u in range(2)]
        o2 = sb("o2", [128, G, D])
        o2T = sb("o2T", [128, G // 2, N])
        x2T = sb("x2T", [128, G // 2, N])
        hT = sb("hT", [128, G, N])
        yb = sb("yb", [128, G, D])
        zb = sb("zb", [128, G, D])
        sqb = sb("sqb", [128, C])
        stb = sb("stb", [128, 3, G])
        x3 = sb("x3", [128, G, D])
        x3T = sb("x3T", [128, G // 2, N])
        x3c = sb("x3c", [128, G, D])
        xo = [sb(f"xo{u}", [128, G, D]) for u in range(2)]

        plan, ends = plan_sort()
        ranks_in = [[first + k * stride for side, first, stride, n in ends for k in range(n) if side == which]
                    for which in range(2)]

        def slots(buffers, run):
            s, first, stride, n = run
            return buffers[s][:, first:first + stride * (n - 1) + 1:stride, :]

        w_in = sem("w_in")
        deg_in = [sem(f"deg_in{k}") for k in range(4)]
        made_pool = sem("made_pool")
        made_dve = sem("made_dve")
        logs_in = sem("logs_in")
        logs = sem("logs")
        over_a, over_b, over_c = (sem(f"over_{k}") for k in "abc")

        names = """maskT nbN0 nbN nbT selfT rowc pos1_ps key1 cnt_ps cnts posN_ps keyN skips drop rem_ps validT
            validN_ps validN qp_ps qs qh ps rpS q2_ps qm q3_ps parts1 ac_ps acs asq mean stt vsum vpos std
            pos2_ps key2 cnt2_ps cnt2s empty1 empty2 hot0 hot2 slot_ps slotP minus_ps slotM extremes mT_ps
            mTs y_ps yss ysum sqf sdf rcf x1 x1T_ps x1Ts h1_ps h1s z1_ps sq1 sd1 rc1 x2 xh x2_ps xm x3p_ps
            parts2 slot2_ps slot2 rankw sorted weighted rowb o2 o2T_ps o2Ts hT_ps hTs y2_ps y2s y2sum sq2
            sd2 rc2 x3 x3T_ps x3Ts x3c_ps x3cs z3_ps z3s z3sum sq3 sd3 rc3 xo selfN pick row_ps below
            below_ps seen_pool chain_dve chain_pool""".split()
        s = {n: sem(n) for n in names}
        adjA_in, adjB_in, adjC_in = (sem(f"adj{k}_in") for k in "ABC")
        x_in = [sem(f"x_in{u}") for u in range(2)]
        stored = [sem(f"stored{u}") for u in range(2)]

        def given(t, per=1, k=None):
            return t.n * per + (per if k is None else k)

        def before(eng, name, t, back=1, per=1, k=None):
            if t.least >= back:
                eng.wait_ge(s[name], (t.n - back) * per + (per if k is None else k))

        WEIGHT_LOADS = 19
        FIRST, OTHERS = slice(0, 16), slice(16, B)
        MADE_POOL = 3

        TENSOR_ORDER = """
            gather2:2@0 b1@1 a2m@2 gather2:3@0 a2l@2 b2@1 a1n@2 gather2:4@0 a1c@2 gather2:5@0 a3@2 gather0:0@2
            gather0:1@2 b3@1 b4@1 c1@-1 gather0:2@2 c2@-1 c3@-1 a5@2 gather0:3@2 a6@2 gather0:4@2 c4@-1
            gather0:5@2 b5@1 gather0:6@2 b6@1 gather0:7@2 c5@-1 a2@3 gather2:0@1 c6@-1 a1@3 gather2:1@1""".split()
        SCALAR_ORDER = """
            gather2:5@0 products:2@-1 b2s@1 products:3@-1 gather0:0@2 b2n@1 products:4@-1 b3@1 a1n@2
            gather0:1@2 a3@2 c1@-1 b4@1 c2@-1 gather0:2@2 c3y@-1 b4n@1 c3@-1 a5@2 gather0:3@2 a6@2 b5@1 c3n@-1
            gather0:4@2 c4@-1 gather0:5@2 b5m@1 gather0:6@2 gather0:7@2 a3s@2 b6@1 c5@-1 c6y@-1 gather2:0@1
            a1b@3 gather2:1@1 a2@3 b1@2 a2m@3 c6@-1 a2l@3 gather2:2@1 c6n@-1 gather2:3@1 products:0@0
            products:1@0 b2@2 gather2:4@1 a1c@3""".split()
        GPSIMD_ORDER = """
            a4@0 a3@0 b0@-1 a6@0 a1@1 a2@1""".split()
        VECTOR_ORDER = """
            sort:46-48@-1 weigh@-1 hots2:10-11@0 hots0:2-4@2 hots2:0-1@1 c1@0 hots0:4-6@2 hots2:1-2@1 b2a@1
            sort:0-2@0 b2c@1 hots0:6-7@2 hots2:2-3@1 sort:2-3@0 hots0:7-9@2 sort:3-4@0 hots0:9-10@2 sort:4-5@0
            quantiles@-1 sort:5-8@0 hots2:3-4@1 sort:8-10@0 a4@2 hots2:4-5@1 hots0:10-11@2 sort:10-13@0
            hots2:5-6@1 sort:13-14@0 b4c@1 hots0:11-12@2 sort:14-15@0 c3a@-1 hots0:12-13@2 a3@2 sort:15-18@0
            c3c@-1 sort:18-19@0 a3b@2 hots2:6-7@1 sort:19-20@0 hots2:7-8@1 a6@2 sort:20-21@0 a1@3 sort:21-27@0
            hots2:8-9@1 sort:27-35@0 a7@2 sort:35-37@0 hots0:0-1@3 sort:37-38@0 hots2:9-10@1 hots0:1-2@3 c6a@-1
            sort:38-43@0 c6c@-1 sort:43-46@0""".split()
        SYNC_ORDER = "load_x@3 load_a@3 load_b@2 load_c@0 store@-1".split()

        def pipeline(eng, part, order, between={}):
            steps = []
            for entry in order:
                name, lag = entry.split("@")
                name, _, which = name.partition(":")
                steps.append((name, [int(k) for k in which.split("-") if k], int(lag)))
            low, high = min(x[2] for x in steps), max(x[2] for x in steps)

            def slot(i, number):
                for name, which, lag in steps:
                    if i is not None or 0 <= number + lag < NG:
                        part[name](Turn(i, number + lag), *which)
                if "restart" in part:
                    part["restart"]()

            first = 2 - low
            turns = (NG - high - first) // 2
            for number in range(-high, first):
                slot(None, number)
                if number + high in between:
                    between[number + high]()
            with eng.Fori(0, turns) as i:
                slot(i, first)
                slot(i, first + 1)
            for number in range(first + 2 * turns, NG - low):
                slot(None, number)

        def load_adj(eng, t, dst, signal, used):
            before(eng, used, t)
            eng.dma_start(dst[:], adj_cols[:, bass.ds(t.g * G, G), :]).then_inc(signal, 16)

        def load_a(eng, t):
            load_adj(eng, t, adjA, adjA_in, "ac_ps")

        def load_b(eng, t):
            load_adj(eng, t, adjB, adjB_in, "z1_ps")

        def load_c(eng, t):
            load_adj(eng, t, adjC, adjC_in, "z3_ps")

        def load_x(eng, t):
            before(eng, "y_ps", t, 2)
            eng.dma_start(xT0[t.u][:], x_pairs[:, bass.ds(t.g * (G // 2), G // 2), :]).then_inc(x_in[t.u], 16)

        def store_group(eng, t):
            eng.wait_ge(s["xo"], given(t))
            eng.dma_start(out[:, bass.ds(t.g * G, G), :], xo[t.u][:]).then_inc(stored[t.u], 16)

        def sync_fast(sp):
            small = [(raw[0:64, 0, :], w_post[0:64, :]), (raw[64:128, 0, :], w_post[0:64, :]),
                     (raw[0:64, 1, :], w_l1), (raw[64:128, 1, :], w_l1), (raw[:, 9, :], w2),
                     (bd[0:64, 0, 0, :], w_pre[64:128, :]), (bd[64:128, 0, 1, :], w_pre[64:128, :]),
                     (bd[0:64, 1, 0, :], w_pre[0:64, :]), (bd[64:128, 1, 1, :], w_pre[0:64, :]),
                     (w1t[0:64, 0, :], w1), (w1t[64:128, 1, :], w1),
                     (b1t[:, :], b1.rearrange("(h a) -> h a", a=1)), (mask8[:, :], node_mask)]
            for k in range(2):
                small.append((raw[:, 3 + 3 * k:6 + 3 * k, :],
                              w_post[D:13 * D, :].rearrange("(f k p) d -> k p f d", f=3, k=2)[k]))
            for k, b in enumerate((b_pre, b_post, b_l1, b2)):
                small.append((biasr[0:1, k, :], b.rearrange("(a d) -> a d", a=1)))
            assert len(small) == WEIGHT_LOADS
            sp.wait_ge(made_pool, 1)
            def load_rows(k):
                sp.dma_start(adj_all[:, k * 16:(k + 1) * 16, :],
                             adj_rows[:, k * 16:(k + 1) * 16, :]).then_inc(deg_in[k], 16)

            load_rows(0)
            for dst, src in small:
                sp.dma_start(dst, src).then_inc(w_in, 16)
            load_x(sp, Turn(None, 0))
            load_a(sp, Turn(None, 0))
            for k in range(1, 4):
                load_rows(k)

            def later(load):
                return lambda t: None if t.i is None and t.g == 0 else load(sp, t)

            pipeline(sp, dict(load_x=later(load_x), load_a=later(load_a), load_b=lambda t: load_b(sp, t),
                              load_c=lambda t: load_c(sp, t), store=lambda t: store_group(sp, t)), SYNC_ORDER)
            for u in range(2):
                sp.wait_ge(stored[u], 16 * (NG // 2))

        def tensor_steps(pe):
            mm = nc.tensor.matmul

            def pair(k):
                return bd[:, k, :, :].rearrange("p a d -> p (a d)")

            def flat(ap):
                return ap.rearrange("p g n -> p (g n)")

            def bias(k):
                return biast[0:1, k + 1, :, :].rearrange("a g d -> a (g d)")

            def two(ps, p):
                return ps[:, p * 128:(p + 1) * 128]

            def positions(of, signal):
                mm(POS[:, :], upto[:, :], flat(of[:, :, :]), start=True, stop=False)
                mm(POS[:, :], member_i[:, :], flat(of[:, :, :]), start=False, stop=True).then_inc(s[signal], 1)

            def a1(t):
                pe.wait_ge(s["maskT"], given(t))
                before(pe, "key2", t)
                positions(maskT, "pos1_ps")

            def a2(t):
                pe.wait_ge(x_in[t.u], t.half * 16 + 16)
                before(pe, "cnt2s", t)
                mm(STAT[:, :], onesf[0:1, :], biast[0:1, 0:2, :, :].rearrange("a k g d -> a (k g d)"), start=True,
                   stop=False, skip_group_check=True)
                for p in range(G // 2):
                    mm(two(STAT, p), xT0[t.u][:, p, :], pair(0), start=False, stop=True, skip_group_check=True)
                for p in range(G // 2):
                    last = mm(two(STAT, p + G // 2), xT0[t.u][:, p, :], pair(1),
                              start=False, stop=True, skip_group_check=True)
                last.then_inc(s["qp_ps"], 1)

            def a1c(t):
                pe.wait_ge(s["parts1"], given(t))
                pe.wait_ge(s["nbT"], given(t))
                for g in range(G):
                    mm(STAT[:, g:g + 1], nbT[:, g, :], onesb[:, :], start=True, stop=True)
                    mm(STAT[:, 8 + g:9 + g], maskT[:, g, :], onesb[:, :], start=True, stop=True)
                for g in range(G):
                    last = mm(STAT[0:KP, 128:256], column[:, g, :], maskT[:, g, :], start=g == 0, stop=g == G - 1)
                last.then_inc(s["cnt_ps"], 1)

            def a1n(t):
                pe.wait_ge(s["key1"], given(t))
                pe.wait_ge(s["nbN"], given(t))
                mm(POS[:, :], member_i[:, :], flat(nbN[:, :, :]), start=True, stop=False, skip_group_check=True)
                pe.wait_ge(s["nbT"], given(t))
                for g in range(G):
                    last = mm(POS[:, g * N:(g + 1) * N], nbT[:, g, :], upto[:, :], start=False, stop=True,
                              skip_group_check=True)
                last.then_inc(s["posN_ps"], 1)

            def minus_part(ps, part, signal):
                mm(ps[:, 0:C], minus_i[:, :], flat(part), start=False, stop=True,
                   skip_group_check=True).then_inc(s[signal], 1)

            def a2m(t):
                pe.wait_ge(s["rpS"], given(t))
                minus_part(STAT, qparts[:, 0, :, :], "q2_ps")

            def a2l(t):
                pe.wait_ge(s["qm"], given(t))
                minus_part(STAT, qparts[:, 1, :, :], "q3_ps")

            def a3(t):
                pe.wait_ge(s["qs"], given(t))
                pe.wait_ge(s["cnts"], given(t))
                pe.wait_ge(adjA_in, 16 * given(t))
                for g in range(G):
                    last = mm(two(STAT, g), adjA[:, g, :], QQ[:, g, :, :].rearrange("p a d -> p (a d)"),
                              start=True, stop=True)
                last.then_inc(s["ac_ps"], 1)

            def kept(ps, own, signal):
                mm(ps[:, :], identb[:, :], flat(own), start=True, stop=False, skip_group_check=True)
                for each in (drop, drop2):
                    for g in range(G):
                        mm(two(ps, g), each[:, g, :], minus_i[:, :], start=False, stop=True, skip_group_check=True)
                    last = mm(ps[:, :], minus_i[:, :], flat(each[:, :, :]), start=False, stop=True,
                              skip_group_check=True)
                last.then_inc(s[signal], 1)

            def a5(t):
                pe.wait_ge(s["drop"], given(t))
                pe.wait_ge(s["keyN"], given(t))
                pe.wait_ge(s["selfT"], given(t))
                kept(POS, selfT[:, :, :], "rem_ps")
                if not t.fast:
                    pe.wait_ge(s["selfN"], t.g + 1)
                    kept(RG1, selfN, "validN_ps")

            def a6(t):
                pe.wait_ge(s["validT"], given(t))
                positions(validT, "pos2_ps")
                pe.wait_ge(s["acs"], given(t))
                for g in range(G):
                    mm(STAT[:, g:g + 1], validT[:, g, :], onesb[:, :], start=True, stop=True)
                for g in range(G):
                    last = mm(STAT[0:KP, 128:256], column[:, g, :], validT[:, g, :], start=g == 0, stop=g == G - 1)
                last.then_inc(s["cnt2_ps"], 1)

            def gather_bank(t, b, slots_in, ready, hot, parts, empty):
                ps = GATHER[b % 2]
                both = range(2 * b, min(2 * b + 2, slots_in))
                mm(ps[:, 0:len(both) * C], empty, fill[:, 2 * b:2 * b + len(both), :, :].rearrange(
                    "k s g d -> k (s g d)"), start=True, stop=False, skip_group_check=True)
                for slot in both:
                    pe.wait_ge(s[ready], given(t, slots_in, slot + 1))
                    for g in range(G):
                        at = (slot % 2) * C + g * D
                        for part in range(3):
                            last = mm(ps[:, at:at + D], hot[:, slot % hot.shape[1], g, :], parts[:, part, g, :],
                                      start=False, stop=True, skip_group_check=True)
                return last

            def b5(t):
                pe.wait_ge(s["xh"], given(t))
                mm(MB[:, 0:C], ident[:, :], flat(x2[t.u][:, :, :]), start=True, stop=False, skip_group_check=True)
                minus_part(MB, xparts[:, 0, :, :], "x2_ps")

            def b6(t):
                pe.wait_ge(s["xm"], given(t))
                minus_part(MB, xparts[:, 1, :, :], "x3p_ps")

            def gather0(t, b):
                if b == 0:
                    pe.wait_ge(s["parts1"], given(t))
                    pe.wait_ge(s["empty1"], given(t))
                    before(pe, "slot2", t, 2, K2B)
                if b < K0B:
                    if b >= 2:
                        pe.wait_ge(s["slotM"], given(t, K0B, b - 1))
                    gather_bank(t, b, K0, "hot0", hot0, qparts, empty1[:, 0, :]).then_inc(s["slot_ps"], 1)
                if b >= 1:
                    pe.wait_ge(s["slotP"], given(t, K0B, b))
                    n = min(2, K0 - 2 * (b - 1))
                    mm(GATHER[(b - 1) % 2][:, 0:n * C], empty1[:, 1, :],
                       fill[:, 2 * b - 2:2 * b - 2 + n, :, :].rearrange("k s g d -> k (s g d)"),
                       start=False, stop=True, skip_group_check=True).then_inc(s["minus_ps"], 1)

            def gather2(t, b):
                if b == 0:
                    pe.wait_ge(s["parts2"], given(t))
                    pe.wait_ge(s["empty2"], given(t))
                    if t.next is not None:
                        pe.wait_ge(s["slotM"], given(t.next, K0B))
                    before(pe, "slot2", t, 1, K2B)
                if b >= 2:
                    pe.wait_ge(s["slot2"], given(t, K2B, b - 1))
                gather_bank(t, b, K2, "hot2", hot2, xparts, empty2[t.u][:, :]).then_inc(s["slot2_ps"], 1)

            def b1(t):
                pe.wait_ge(s["extremes"], given(t))
                pe.wait_ge(s["std"], given(t))
                before(pe, "parts2", t)
                for k in range(2):
                    for g in range(G):
                        last = nc.tensor.transpose(two((MB, MB2)[k], g),
                                                   m4[:, g, 2 * k:2 * k + 2, :].rearrange("p a d -> p (a d)"),
                                                   ident[:, :])
                    last.then_inc(s["mT_ps"], 1)

            def b2(t):
                pe.wait_ge(s["mTs"], given(t, 2))
                for p in range(G // 2):
                    both = (MB, MB2)[p][:, 0:6 * D].rearrange("p (a f d) -> p a f d", a=2, f=3)
                    mm(both[:, :, 0, :], onesf[0:1, :], biast[0:1, 2, 0:2, :], start=True, stop=False,
                       skip_group_check=True)
                    mm(both[:, :, 0, :], xT0[t.u][:, p, :], bd[:, 2, :, :], start=False, stop=False,
                       skip_group_check=True)
                    for a in range(2):
                        for k in range(2):
                            last = mm(both[:, a, :, :], mT[:, k, 2 * p + a, :], wpost[:, k, :, :],
                                      start=False, stop=True, skip_group_check=True)
                last.then_inc(s["y_ps"], 1)

            def b3(t):
                pe.wait_ge(s["x1"], given(t))
                for p in range(G // 2):
                    last = nc.tensor.transpose(two(MB, p), x1[:, 2 * p:2 * p + 2, :].rearrange("p a d -> p (a d)"),
                                               ident[:, :])
                last.then_inc(s["x1T_ps"], 1)
                pe.wait_ge(s["x1Ts"], given(t))
                for p in range(G // 2):
                    last = mm(two(MB, p + G // 2), x1T[:, p, :], pair(3), start=True, stop=True)
                last.then_inc(s["h1_ps"], 1)

            def b4(t):
                pe.wait_ge(s["ysum"], given(t))
                mm(MB2[:, 0:C], onesf[0:1, :], bias(2), start=True, stop=False, skip_group_check=True)
                for p in range(G // 2):
                    mm(two(MB2, p), x1T[:, p, :], pair(4), start=False, stop=False, skip_group_check=True)
                pe.wait_ge(s["h1s"], given(t))
                pe.wait_ge(adjB_in, 16 * given(t))
                for g in range(G):
                    last = mm(MB2[:, g * D:(g + 1) * D], adjB[:, g, :], h1[:, g, :],
                              start=False, stop=True, skip_group_check=True)
                last.then_inc(s["z1_ps"], 1)

            def c1(t):
                pe.wait_ge(s["o2"], given(t))
                before(pe, "z3sum", t)
                for p in range(G // 2):
                    nc.tensor.transpose(two(PX, p + G // 2),
                                        x2[t.u][:, 2 * p:2 * p + 2, :].rearrange("p a d -> p (a d)"), ident[:, :])
                for p in range(G // 2):
                    last = nc.tensor.transpose(two(PX, p), o2[:, 2 * p:2 * p + 2, :].rearrange("p a d -> p (a d)"),
                                               ident[:, :])
                last.then_inc(s["o2T_ps"], 1)

            def c2(t):
                pe.wait_ge(s["o2Ts"], given(t))
                before(pe, "x3cs", t)
                for a in range(2):
                    last = mm(PX2[:, a * C:(a + 1) * C], w1t[:, a, :], flat(o2T[:, :, :]), start=True, stop=True)
                last.then_inc(s["hT_ps"], 1)

            def c3(t):
                mm(PX[:, 0:C], onesf[0:1, :], bias(3), start=True, stop=False, skip_group_check=True)
                for p in range(G // 2):
                    mm(two(PX, p + G // 2), x2T[:, p, :], pair(4), start=False, stop=True, skip_group_check=True)
                pe.wait_ge(s["hTs"], given(t))
                for g in range(G):
                    last = mm(PX[:, g * D:(g + 1) * D], hT[:, (g % 2) * (G // 2) + g // 2, :], raw[:, 9, :],
                              start=False, stop=True, skip_group_check=True)
                last.then_inc(s["y2_ps"], 1)

            def c4(t):
                pe.wait_ge(s["x3"], given(t))
                for p in range(G // 2):
                    last = nc.tensor.transpose(two(PX, p), x3[:, 2 * p:2 * p + 2, :].rearrange("p a d -> p (a d)"),
                                               ident[:, :])
                last.then_inc(s["x3T_ps"], 1)

            def c5(t):
                pe.wait_ge(s["x3Ts"], given(t))
                for p in range(G // 2):
                    last = mm(two(PX2, p), x3T[:, p, :], pair(4), start=True, stop=True)
                last.then_inc(s["x3c_ps"], 1)

            def c6(t):
                pe.wait_ge(s["x3cs"], given(t))
                pe.wait_ge(adjC_in, 16 * given(t))
                for p in range(G // 2):
                    mm(two(PX, p), x3T[:, p, :], pair(4), start=True, stop=False, skip_group_check=True)
                    for g in (2 * p, 2 * p + 1):
                        last = mm(PX[:, g * D:(g + 1) * D], adjC[:, g, :], x3c[:, g, :], start=False, stop=True,
                                  skip_group_check=True)
                last.then_inc(s["z3_ps"], 1)

            def general0(t):
                with pe.Fori(0, N) as m:
                    pe.wait_ge(s["parts1"], given(t))
                    node_row(t, m, 0, qparts)

            def general2(t):
                with pe.Fori(0, N) as m:
                    pe.wait_ge(s["parts2"], given(t))
                    node_row(t, m, N, xparts)
                    pe.wait_ge(s["below"], t.g * N + m + 1)
                    for g in range(G):
                        last = mm(RG1[:, g * D:(g + 1) * D], validT[:, g, :], below[:, g, :], start=True, stop=True)
                    last.then_inc(s["below_ps"], 1)

            def node_row(t, m, offset, parts):
                pe.wait_ge(s["pick"], t.g * (2 * N) + m + offset + 1)
                for part in range(3):
                    last = mm(RG0[:, 0:C], pick, flat(parts[:, part, :, :]), start=part == 0, stop=part == 2)
                last.then_inc(s["row_ps"], 1)

            return dict(a1=a1, a1c=a1c, a1n=a1n, a2=a2, a2m=a2m, a2l=a2l, b5=b5, b6=b6, a3=a3, a5=a5, a6=a6, gather0=gather0, b1=b1, b2=b2, b3=b3,
                        b4=b4, gather2=gather2, c1=c1, c2=c2, c3=c3, c4=c4, c5=c5, c6=c6, general0=general0,
                        general2=general2)

        def tensor_fast(pe):
            part = tensor_steps(pe)
            pe.wait_ge(made_pool, MADE_POOL)
            pe.wait_ge(made_dve, 1)
            pipeline(pe, part, TENSOR_ORDER)
            pe.wait_ge(over_a, 1)
            nc.tensor.transpose(PX[0:1, 0:128], excess[:, 2:3], ident[:, :]).then_inc(over_b, 1)

        def scalar_steps(act):
            A = nc.scalar.activation

            def flat(ap):
                return ap.rearrange("p g d -> p (g d)")

            def root(t, st, sq, z, squared, signal):
                for g in range(G):
                    last = A(sq[:, g * D:(g + 1) * D], z[:, g * D:(g + 1) * D], ACT.Square,
                             accum_out=st[:, 0, g:g + 1])
                last.then_inc(s[squared], 1)
                act.wait_ge(s[squared], given(t))
                A(st[:, 1, :], st[:, 0, :], ACT.Sqrt, bias=sqrt_eps[:, 1:2], scale=1.0 / D).then_inc(s[signal], 1)

            def norm(t, dst, z, st, inverse, signal):
                act.wait_ge(s[inverse], given(t))
                for g in range(G):
                    last = A(dst[:, g, :], z[:, g * D:(g + 1) * D], ACT.Copy, scale=st[:, 2, g:g + 1])
                last.then_inc(s[signal], 1)

            def key(dst, signal):
                A(flat(dst), POS[:, :], ACT.Relu, bias=not_member[:, 0:1]).then_inc(s[signal], 1)

            def a1b(t):
                act.wait_ge(s["pos1_ps"], given(t))
                if t.fast:
                    before(act, "hot0", t, 1, K0)
                key(key1[:, :, :], "key1")

            def a1n(t):
                act.wait_ge(s["posN_ps"], given(t))
                before(act, "drop", t)
                key(keyN[:, :, :], "keyN")

            def a5(t):
                act.wait_ge(s["rem_ps"], given(t))
                A(flat(validT[:, :, :]), POS[:, :], ACT.Relu).then_inc(s["validT"], 1)
                if not t.fast:
                    act.wait_ge(s["validN_ps"], t.g + 1)
                    A(flat(validN), RG1[:, :], ACT.Relu).then_inc(s["validN"], 1)

            def a1c(t):
                act.wait_ge(s["cnt_ps"], given(t))
                A(cnt[:, 0, :], STAT[:, 0:G], ACT.Copy)
                A(cnt[:, 1, :], STAT[:, 8:8 + G], ACT.Copy)
                A(cntT1[:, :], STAT[0:KP, 128:256], ACT.Copy).then_inc(s["cnts"], 1)

            def a2(t):
                q = STAT[:, 0:C].rearrange("p (g d) -> p g d", g=G)
                act.wait_ge(s["qp_ps"], given(t))
                if t.fast:
                    before(act, "slot_ps", t, 1, K0B)
                before(act, "extremes", t)
                A(QQ[:, :, 0, :], q, ACT.Copy)
                A(QQ[:, :, 1, :], q, ACT.Square).then_inc(s["qs"], 1)
                A(flat(qparts[:, 0, :, :]), STAT[:, 0:C], ACT.Copy).then_inc(s["qh"], 1)
                A(flat(pS[:, :, :]), STAT[:, C:2 * C], ACT.Copy).then_inc(s["ps"], 1)
                act.wait_ge(s["rowc"], given(t))
                for g in range(G):
                    last = A(rp[:, g, :], STAT[:, C + g * D:C + (g + 1) * D], ACT.Copy,
                             scale=rowc[t.u][:, RATIO, g:g + 1])
                last.then_inc(s["rpS"], 1)

            def a2m(t):
                act.wait_ge(s["q2_ps"], given(t))
                A(flat(qparts[:, 1, :, :]), STAT[:, 0:C], ACT.Copy).then_inc(s["qm"], 1)

            def a2l(t):
                act.wait_ge(s["q3_ps"], given(t))
                A(flat(qparts[:, 2, :, :]), STAT[:, 0:C], ACT.Copy).then_inc(s["parts1"], 1)

            def a3(t):
                act.wait_ge(s["ac_ps"], given(t))
                for g in range(G):
                    last = A(ac[:, g, :, :].rearrange("p a d -> p (a d)"), STAT[:, g * 128:(g + 1) * 128], ACT.Copy,
                             scale=rowc[t.u][:, INV, g:g + 1])
                last.then_inc(s["acs"], 1)
                act.wait_ge(s["acs"], given(t))
                A(asq[:, :, :], ac[:, :, 0, :], ACT.Square).then_inc(s["asq"], 1)

            def a6(t):
                act.wait_ge(s["pos2_ps"], given(t))
                if t.fast:
                    before(act, "hot2", t, 2, K2)
                key(key2[t.u][:, :, :], "key2")
                act.wait_ge(s["cnt2_ps"], given(t))
                before(act, "rankw", t, 2)
                A(cnt2[t.u][:, :], STAT[:, 0:G], ACT.Copy)
                A(cntT2[:, :], STAT[0:KP, 128:256], ACT.Copy).then_inc(s["cnt2s"], 1)

            def a3s(t):
                act.wait_ge(s["vsum"], given(t))
                before(act, "mT_ps", t, 1, 2)
                A(vr[:, :, :], vr[:, :, :], ACT.Relu).then_inc(s["vpos"], 1)
                act.wait_ge(s["vpos"], given(t))
                A(m4[:, :, 3, :], vr[:, :, :], ACT.Sqrt, bias=sqrt_eps[:, 0:1]).then_inc(s["std"], 1)

            def gather0(t, b):
                if b == 0:
                    before(act, "extremes", t)
                if b < K0B:
                    n = min(2, K0 - 2 * b)
                    act.wait_ge(s["slot_ps"], given(t, K0B, b + 1))
                    A(flat(slotP[:, 2 * b:2 * b + n, :]), GATHER[b % 2][:, 0:n * C],
                      ACT.Copy).then_inc(s["slotP"], 1)
                if b >= 1:
                    n = min(2, K0 - 2 * (b - 1))
                    act.wait_ge(s["minus_ps"], given(t, K0B, b))
                    A(flat(slotM[:, 2 * b - 2:2 * b - 2 + n, :]), GATHER[(b - 1) % 2][:, 0:n * C],
                      ACT.Copy).then_inc(s["slotM"], 1)

            def b1(t):
                for k in range(2):
                    act.wait_ge(s["mT_ps"], given(t, 2, k + 1))
                    A(flat(mT[:, k, :, :]), (MB, MB2)[k][:, :], ACT.Copy).then_inc(s["mTs"], 1)

            def b2(t):
                act.wait_ge(s["y_ps"], given(t))
                for f, which in ((1, AMP), (2, ATT)):
                    for g in range(G):
                        o = (g % 2) * 3 * D + f * D
                        last = A(ys[:, f - 1, g, :], (MB, MB2)[g // 2][:, o:o + D], ACT.Copy,
                                 scale=rowc[t.u][:, which, g:g + 1])
                last.then_inc(s["yss"], 1)

            def b2s(t):
                act.wait_ge(s["ysum"], given(t))
                root(t, stf, sqf, flat(zf[:, :, :]), "sqf", "sdf")

            def b2n(t):
                norm(t, x1, flat(zf[:, :, :]), stf, "rcf", "x1")

            def b3(t):
                act.wait_ge(s["x1T_ps"], given(t))
                A(flat(x1T[:, :, :]), MB[:, 0:C], ACT.Copy).then_inc(s["x1Ts"], 1)
                act.wait_ge(s["h1_ps"], given(t))
                A(flat(h1[:, :, :]), MB[:, C:2 * C], ACT.Copy).then_inc(s["h1s"], 1)

            def b4(t):
                act.wait_ge(s["z1_ps"], given(t))
                root(t, stf, sqf, MB2[:, 0:C], "sq1", "sd1")

            def b4n(t):
                before(act, "o2T_ps", t, 2)
                norm(t, x2[t.u], MB2[:, 0:C], stf, "rc1", "x2")

            def b5(t):
                act.wait_ge(s["x2"], given(t))
                if t.fast:
                    before(act, "slot2_ps", t, 1, K2B)
                A(flat(xparts[:, 0, :, :]), flat(x2[t.u][:, :, :]), ACT.Copy).then_inc(s["xh"], 1)

            def b5m(t):
                act.wait_ge(s["x2_ps"], given(t))
                A(flat(xparts[:, 1, :, :]), MB[:, 0:C], ACT.Copy).then_inc(s["xm"], 1)

            def b6(t):
                act.wait_ge(s["x3p_ps"], given(t))
                A(flat(xparts[:, 2, :, :]), MB[:, 0:C], ACT.Copy).then_inc(s["parts2"], 1)

            def gather2(t, b):
                n = min(2, K2 - 2 * b)
                act.wait_ge(s["slot2_ps"], given(t, K2B, b + 1))
                A(flat(slot2[t.u][:, 2 * b:2 * b + n, :]), GATHER[b % 2][:, 0:n * C],
                  ACT.Copy).then_inc(s["slot2"], 1)

            def products(t, which):
                act.wait_ge(s["sorted"], given(t))
                act.wait_ge(s["rankw"], given(t))
                place = ranks_in[0][which]
                for g in range(G):
                    one = slot2[t.u][:, place, g * D:(g + 1) * D]
                    last = A(one, one, ACT.Copy, scale=rankw[t.u][:, place, g:g + 1])
                last.then_inc(s["weighted"], 1)

            def scaled(t, which, signal):
                act.wait_ge(s["rowb"], given(t))
                for g in range(G):
                    last = A(yb[:, g, :], PX[:, g * D:(g + 1) * D], ACT.Copy, scale=rowb[t.u][:, which, g:g + 1])
                last.then_inc(s[signal], 1)

            def c3y(t):
                act.wait_ge(s["y2_ps"], given(t))
                scaled(t, MASK - RDEN, "y2s")

            def c6y(t):
                act.wait_ge(s["z3_ps"], given(t))
                scaled(t, 0, "z3s")

            def c1(t):
                act.wait_ge(s["o2T_ps"], given(t))
                A(flat(x2T[:, :, :]), PX[:, C:2 * C], ACT.Copy)
                A(flat(o2T[:, :, :]), PX[:, 0:C], ACT.Copy).then_inc(s["o2Ts"], 1)

            def c2(t):
                act.wait_ge(s["hT_ps"], given(t))
                A(flat(hT[:, :, :]), PX2[:, :], ACT.Relu, bias=b1t[:, 0:1]).then_inc(s["hTs"], 1)

            def c3(t):
                act.wait_ge(s["y2sum"], given(t))
                root(t, stb, sqb, flat(zb[:, :, :]), "sq2", "sd2")

            def c3n(t):
                norm(t, x3, flat(zb[:, :, :]), stb, "rc2", "x3")

            def c4(t):
                act.wait_ge(s["x3T_ps"], given(t))
                A(flat(x3T[:, :, :]), PX[:, 0:C], ACT.Copy).then_inc(s["x3Ts"], 1)

            def c5(t):
                act.wait_ge(s["x3c_ps"], given(t))
                A(flat(x3c[:, :, :]), PX2[:, 0:C], ACT.Copy).then_inc(s["x3cs"], 1)

            def c6(t):
                act.wait_ge(s["z3sum"], given(t))
                root(t, stb, sqb, flat(zb[:, :, :]), "sq3", "sd3")

            def c6n(t):
                if t.least >= 2:
                    act.wait_ge(stored[t.u], t.half * 16)
                norm(t, xo[t.u], flat(zb[:, :, :]), stb, "rc3", "xo")

            return dict(products=products, c3y=c3y, c6y=c6y, a1b=a1b, a1n=a1n, a5=a5, a2m=a2m, a2l=a2l, b2n=b2n, b4n=b4n, b5m=b5m, b6=b6, c3n=c3n,
                        c6n=c6n, a1c=a1c, a2=a2, a3=a3, a6=a6, a3s=a3s, gather0=gather0, b1=b1, b2=b2, b2s=b2s, b3=b3, b4=b4,
                        b5=b5, gather2=gather2, c1=c1, c2=c2, c3=c3, c4=c4, c5=c5, c6=c6)

        def scalar_fast(act):
            part = scalar_steps(act)

            def logarithm(graphs, part):
                act.wait_ge(logs_in, part)
                nc.scalar.activation(rtmp[:, 1, graphs], rtmp[:, 0, graphs], ACT.Ln).then_inc(logs, 1)

            logarithm(FIRST, 1)
            act.wait_ge(made_dve, 1)
            pipeline(act, part, SCALAR_ORDER, {1: lambda: logarithm(OTHERS, 2)})

        def gpsimd_steps(pool):
            P = nc.gpsimd
            count = [0]

            def own(ins):
                count[0] += 1
                ins.then_inc(s["chain_pool"], 1)
                pool.wait_ge(s["chain_pool"], count[0])

            def ready(name, t):
                pool.wait_ge(s[name], given(t))
                pool.sem_inc(s["seen_pool"], 1)

            def constants():
                own(P.memset(w1t[:, :, :], 0.0))
                P.memset(bd[:, :, :, :], 0.0).then_inc(made_pool, 1)
                own(P.memset(ident[:, :], 0.0))
                own(P.affine_select(out=ident[:, :], in_=ident[:, :], compare_op=ALU.not_equal, fill=1.0,
                                    base=0, pattern=[[-1, 128]], channel_multiplier=1))
                P.tensor_copy(identb[:, :], ident[:, :])
                P.tensor_scalar(minus_i[:, :], ident[:, :], -1.0, None, ALU.mult)
                P.tensor_scalar(member_i[:, :], ident[:, :], MEMBER, None, ALU.mult)
                P.memset(not_member[:, :], -MEMBER)
                own(P.memset(onesf[:, :], 1.0))
                P.memset(onesb[:, :], 1.0)
                P.affine_select(out=upto[:, :], in_=onesf[:, :], compare_op=ALU.is_ge, fill=0.0,
                                base=0, pattern=[[1, 128]], channel_multiplier=-1)
                own(P.memset(column[:, :, :], 0.0))
                for g in range(G):
                    P.memset(column[:, g, g::G], 1.0)
                own(P.memset(fill[:, :, :, :], 0.0))
                own(P.affine_select(out=fill[:, :, :, :], in_=fill[:, :, :, :], compare_op=ALU.not_equal, fill=EMPTY,
                                    base=0, pattern=[[-G, K0], [-1, G], [0, D]], channel_multiplier=1))
                own(P.memset(slot_no[:, :], float(K0)))
                for k in range(K0 - 1, 0, -1):
                    own(P.affine_select(out=slot_no[:, :], in_=slot_no[:, :], compare_op=ALU.is_ge, fill=float(k),
                                        base=-G * k, pattern=[[0, 1]], channel_multiplier=1))
                P.memset(sqrt_eps[:, 0:1], PNA_EPS)
                P.memset(sqrt_eps[:, 1:2], LN_EPS)
                for r in range(K2):
                    P.memset(rank_of[:, :, PLACE[r], :], float(r))
                for k in range(3):
                    P.memset(tau_w[:, k, :, :], QUANTILE_WEIGHTS[k])
                own(P.memset(most[:, :, :], 0.0))
                P.sem_inc(made_pool, MADE_POOL - 1)

            def a1(t):
                ready("nbN0", t)
                P.affine_select(out=nbN[:, :, :], in_=nbN[:, :, :], compare_op=ALU.not_equal, fill=0.0,
                                base=0, pattern=[[0, G], [-1, N]], channel_multiplier=1).then_inc(s["nbN"], 1)
                if not t.fast:
                    ready("nbN", t)
                    P.affine_select(out=selfN[:, :, :], in_=nbN[:, :, :], compare_op=ALU.not_equal, fill=1.0,
                                    base=0, pattern=[[0, G], [-1, N]], channel_multiplier=1).then_inc(s["selfN"], 1)
                ready("maskT", t)
                P.affine_select(out=nbT[:, :, :], in_=maskT[:, :, :], compare_op=ALU.not_equal, fill=0.0,
                                base=0, pattern=[[0, G], [-1, N]], channel_multiplier=1).then_inc(s["nbT"], 1)
                P.affine_select(out=selfT[:, :, :], in_=maskT[:, :, :], compare_op=ALU.not_equal, fill=1.0,
                                base=0, pattern=[[0, G], [-1, N]], channel_multiplier=1).then_inc(s["selfT"], 1)

            def a2(t):
                if t.fast:
                    before(pool, "minus_ps", t, 1, K0B)
                    pool.sem_inc(s["seen_pool"], 1)
                ready("cnts", t)
                P.tensor_scalar(empty1[:, 0, :], cntT1[:, :], slot_no[:, 0:1], None, ALU.is_lt)
                P.tensor_scalar(empty1[:, 1, :], cntT1[:, :], slot_no[:, 0:1], -2.0, ALU.is_lt,
                                ALU.mult).then_inc(s["empty1"], 1)

            def a3(t):
                ready("rpS", t)
                P.tensor_tensor(wpt[:, 0, :, :], pS[:, :, :], rp[:, :, :], ALU.subtract)
                ready("mean", t)
                own(P.tensor_tensor(wpt[:, 1, :, :], m4[:, :, 0, :], ac[:, :, 0, :], ALU.add))
                P.tensor_tensor(wpt[:, 1, :, :], wpt[:, 1, :, :], wpt[:, 0, :, :], ALU.mult).then_inc(s["stt"], 1)

            def a4(t):
                ready("cnts", t)
                before(pool, "drop", t)
                pool.sem_inc(s["seen_pool"], 1)
                own(P.tensor_scalar(skp[:, 0, :], cnt[:, 0, :], 0.5, 0.25, ALU.mult, ALU.add))
                own(P.tensor_scalar(skp[:, 1, :], skp[:, 0, :], ROUND, None, ALU.add))
                own(P.tensor_scalar(skp[:, 0, :], skp[:, 1, :], -ROUND, None, ALU.add))
                own(P.tensor_scalar(skp[:, 1, :], cnt[:, 0, :], DILATE_ABOVE, None, ALU.is_gt))
                ready("rowc", t)
                own(P.tensor_tensor(skp[:, 2, :], skp[:, 1, :], rowc[t.u][:, MASK, :], ALU.mult))
                own(P.tensor_tensor(skp[:, 3, :], skp[:, 0, :], skp[:, 2, :], ALU.mult))
                own(P.tensor_tensor(skp[:, 4, :], skp[:, 3, :], skp[:, 2, :], ALU.add))
                own(P.tensor_scalar(skp[:, 4, :], skp[:, 4, :], -1.0, None, ALU.add))
                P.tensor_tensor(skp[:, 5, :], skp[:, 4, :], skp[:, 3, :], ALU.add).then_inc(s["skips"], 1)

            def a6(t):
                ready("cnt2s", t)
                P.tensor_scalar(empty2[t.u][:, :], cntT2[:, :], slot_no[:, 0:1], None, ALU.is_lt).then_inc(s["empty2"], 1)

            def b0(t):
                before(pool, "o2", t, 2)
                pool.sem_inc(s["seen_pool"], 1)
                for k in range(3):
                    own(P.tensor_scalar(post[:, k, :], cnt2[t.u][:, :], -1.0, TAUS[k], ALU.add, ALU.mult))
                own(P.tensor_tensor(hatd[:, :, :, :], rank_of[:, :, :, :],
                                    post[:, :, :].unsqueeze(2).broadcast_to([128, 3, K2, G]), ALU.subtract))
                own(P.tensor_scalar(hatn[:, :, :, :], hatd[:, :, :, :], 0.0, 2.0, ALU.max, ALU.mult))
                own(P.tensor_tensor(hatd[:, :, :, :], hatn[:, :, :, :], hatd[:, :, :, :], ALU.subtract))
                own(P.tensor_scalar(hatd[:, :, :, :], hatd[:, :, :, :], -1.0, 1.0, ALU.mult, ALU.add))
                own(P.tensor_scalar(hatd[:, :, :, :], hatd[:, :, :, :], 0.0, None, ALU.max))
                own(P.tensor_tensor(hatd[:, :, :, :], hatd[:, :, :, :], tau_w[:, :, :, :], ALU.mult))
                own(P.tensor_tensor(hatn[:, 0, :, :], hatd[:, 0, :, :], hatd[:, 1, :, :], ALU.add))
                P.tensor_tensor(rankw[t.u][:, :, :], hatn[:, 0, :, :], hatd[:, 2, :, :],
                                ALU.add).then_inc(s["rankw"], 1)

            def restart():
                pool.sem_clear(s["chain_pool"])
                count[0] = 0

            return dict(constants=constants, restart=restart, a1=a1, a2=a2, a3=a3, a4=a4, a6=a6, b0=b0)

        def gpsimd_fast(pool):
            part = gpsimd_steps(pool)
            part["constants"]()

            pipeline(pool, part, GPSIMD_ORDER)

        def vector_steps(dve):
            V = nc.vector
            count = [0]

            def own(ins):
                count[0] += 1
                ins.then_inc(s["chain_dve"], 1)
                dve.wait_ge(s["chain_dve"], count[0])

            marks = {}

            def mark(what, ins):
                count[0] += 1
                ins.then_inc(s["chain_dve"], 1)
                marks.setdefault(what, []).append(count[0])

            def need(what, back):
                if what in marks:
                    dve.wait_ge(s["chain_dve"], marks[what][-1 - back])

            def per_row(ap, n=D):
                return ap.unsqueeze(2).broadcast_to([128, ap.shape[1], n])

            def flat(ap):
                return ap.rearrange("p g d -> p (g d)")

            def degrees(graphs):
                for k in range(graphs.start // 16, graphs.stop // 16):
                    dve.wait_ge(deg_in[k], 16)
                    own(V.tensor_reduce(deg[:, k * 16:(k + 1) * 16], adj_all[:, k * 16:(k + 1) * 16, :], AX.X, ALU.add))
                V.tensor_scalar(rtmp[:, 0, graphs], deg[:, graphs], 1.0, None, ALU.add).then_inc(logs_in, 1)

            def factors(graphs, part):
                dve.wait_ge(logs_in, part)
                own(V.reciprocal(rows[:, RDEN, graphs], rtmp[:, 0, graphs]))
                own(V.tensor_scalar(rows[:, RDEN, graphs], rows[:, RDEN, graphs], FLT_MAX, None, ALU.min))
                own(V.tensor_scalar(rows[:, RATIO, graphs], deg[:, graphs], 1.0, None, ALU.max))
                own(V.reciprocal(rows[:, INV, graphs], rows[:, RATIO, graphs]))
                own(V.tensor_tensor(rows[:, RATIO, graphs], deg[:, graphs], rows[:, INV, graphs], ALU.mult))
                dve.wait_ge(logs, part)
                own(V.tensor_scalar(rows[:, AMP, graphs], rtmp[:, 1, graphs], 1.0 / AVG_D_LOG, None, ALU.mult))
                own(V.tensor_scalar(rtmp[:, 0, graphs], rtmp[:, 1, graphs], PNA_EPS, None, ALU.max))
                own(V.reciprocal(rtmp[:, 1, graphs], rtmp[:, 0, graphs]))
                own(V.tensor_scalar(rows[:, ATT, graphs], rtmp[:, 1, graphs], AVG_D_LOG, None, ALU.mult))

            def prepare():
                degrees(FIRST)
                factors(FIRST, 1)
                dve.wait_ge(w_in, 16 * WEIGHT_LOADS)
                own(V.tensor_copy(rows[:, MASK, :], mask8[:, :]))

                dve.wait_ge(made_pool, MADE_POOL)
                own(V.tensor_copy(raw[0:64, 2, :], ident[0:64, 0:64]))
                own(V.tensor_copy(raw[64:128, 2, :], ident[64:128, 64:128]))
                own(V.tensor_tensor(raw[:, 0, :], raw[:, 0, :], raw[:, 2, :], ALU.add))
                own(V.tensor_reduce(rawmean[:, :], raw[:, :, :], AX.X, ALU.add))
                own(V.tensor_scalar(rawmean[:, :], rawmean[:, :], 1.0 / D, None, ALU.mult))
                own(V.tensor_tensor(raw[:, :, :], raw[:, :, :], per_row(rawmean[:, :]), ALU.subtract))
                for block_of, k in ((0, 2), (1, 3), (2, 4)):
                    V.tensor_copy(bd[0:64, k, 0, :], raw[0:64, block_of, :])
                    V.tensor_copy(bd[64:128, k, 1, :], raw[64:128, block_of, :])
                own(V.tensor_copy(wpost[:, :, :, :].rearrange("p k f d -> p (k f) d"), raw[:, 3:9, :]))
                own(V.tensor_reduce(biasm[0:1, :], biasr[0:1, :, :], AX.X, ALU.add))
                own(V.tensor_scalar(biasm[0:1, :], biasm[0:1, :], 1.0 / D, None, ALU.mult))
                own(V.memset(biasm[0:1, 0:1], 0.0))
                own(V.tensor_tensor(biasr[0:1, :, :], biasr[0:1, :, :],
                                    biasm[0:1, :].unsqueeze(2).broadcast_to([1, 4, D]), ALU.subtract))
                own(V.memset(biast[0:1, 0, :, :], 0.0))
                own(V.tensor_copy(biast[0:1, 1:5, :, :], biasr[0:1, :, :].unsqueeze(2).broadcast_to([1, 4, G, D])))
                dve.sem_inc(made_dve, 1)

            def hots(t, lo, hi, slots_in, hot, key, signal, used):
                ring, banks = hot.shape[1], (slots_in + 1) // 2
                for k in range(lo, hi):
                    if k >= ring:
                        dve.wait_ge(s[used], given(t, banks, (k - ring) // 2 + 1))
                    else:
                        last = k + (slots_in - 1 - k) // ring * ring
                        before(dve, used, t, 1, banks, last // 2 + 1)
                    V.tensor_scalar(hot[:, k % ring, :, :], key, k + 1.0, None, ALU.is_equal).then_inc(s[signal], 1)

            def hots0(t, lo, hi):
                dve.wait_ge(s["key1"], given(t))
                hots(t, lo, hi, K0, hot0, key1[:, :, :], "hot0", "slot_ps")

            def hots2(t, lo, hi):
                dve.wait_ge(s["key2"], given(t))
                hots(t, lo, hi, K2, hot2, key2[t.u][:, :, :], "hot2", "slot2_ps")

            def a1(t):
                dve.wait_ge(adjA_in, 16 * given(t))
                V.tensor_scalar(maskT[:, :, :], adjA[:, :, :], 0.0, None, ALU.is_gt).then_inc(s["maskT"], 1)
                V.tensor_scalar(nbN[:, :, :], adj_all[:, bass.ds(t.g * G, G), :], 0.0, None,
                                ALU.is_gt).then_inc(s["nbN0"], 1)
                V.tensor_copy(rowc[t.u][:, :, :], rows[:, :, bass.ds(t.g * G, G)]).then_inc(s["rowc"], 1)

            def a4(t):
                dve.wait_ge(s["keyN"], given(t))
                dve.wait_ge(s["skips"], given(t))
                before(dve, "validT", t)
                for k, each in ((4, drop), (5, drop2)):
                    for g in range(G):
                        last = V.tensor_scalar(each[:, g, :], keyN[:, g, :], skp[:, k, g:g + 1], None, ALU.is_equal)
                last.then_inc(s["drop"], 1)

            def a3(t):
                dve.wait_ge(s["acs"], given(t))
                dve.wait_ge(s["rpS"], given(t))
                before(dve, "mT_ps", t, 1, 2)
                V.tensor_tensor(m4[:, :, 0, :], rp[:, :, :], ac[:, :, 0, :], ALU.add).then_inc(s["mean"], 1)
                dve.wait_ge(s["asq"], given(t))
                own(V.tensor_tensor(vr[:, :, :], ac[:, :, 1, :], asq[:, :, :], ALU.subtract))

            def a3b(t):
                dve.wait_ge(s["stt"], given(t))
                V.tensor_tensor(vr[:, :, :], vr[:, :, :], wpt[:, 1, :, :], ALU.add).then_inc(s["vsum"], 1)

            def a6(t):
                dve.wait_ge(s["cnt2s"], given(t))
                V.tensor_tensor(most[:, 0, :], most[:, 0, :], cnt[:, 1, :], ALU.max)
                own(V.tensor_tensor(most[:, 1, :], most[:, 1, :], cnt2[t.u][:, :], ALU.max))

            def a7(t):
                dve.wait_ge(s["slotP"], given(t, K0B))
                dve.wait_ge(s["slotM"], given(t, K0B))
                pairs = ((slotP, ALU.min), (slotM, ALU.max))
                for buf, op in pairs:
                    mark("tree", V.tensor_tensor(buf[:, 0:6, :], buf[:, 0:6, :], buf[:, 6:12, :], op))
                for buf, op in pairs:
                    need("tree", 1)
                    mark("tree", V.tensor_tensor(buf[:, 0:3, :], buf[:, 0:3, :], buf[:, 3:6, :], op))
                for buf, op in pairs:
                    need("tree", 1)
                    mark("tree", V.tensor_tensor(buf[:, 0:2, :], buf[:, 0:2, :], buf[:, 2:13:10, :], op))
                for buf, op in pairs:
                    need("tree", 1)
                    mark("tree", V.tensor_tensor(buf[:, 0, :], buf[:, 0, :], buf[:, 1, :], op))
                dve.wait_ge(s["ps"], given(t))
                for (buf, op), k, most_of in zip(pairs, (2, 1), (NEG_BIG, -NEG_BIG)):
                    need("tree", 1 if k == 2 else 0)
                    last = V.scalar_tensor_tensor(out=m4[:, :, k, :], in0=buf[:, 0, :].rearrange(
                        "p (g d) -> p g d", g=G), scalar=most_of, in1=pS[:, :, :], op0=op, op1=ALU.add)
                last.then_inc(s["extremes"], 1)

            def invert(t, st, root, signal):
                dve.wait_ge(s[root], given(t))
                V.reciprocal(st[:, 2, :], st[:, 1, :]).then_inc(s[signal], 1)

            def b2a(t):
                dve.wait_ge(s["yss"], given(t))
                own(V.tensor_tensor(zf[:, :, :], ys[:, 0, :, :], ys[:, 1, :, :], ALU.add))
                for p in range(G // 2):
                    y = (MB, MB2)[p][:, 0:6 * D].rearrange("p (a f d) -> p a f d", a=2, f=3)[:, :, 0, :]
                    last = V.tensor_tensor(zf[:, 2 * p:2 * p + 2, :], y, zf[:, 2 * p:2 * p + 2, :], ALU.add)
                last.then_inc(s["ysum"], 1)

            def b2c(t):
                invert(t, stf, "sdf", "rcf")

            def b4c(t):
                invert(t, stf, "sd1", "rc1")

            def c1(t):
                before(dve, "z3s", t, 2)
                V.tensor_copy(rowb[t.u][:, :, :], rows[:, RDEN:MASK + 1, bass.ds(t.g * G, G)]).then_inc(s["rowb"], 1)

            def c3a(t):
                dve.wait_ge(s["y2s"], given(t))
                V.tensor_tensor(flat(zb[:, :, :]), PX[:, C:2 * C], flat(yb[:, :, :]), ALU.add).then_inc(s["y2sum"], 1)

            def c3c(t):
                invert(t, stb, "sd2", "rc2")

            def c6a(t):
                dve.wait_ge(s["z3s"], given(t))
                V.tensor_tensor(zb[:, :, :], yb[:, :, :], x3c[:, :, :], ALU.add).then_inc(s["z3sum"], 1)

            def c6c(t):
                invert(t, stb, "sd3", "rc3")

            steps = [(layer, step) for layer, todo in enumerate(plan) for step in todo]

            def sort(t, lo, hi):
                buffers = (slot2[t.u], swap)
                for k in range(lo, min(hi, len(steps))):
                    layer, (is_min, in0, in1, dst) = steps[k]
                    if k == 0:
                        dve.wait_ge(s["slot2"], given(t, K2B))
                        need("weigh", 0)
                    elif steps[k - 1][0] != layer:
                        need("sort", 0)
                    each = V.tensor_tensor(slots(buffers, dst), slots(buffers, in0), slots(buffers, in1),
                                           ALU.min if is_min else ALU.max)
                    if k + 1 < len(steps):
                        mark("sort", each)
                    else:
                        each.then_inc(s["sorted"], 1)

            def weigh(t):
                dve.wait_ge(s["sorted"], given(t))
                dve.wait_ge(s["rankw"], given(t))
                for place in ranks_in[1]:
                    mark("weigh", V.tensor_tensor(slot2[t.u][:, place, :].rearrange("p (g d) -> p g d", g=G),
                                                  swap[:, place, :].rearrange("p (g d) -> p g d", g=G),
                                                  per_row(rankw[t.u][:, place, :]), ALU.mult))

            def quantiles(t):
                dve.wait_ge(s["weighted"], given(t, len(ranks_in[0])))
                need("weigh", 0)
                prod = slot2[t.u]
                own(V.tensor_tensor(prod[:, 0:4, :], prod[:, 0:4, :], prod[:, 6:10, :], ALU.add))
                own(V.tensor_tensor(prod[:, 0:2, :], prod[:, 0:2, :], prod[:, 2:4, :], ALU.add))
                own(V.tensor_tensor(prod[:, 0, :], prod[:, 0, :], prod[:, 1, :], ALU.add))
                own(V.tensor_tensor(prod[:, 0, :], prod[:, 0, :], prod[:, 10, :], ALU.add))
                V.tensor_tensor(flat(o2[:, :, :]), prod[:, 0, :], flat(x2[t.u][:, :, :]), ALU.add).then_inc(s["o2"], 1)

            def restart():
                if marks:
                    dve.wait_ge(s["chain_dve"], count[0])
                    marks.clear()
                dve.sem_clear(s["chain_dve"])
                count[0] = 0

            def node(ap, m):
                return ap[:, :, bass.ds(m, 1)].broadcast_to([128, G, D])

            def pick_node(m):
                V.tensor_copy(pick, identb[:, bass.ds(m, 1)].broadcast_to([128, 128])).then_inc(s["pick"], 1)

            def general0(t):
                own(V.tensor_scalar(off[:, :, :], adj_all[:, bass.ds(t.g * G, G), :], 0.0, NEG_BIG,
                                    ALU.is_gt, ALU.mult))
                own(V.tensor_scalar(off[:, :, :], off[:, :, :], -NEG_BIG, None, ALU.add))
                own(V.memset(gmax[:, :, :], -FLT_MAX))
                own(V.memset(gmin[:, :, :], FLT_MAX))
                row = RG0[:, 0:C].rearrange("p (g d) -> p g d", g=G)
                with dve.Fori(0, N) as m:
                    restart()
                    pick_node(m)
                    dve.wait_ge(s["row_ps"], t.g * (2 * N) + m + 1)
                    own(V.tensor_tensor(gtmp[:, 0, :, :], row, node(off, m), ALU.add))
                    own(V.tensor_tensor(gmax[:, :, :], gmax[:, :, :], gtmp[:, 0, :, :], ALU.max))
                    own(V.tensor_tensor(gtmp[:, 0, :, :], row, node(off, m), ALU.subtract))
                    own(V.tensor_tensor(gmin[:, :, :], gmin[:, :, :], gtmp[:, 0, :, :], ALU.min))
                dve.wait_ge(s["ps"], given(t))
                own(V.tensor_tensor(m4[:, :, 2, :], gmin[:, :, :], pS[:, :, :], ALU.add))
                V.tensor_tensor(m4[:, :, 1, :], gmax[:, :, :], pS[:, :, :], ALU.add).then_inc(s["extremes"], 1)

            def general2(t):
                own(V.tensor_tensor(earlier, upto[:, :], identb[:, :], ALU.subtract))
                own(V.memset(gmax[:, :, :], 0.0))
                dve.wait_ge(s["rankw"], given(t))
                row = RG0[:, 0:C].rearrange("p (g d) -> p g d", g=G)
                rank = RG1[:, 0:C].rearrange("p (g d) -> p g d", g=G)
                with dve.Fori(0, N) as m:
                    restart()
                    pick_node(m)
                    dve.wait_ge(s["row_ps"], t.g * (2 * N) + m + N + 1)
                    own(V.tensor_tensor(gtmp[:, 0, :, :], x2[t.u][:, :, :], row, ALU.is_lt))
                    own(V.tensor_tensor(gtmp[:, 1, :, :], x2[t.u][:, :, :], row, ALU.is_le))
                    own(V.tensor_tensor(gtmp[:, 1, :, :], gtmp[:, 1, :, :], gtmp[:, 0, :, :], ALU.subtract))
                    own(V.tensor_tensor(gtmp[:, 1, :, :], gtmp[:, 1, :, :],
                                        slotP[:, 6, bass.ds(m, 1)].unsqueeze(1).broadcast_to([128, G, D]), ALU.mult))
                    V.tensor_tensor(below[:, :, :], gtmp[:, 1, :, :], gtmp[:, 0, :, :],
                                    ALU.add).then_inc(s["below"], 1)
                    dve.wait_ge(s["below_ps"], t.g * N + m + 1)
                    for k in range(3):
                        own(V.tensor_tensor(gtmp[:, 0, :, :], rank, per_row(post[:, k, :]), ALU.subtract))
                        own(V.tensor_scalar(gtmp[:, 1, :, :], gtmp[:, 0, :, :], -1.0, None, ALU.mult))
                        own(V.tensor_tensor(gtmp[:, 0, :, :], gtmp[:, 0, :, :], gtmp[:, 1, :, :], ALU.max))
                        own(V.tensor_scalar(gtmp[:, 0, :, :], gtmp[:, 0, :, :], -1.0, 1.0, ALU.mult, ALU.add))
                        own(V.tensor_scalar(gtmp[:, 0, :, :], gtmp[:, 0, :, :], 0.0, QUANTILE_WEIGHTS[k],
                                            ALU.max, ALU.mult))
                        if k == 0:
                            own(V.tensor_copy(gmin[:, :, :], gtmp[:, 0, :, :]))
                        else:
                            own(V.tensor_tensor(gmin[:, :, :], gmin[:, :, :], gtmp[:, 0, :, :], ALU.add))
                    own(V.tensor_tensor(gmin[:, :, :], gmin[:, :, :], node(validN, m), ALU.mult))
                    own(V.tensor_tensor(gmin[:, :, :], gmin[:, :, :], row, ALU.mult))
                    own(V.tensor_tensor(gmax[:, :, :], gmax[:, :, :], gmin[:, :, :], ALU.add))
                V.tensor_tensor(o2[:, :, :], gmax[:, :, :], x2[t.u][:, :, :], ALU.add).then_inc(s["o2"], 1)

            def check_counts():
                own(V.tensor_reduce(mostn[:, :], most[:, :, :], AX.X, ALU.max))
                own(V.tensor_scalar(excess[:, 0:1], mostn[:, 0:1], float(K0), None, ALU.is_gt))
                own(V.tensor_scalar(excess[:, 1:2], mostn[:, 1:2], float(K2), None, ALU.is_gt))
                V.tensor_tensor(excess[:, 2:3], excess[:, 0:1], excess[:, 1:2], ALU.max).then_inc(over_a, 1)
                dve.wait_ge(over_b, 1)
                own(V.tensor_reduce(over[0:1, :], PX[0:1, 0:128], AX.X, ALU.max))
                V.tensor_copy(overi[0:1, :], over[0:1, :]).then_inc(over_c, 1)

            return dict(prepare=prepare, degrees=degrees, factors=factors, restart=restart, sort=sort, quantiles=quantiles, weigh=weigh, a1=a1,
                        a3=a3, a3b=a3b, a4=a4, a6=a6, a7=a7, hots0=hots0, hots2=hots2, b2a=b2a, b2c=b2c,
                        b4c=b4c, c1=c1, c3a=c3a, c3c=c3c, c6a=c6a,
                        c6c=c6c,
                        general0=general0, general2=general2, check_counts=check_counts)

        def vector_fast(dve):
            part = vector_steps(dve)
            part["prepare"]()
            pipeline(dve, part, VECTOR_ORDER, {0: lambda: part["degrees"](OTHERS),
                                               2: lambda: part["factors"](OTHERS, 2)})
            part["check_counts"]()

        with nc.Block() as block:
            block.sync(sync_fast)
            block.tensor(tensor_fast)
            block.scalar(scalar_fast)
            block.gpsimd(gpsimd_fast)
            block.vector(vector_fast)

        GENERAL = {
            "tensor": ("a1", "a2", "a2m", "a2l", "a1c", "a1n", "a3", "a5", "a6", "general0", "b1", "b2", "b3", "b4",
                       "b5", "b6", "general2", "c1", "c2", "c3", "c4", "c5", "c6"),
            "scalar": ("a1b", "a2", "a2m", "a2l", "a1c", "a1n", "a3", "a5", "a6", "a3s", "b1", "b2", "b2s", "b2n", "b3",
                       "b4", "b4n", "b5", "b5m", "b6", "c1", "c2", "c3y", "c3", "c3n", "c4", "c5", "c6y", "c6", "c6n"),
            "gpsimd": ("a1", "a4", "a2", "a3", "a6", "b0"),
            "vector": ("a1", "a4", "a3", "a3b", "a6", "general0", "b2a", "b2c", "b4c",
                       "general2", "c1", "c3a", "c3c", "c6a", "c6c"),
        }

        def general(eng, part, order):
            if "restart" in part:
                part["restart"]()
            with eng.Fori(0, NG // 2) as i:
                for u in range(2):
                    for step in order:
                        part[step](Turn(i, u, NG))
                    if "restart" in part:
                        part["restart"]()

        any_over = nc.values_load(overi[0:1, 0:1], min_val=0, max_val=1)
        with nc.If(any_over > 0):
            with nc.Block() as block:
                @block.sync
                def _(sp):
                    with sp.Fori(0, NG // 2) as i:
                        for u in range(2):
                            t = Turn(i, u, NG)
                            load_a(sp, t)
                            load_x(sp, t)
                            load_b(sp, t)
                            load_c(sp, t)
                            store_group(sp, t)
                    for u in range(2):
                        sp.wait_ge(stored[u], 16 * NG)

                @block.tensor
                def _(pe):
                    general(pe, tensor_steps(pe), GENERAL["tensor"])

                @block.scalar
                def _(act):
                    general(act, scalar_steps(act), GENERAL["scalar"])

                @block.gpsimd
                def _(pool):
                    general(pool, gpsimd_steps(pool), GENERAL["gpsimd"])

                @block.vector
                def _(dve):
                    general(dve, vector_steps(dve), GENERAL["vector"])


def kernel(**inputs):
    import concourse.bacc as bacc
    from concourse.bass_utils import run_bass_kernel_spmd

    a = {k: np.asarray(v) for k, v in inputs.items()}
    x, adj = a["x"], a["adj"]
    laid = {
        "x_pairs": x.reshape(B // 2, 2, N, D).transpose(1, 3, 0, 2).reshape(2 * D, B // 2, N),
        "adj_rows": adj.transpose(1, 0, 2),
        "adj_cols": adj.transpose(2, 0, 1),
        "node_mask": a["nodemask"].view(np.uint8).T,
        "w_pre": a["L0_gnn_W_pre"], "b_pre": a["L0_gnn_b_pre"],
        "w_post": a["L0_gnn_W_post"], "b_post": a["L0_gnn_b_post"],
        "w_l1": a["L1_gnn_weight"], "b_l1": a["L1_gnn_bias"],
        "w1": a["L2_gnn_W1"], "b1": a["L2_gnn_b1"], "w2": a["L2_gnn_W2"], "b2": a["L2_gnn_b2"],
    }
    nc = bacc.Bacc("TRN2", target_bir_lowering=False, num_devices=1)
    arrays, args = {}, []
    for name, v in laid.items():
        v = np.ascontiguousarray(v)
        arrays[f"{name}_dram"] = v
        args.append(nc.dram_tensor(f"{name}_dram", v.shape, mybir.dt.from_np(v.dtype), kind="ExternalInput").ap())
    args.append(nc.dram_tensor("out_dram", (N, B, D), F32, kind="ExternalOutput").ap())
    adj_kernel(nc, *args)
    got = run_bass_kernel_spmd(nc, [arrays], core_ids=[0]).results[0]["out_dram"]
    return np.ascontiguousarray(np.transpose(got, (1, 0, 2)))
```
